# Optimizing a Trainium2 kernel written in Bass

```python
import numpy as np
import jax
import jax.numpy as jnp

def _softmax(x, axis=-1):
    return jax.nn.softmax(x, axis=axis)

def _gelu(x):
    return jax.nn.gelu(x, approximate=True)

def _silu(x):
    return jax.nn.silu(x)

def _sigmoid(x):
    return jax.nn.sigmoid(x)

def _layernorm(x, axis=-1, eps=1e-05):
    m = jnp.mean(x, axis=axis, keepdims=True)
    v = jnp.var(x, axis=axis, keepdims=True)
    return (x - m) / jnp.sqrt(v + eps)

def _scatter_add(tgt, idx, src, axis=0):
    return tgt.at[idx].add(src)

def _segment_sum(src, seg, n):
    return jax.ops.segment_sum(src, seg, n)
kernel_name = 'mk_cond_resid_d4_seqx_r4_92eefc'

def setup_inputs(seed: int=0):
    np.random.seed(seed)
    _w = jnp.asarray

    def _rec_inputs():
        import jax
        import jax.numpy as jnp
        _rk = jax.random.key(seed)
        x = -0.0003929 + 0.9999 * jax.random.normal(jax.random.fold_in(_rk, 1), (64, 64, 512), jnp.float32)
        _lenS = 64 - jax.random.randint(jax.random.fold_in(_rk, 7), (64,), 0, max(1, 64 // 4) + 1, jnp.int32)
        _lenS2 = 64 - jax.random.randint(jax.random.fold_in(_rk, 8), (64,), 0, max(1, 64 // 4) + 1, jnp.int32)
        cond_2048 = 0.00782532 + 1.00527 * jax.random.normal(jax.random.fold_in(_rk, 11), (64, 512), jnp.float32)
        return (x, cond_2048)
    x, cond_2048 = _rec_inputs()

    def _L0_cond_setup():
        import jax, jax.numpy as jnp
        import numpy as np
        HEADS = 16
        EPS = 1e-06

        def _rms_norm(x, g):
            xf = x.astype(jnp.float32)
            y = xf * jax.lax.rsqrt(jnp.mean(xf * xf, axis=-1, keepdims=True) + EPS)
            return y.astype(x.dtype) * g
        key = jax.random.key(seed)
        ks = jax.random.split(key, 6)
        b, n, dim, emb_dim = (4, 512, 512, 512)
        d_head = dim // HEADS
        return {'x': jax.random.normal(ks[0], (b, n, dim), jnp.float32), 'emb': jax.random.normal(ks[1], (b, 1, emb_dim), jnp.float32), 'W_emb': jax.random.normal(ks[2], (emb_dim, 2 * dim), jnp.float32) * emb_dim ** (-0.5), 'b_emb': jnp.zeros((2 * dim,), jnp.float32), 'g_norm': jnp.ones((dim,), jnp.float32), 'W_qkv': jax.random.normal(ks[3], (dim, 3 * dim), jnp.float32) * dim ** (-0.5), 'g_q': jnp.ones((d_head,), jnp.float32), 'g_k': jnp.ones((d_head,), jnp.float32), 'W_out': jax.random.normal(ks[4], (dim, dim), jnp.float32) * dim ** (-0.5)}
    _L0_cond_all = _L0_cond_setup()
    _L0_cond_in = {k: v for k, v in _L0_cond_all.items() if k in ('W_emb', 'b_emb', 'g_norm', 'W_qkv', 'g_q', 'g_k', 'W_out')}
    del _L0_cond_all

    def _L1_cond_setup():
        import jax, jax.numpy as jnp
        import numpy as np
        N, C, L_IN, L_OUT = (32, 64, 512, 512)
        key = jax.random.key(seed)
        k1, k2 = jax.random.split(key)
        inp = jax.random.normal(k1, (N, C, L_IN), dtype=jnp.float32)
        grid = jax.random.uniform(k2, (N, L_OUT), dtype=jnp.float32) * 2.0 - 1.0
        return {'input': inp, 'grid': grid, 'padding_mode': 1, 'align_corners': 1}
    _L1_cond_all = _L1_cond_setup()
    _L1_cond_in = {k: v for k, v in _L1_cond_all.items() if k in ()}
    del _L1_cond_all

    def _L2_cond_setup():
        import jax, jax.numpy as jnp
        import numpy as np
        B, T, D = (16, 128, 512)
        key = jax.random.key(seed)
        k0, k1, k2, k3 = jax.random.split(key, 4)
        scale = 1.0 / np.sqrt(D)
        return {'initial_state': jax.random.normal(k0, (B, D), jnp.float32), 'inputs': jax.random.normal(k1, (B, T, D), jnp.float32), 'W_ih': jax.random.normal(k2, (D, 3 * D), jnp.float32) * scale, 'W_hh': jax.random.normal(k3, (D, 3 * D), jnp.float32) * scale, 'b_ih': jnp.zeros((3 * D,), jnp.float32), 'b_hh': jnp.zeros((3 * D,), jnp.float32)}
    _L2_cond_all = _L2_cond_setup()
    _L2_cond_in = {k: v for k, v in _L2_cond_all.items() if k in ('W_ih', 'W_hh', 'b_ih', 'b_hh')}
    del _L2_cond_all

    def _L3_cond_setup():
        import jax, jax.numpy as jnp
        import numpy as np
        DT = 0.01
        EPSILON = 0.08
        ALPHA = 0.7
        BETA = 0.8
        CLAMP = 20.0
        B, T, N = (64, 128, 512)

        def _derivative(q, p, drive, coupling, bias):
            i_couple = jnp.tanh(q) @ coupling.T
            dq = q - q ** 3 / 3.0 - p + drive + i_couple + bias
            dp = EPSILON * (q + ALPHA - BETA * p)
            return (dq, dp)

        def _rk4_step(q, p, drive, coupling, bias):
            dq1, dp1 = _derivative(q, p, drive, coupling, bias)
            dq2, dp2 = _derivative(q + 0.5 * DT * dq1, p + 0.5 * DT * dp1, drive, coupling, bias)
            dq3, dp3 = _derivative(q + 0.5 * DT * dq2, p + 0.5 * DT * dp2, drive, coupling, bias)
            dq4, dp4 = _derivative(q + DT * dq3, p + DT * dp3, drive, coupling, bias)
            q_next = q + DT / 6.0 * (dq1 + 2 * dq2 + 2 * dq3 + dq4)
            p_next = p + DT / 6.0 * (dp1 + 2 * dp2 + 2 * dp3 + dp4)
            q_next = jnp.clip(q_next, -CLAMP, CLAMP)
            p_next = jnp.clip(p_next, -CLAMP, CLAMP)
            return (q_next, p_next)
        key = jax.random.key(seed)
        k1, k2, k3, k4 = jax.random.split(key, 4)
        return {'q0': jax.random.normal(k1, (B, N), dtype=jnp.float32), 'p0': jax.random.normal(k2, (B, N), dtype=jnp.float32), 'input_drive_seq': jax.random.normal(k3, (B, T, N), dtype=jnp.float32), 'coupling': jax.random.normal(k4, (N, N), dtype=jnp.float32) * 0.01, 'bias': jnp.zeros((N,), dtype=jnp.float32)}
    _L3_cond_all = _L3_cond_setup()
    _L3_cond_in = {k: v for k, v in _L3_cond_all.items() if k in ('coupling', 'bias')}
    del _L3_cond_all
    return {'x': x, 'cond_2048': cond_2048, 'L0_cond_W_emb': _L0_cond_in['W_emb'], 'L0_cond_b_emb': _L0_cond_in['b_emb'], 'L0_cond_g_norm': _L0_cond_in['g_norm'], 'L0_cond_W_qkv': _L0_cond_in['W_qkv'], 'L0_cond_g_q': _L0_cond_in['g_q'], 'L0_cond_g_k': _L0_cond_in['g_k'], 'L0_cond_W_out': _L0_cond_in['W_out'], 'L2_cond_W_ih': _L2_cond_in['W_ih'], 'L2_cond_W_hh': _L2_cond_in['W_hh'], 'L2_cond_b_ih': _L2_cond_in['b_ih'], 'L2_cond_b_hh': _L2_cond_in['b_hh'], 'L3_cond_coupling': _L3_cond_in['coupling'], 'L3_cond_bias': _L3_cond_in['bias']}

def reference(x, cond_2048, L0_cond_W_emb, L0_cond_b_emb, L0_cond_g_norm, L0_cond_W_qkv, L0_cond_g_q, L0_cond_g_k, L0_cond_W_out, L2_cond_W_ih, L2_cond_W_hh, L2_cond_b_ih, L2_cond_b_hh, L3_cond_coupling, L3_cond_bias):
    import jax
    import jax.numpy as jnp

    def _L0_cond_ref(x, emb, W_emb, b_emb, g_norm, W_qkv, g_q, g_k, W_out):
        import jax, jax.numpy as jnp
        import numpy as np
        HEADS = 16
        EPS = 1e-06

        def _rms_norm(x, g):
            xf = x.astype(jnp.float32)
            y = xf * jax.lax.rsqrt(jnp.mean(xf * xf, axis=-1, keepdims=True) + EPS)
            return y.astype(x.dtype) * g
        b, n, dim = x.shape
        h = HEADS
        d = dim // h
        scale_shift = emb @ W_emb + b_emb
        scale, shift = jnp.split(scale_shift, 2, axis=-1)
        xn = _rms_norm(x, g_norm) * (1.0 + scale) + shift
        qkv = xn @ W_qkv
        qkv = qkv.reshape(b, n, 3, h, d)
        q, k, v = jnp.moveaxis(qkv, 2, 0)
        q = jnp.swapaxes(q, 1, 2)
        k = jnp.swapaxes(k, 1, 2)
        v = jnp.swapaxes(v, 1, 2)
        q = _rms_norm(q, g_q)
        k = _rms_norm(k, g_k)
        logits = jnp.einsum('bhqd,bhkd->bhqk', q, k) * d ** (-0.5)
        attn = jax.nn.softmax(logits, axis=-1)
        o = jnp.einsum('bhqk,bhkd->bhqd', attn, v)
        o = jnp.swapaxes(o, 1, 2).reshape(b, n, dim)
        return o + o @ W_out

    def _L1_cond_ref(input, grid, padding_mode, align_corners):
        import jax, jax.numpy as jnp
        import numpy as np
        N, C, L_IN, L_OUT = (32, 64, 512, 512)
        L = input.shape[2]
        if align_corners:
            ix = (grid + 1.0) * 0.5 * (L - 1)
        else:
            ix = ((grid + 1.0) * L - 1.0) * 0.5
        x0 = jnp.floor(ix)
        w1 = ix - x0
        w0 = 1.0 - w1
        i0 = x0.astype(jnp.int32)
        i1 = i0 + 1
        i0c = jnp.clip(i0, 0, L - 1)
        i1c = jnp.clip(i1, 0, L - 1)
        v0 = jnp.take_along_axis(input, i0c[:, None, :], axis=2)
        v1 = jnp.take_along_axis(input, i1c[:, None, :], axis=2)
        if padding_mode:
            return w0[:, None, :] * v0 + w1[:, None, :] * v1
        else:
            m0 = ((i0 >= 0) & (i0 < L)).astype(input.dtype)
            m1 = ((i1 >= 0) & (i1 < L)).astype(input.dtype)
            return (w0 * m0)[:, None, :] * v0 + (w1 * m1)[:, None, :] * v1

    def _L2_cond_ref(initial_state, inputs, W_ih, W_hh, b_ih, b_hh):
        import jax, jax.numpy as jnp
        import numpy as np
        B, T, D = (16, 128, 512)
        "ScanOverTime(GRU cell): sequential per-timestep module call with\n            dict-state passing; merge_dict_trees stacks the per-step\n            'state_predicted' tensors along axis=1 -> [B, T, D]."

        def cell(h, x):
            gi = x @ W_ih + b_ih
            gh = h @ W_hh + b_hh
            i_r, i_z, i_n = jnp.split(gi, 3, axis=-1)
            h_r, h_z, h_n = jnp.split(gh, 3, axis=-1)
            r = jax.nn.sigmoid(i_r + h_r)
            z = jax.nn.sigmoid(i_z + h_z)
            n = jnp.tanh(i_n + r * h_n)
            h_new = (1.0 - z) * n + z * h
            return (h_new, h_new)
        xs = jnp.swapaxes(inputs, 0, 1)
        _, hs = jax.lax.scan(cell, initial_state, xs)
        return jnp.swapaxes(hs, 0, 1)

    def _L3_cond_ref(q0, p0, input_drive_seq, coupling, bias):
        import jax, jax.numpy as jnp
        import numpy as np
        DT = 0.01
        EPSILON = 0.08
        ALPHA = 0.7
        BETA = 0.8
        CLAMP = 20.0
        B, T, N = (64, 128, 512)

        def _derivative(q, p, drive, coupling, bias):
            i_couple = jnp.tanh(q) @ coupling.T
            dq = q - q ** 3 / 3.0 - p + drive + i_couple + bias
            dp = EPSILON * (q + ALPHA - BETA * p)
            return (dq, dp)

        def _rk4_step(q, p, drive, coupling, bias):
            dq1, dp1 = _derivative(q, p, drive, coupling, bias)
            dq2, dp2 = _derivative(q + 0.5 * DT * dq1, p + 0.5 * DT * dp1, drive, coupling, bias)
            dq3, dp3 = _derivative(q + 0.5 * DT * dq2, p + 0.5 * DT * dp2, drive, coupling, bias)
            dq4, dp4 = _derivative(q + DT * dq3, p + DT * dp3, drive, coupling, bias)
            q_next = q + DT / 6.0 * (dq1 + 2 * dq2 + 2 * dq3 + dq4)
            p_next = p + DT / 6.0 * (dp1 + 2 * dp2 + 2 * dp3 + dp4)
            q_next = jnp.clip(q_next, -CLAMP, CLAMP)
            p_next = jnp.clip(p_next, -CLAMP, CLAMP)
            return (q_next, p_next)
        drive_tbn = jnp.swapaxes(input_drive_seq, 0, 1)

        def scan_fn(carry, drive):
            q, p = carry
            q, p = _rk4_step(q, p, drive, coupling, bias)
            return ((q, p), q)
        (_, _), q_trace_tbn = jax.lax.scan(scan_fn, (q0, p0), drive_tbn)
        return jnp.swapaxes(q_trace_tbn, 0, 1)
    x = x + _L0_cond_ref(x, cond_2048[:, None, :], L0_cond_W_emb, L0_cond_b_emb, L0_cond_g_norm, L0_cond_W_qkv, L0_cond_g_q, L0_cond_g_k, L0_cond_W_out)
    x = x + _L1_cond_ref(x, cond_2048, 1, 1)
    x = x + _L2_cond_ref(cond_2048, x, L2_cond_W_ih, L2_cond_W_hh, L2_cond_b_ih, L2_cond_b_hh)
    x = x + _L3_cond_ref(cond_2048, cond_2048, x, L3_cond_coupling, L3_cond_bias)
    return x

_drawn_inputs = setup_inputs


def setup_inputs(seed=0):
    import zlib

    import numpy as np

    out = dict(_drawn_inputs(seed))
    spreads = {'L0_cond_b_emb': (0.0, 0.1),
     'L0_cond_g_norm': (1.0, 0.2),
     'L0_cond_g_q': (1.0, 0.578),
     'L0_cond_g_k': (1.0, 0.2),
     'L2_cond_b_ih': (0.0, 0.483),
     'L2_cond_b_hh': (0.0, 0.736),
     'L3_cond_bias': (0.0, 0.655)}
    factors = {'L3_cond_coupling': 3.393}
    for name, (base, spread) in spreads.items():
        noise = np.random.default_rng([zlib.crc32(name.encode()), seed]).standard_normal(out[name].shape)
        drawn = base * np.exp(spread * noise) if base else spread * noise
        out[name] = jnp.asarray(drawn.astype(out[name].dtype))
    for name, factor in factors.items():
        out[name] = (out[name] * factor).astype(out[name].dtype)
    return out
```

```python
from contextlib import ExitStack

import concourse.bass as bass
from concourse import mybir

ALU = mybir.AluOpType
ACT = mybir.ActivationFunctionType
AX = mybir.AxisListType
F32 = mybir.dt.float32
F16 = mybir.dt.float16
I32 = mybir.dt.int32

WS = 64.0
PART = 128
EPS = 1e-6
HEADS = 16
DT, EPSILON, ALPHA, BETA, CLAMP = 0.01, 0.08, 0.7, 0.8, 20.0


class Pair:

    def __init__(self, n, half, u):
        self.n, self.half, self.u = n, half, u

    def later(self, d, count):
        n = self.n + d
        return None if isinstance(n, int) and n >= count else n


def need(eng, sem, value):
    if isinstance(value, int) and value <= 0:
        return
    eng.wait_ge(sem, value)


def program(nc, x, cond, W_emb, b_emb, g_norm, W_qkv, g_q, g_k, W_out, W_ih, W_hh, b_ih, b_hh,
            coupling, bias, out, rows_dram):
    B, T, D = x.shape
    KC = D // PART
    G3 = W_ih.shape[1]
    DH = D // HEADS
    NPAIR = B // 2
    TOK = 2 * T
    assert TOK == PART and KC == 4 and B == 64 and T == 64

    with ExitStack() as ctx:
        def sb(name, shape, dt=F32, stack=ctx):
            return stack.enter_context(nc.sbuf_tensor(name, shape, dt))

        def sem(name, stack=ctx):
            return stack.enter_context(nc.semaphore(name))

        XR = sb("XR", [PART, T, KC, B])
        condT = sb("condT", [PART, KC, B])
        ident = sb("ident", [PART, PART])
        with ExitStack() as attn:
            keep = dict(
                Wqkv=sb("Wqkv", [PART, 2, KC, G3], F16, attn), Wo=sb("Wo", [PART, 2, KC, D], F16, attn),
                modA=sb("modA", [PART, KC, B], F32, attn), modB=sb("modB", [PART, KC, B], F32, attn),
                WT=sb("WT", [PART, 2, KC, B], F32, attn), lidx=sb("lidx", [PART, 2, KC], F32, attn),
                gqk=sb("gqk", [PART, 1], F32, attn), mhalf=sb("mhalf", [PART, 2 * HEADS], F32, attn),
                Vbd=[sb(f"Vbd{u}", [PART, 2, 2, HEADS // 2, 64], F16, attn) for u in range(2)])
            with ExitStack() as s:
                setup(nc, s, XR, condT, ident, keep, cond, W_emb, b_emb, g_norm, W_qkv, g_q, g_k, W_out, rows_dram)
            with ExitStack() as s:
                attention_and_sampling(nc, s, XR, ident, keep, x, rows_dram)
        with ExitStack() as s:
            recurrences(nc, s, XR, condT, ident, W_ih, W_hh, b_ih, b_hh, coupling, bias, out)


def setup(nc, ctx, XR, condT, ident, keep, cond, W_emb, b_emb, g_norm, W_qkv, g_q, g_k, W_out, rows_dram):
    B, D = cond.shape
    KC = D // PART
    G3 = W_qkv.shape[1]
    DH = g_q.shape[0]
    Wqkv, Wo, modA, modB = keep["Wqkv"], keep["Wo"], keep["modA"], keep["modB"]
    WT, lidx, gqk, mhalf, Vbd = keep["WT"], keep["lidx"], keep["gqk"], keep["mhalf"], keep["Vbd"]

    def sb(name, shape, dt=F32):
        return ctx.enter_context(nc.sbuf_tensor(name, shape, dt))

    def sem(name):
        return ctx.enter_context(nc.semaphore(name))

    room = XR[:, :, :, :].rearrange("p t c b -> p (t c b)")
    wq32 = room[:, 0:KC * G3].rearrange("p (c n) -> p c n", c=KC)
    wo32 = room[:, KC * G3:KC * (G3 + D)].rearrange("p (c n) -> p c n", c=KC)
    we32 = room[:, KC * (G3 + D):KC * (G3 + 3 * D)].rearrange("p (c n) -> p c n", c=KC)
    condtok = sb("condtok", [B, D])
    bemb = sb("bemb", [PART, 2 * KC])
    gnorm = sb("gnorm", [PART, KC])
    gq = sb("gq", [PART, 2])
    ix = sb("ix", [B, D])
    iint = sb("iint", [B, D], I32)
    ir = sb("ir", [B, D])
    igt = sb("igt", [B, D])
    i0 = sb("i0", [B, D])
    i0h = sb("i0h", [B, D], F16)
    w1 = sb("w1", [B, D])
    psC = ctx.enter_context(nc.psum_tensor("psC", [PART, KC, B], F32))
    psW = ctx.enter_context(nc.psum_tensor("psW", [PART, KC, B], F32))
    psE = ctx.enter_context(nc.psum_tensor("psE", [PART, 2 * KC, B], F32))

    cond_in, small_in, wemb_in, wqkv_in, wo_in = (sem(n) for n in ("cond_in", "small_in", "wemb_in", "wqkv_in", "wo_in"))
    rows_out = sem("rows_out")
    consts = sem("consts")
    grid_step = sem("grid_step")
    rows_ready, w1_ready = sem("rows_ready"), sem("w1_ready")
    cond_T, cond_kept, w1_T, emb_done = sem("cond_T"), sem("cond_kept"), sem("w1_T"), sem("emb_done")
    wo_plus, hi_done, mod_step, fold = sem("wo_plus"), sem("hi_done"), sem("mod_step"), sem("fold")
    block = ctx.enter_context(nc.Block())

    @block.sync
    def _(sp):
        sp.dma_start(condtok[:, :], cond).then_inc(cond_in, 16)
        sp.dma_start(we32, W_emb.rearrange("(c p) n -> p c n", p=PART)).then_inc(wemb_in, 16)
        sp.dma_start(wo32, W_out.rearrange("(c p) n -> p c n", p=PART)).then_inc(wo_in, 16)
        sp.dma_start(wq32, W_qkv.rearrange("(c p) n -> p c n", p=PART)).then_inc(wqkv_in, 16)
        sp.wait_ge(rows_ready, 1)
        sp.dma_start(rows_dram, i0h[:, :]).then_inc(rows_out, 16)
        sp.wait_ge(rows_out, 16)

    @block.gpsimd
    def _(pool):
        nc.gpsimd.memset(ident[:, :], 0.0).then_inc(consts, 1)
        pool.wait_ge(consts, 1)
        nc.gpsimd.affine_select(out=ident[:, :], in_=ident[:, :], compare_op=ALU.not_equal, fill=1.0, base=0,
                                pattern=[[-1, PART]], channel_multiplier=1).then_inc(consts, 1)
        nc.gpsimd.iota(lidx[:, :, :], pattern=[[-1, 2], [PART, KC]], base=0, channel_multiplier=1,
                       allow_small_or_imprecise_dtypes=True).then_inc(consts, 1)
        nc.gpsimd.memset(mhalf[:, :], -0.5).then_inc(consts, 1)
        for v in Vbd:
            nc.gpsimd.memset(v[:, :, :, :, :], 0.0).then_inc(consts, 1)

    @block.scalar
    def _(act):
        with nc.allow_non_contiguous_dma("small vectors, laid along the partitions"):
            act.dma_start(bemb[:, :], b_emb.rearrange("(c p) -> p c", p=PART)).then_inc(small_in, 16)
            act.dma_start(gnorm[:, :], g_norm.rearrange("(c p) -> p c", p=PART)).then_inc(small_in, 16)
            for n, g in enumerate((g_q, g_k)):
                for q in range(PART // DH):
                    act.dma_start(gq[q * DH:(q + 1) * DH, n:n + 1], g.rearrange("(p a) -> p a", a=1)).then_inc(small_in, 16)
        act.wait_ge(cond_T, 1)
        nc.scalar.activation(condT[:, :, :], psC[:, :, :], ACT.Copy).then_inc(cond_kept, 1)
        act.wait_ge(wo_plus, 1)
        for c in range(KC):
            nc.scalar.activation(Wo[:, 0, c, :], wo32[:, c, :], ACT.Copy, scale=WS).then_inc(hi_done, 1)
        act.wait_ge(wqkv_in, 16)
        for c in range(KC):
            nc.scalar.activation(Wqkv[:, 0, c, :], wq32[:, c, :], ACT.Copy, scale=WS).then_inc(hi_done, 1)

    @block.vector
    def _(dve):
        v = nc.vector
        dve.wait_ge(cond_in, 16)
        v.tensor_scalar(ix[:, :], condtok[:, :], 1.0, 0.5, ALU.add, ALU.mult).then_inc(grid_step, 1)
        dve.wait_ge(grid_step, 1)
        v.tensor_scalar(ix[:, :], ix[:, :], float(D - 1), 0.0, ALU.mult, ALU.max).then_inc(grid_step, 1)
        dve.wait_ge(grid_step, 2)
        v.tensor_scalar(ix[:, :], ix[:, :], float(D - 1), None, ALU.min).then_inc(grid_step, 1)
        dve.wait_ge(grid_step, 3)
        v.tensor_copy(iint[:, :], ix[:, :]).then_inc(grid_step, 1)
        dve.wait_ge(grid_step, 4)
        v.tensor_copy(ir[:, :], iint[:, :]).then_inc(grid_step, 1)
        dve.wait_ge(grid_step, 5)
        v.tensor_tensor(igt[:, :], ir[:, :], ix[:, :], ALU.is_gt).then_inc(grid_step, 1)
        dve.wait_ge(grid_step, 6)
        v.tensor_tensor(i0[:, :], ir[:, :], igt[:, :], ALU.subtract).then_inc(grid_step, 1)
        dve.wait_ge(grid_step, 7)
        v.tensor_copy(i0h[:, :], i0[:, :]).then_inc(rows_ready, 1)
        v.tensor_tensor(w1[:, :], ix[:, :], i0[:, :], ALU.subtract).then_inc(w1_ready, 1)
        dve.wait_ge(w1_T, 1)
        v.tensor_copy(WT[:, 1, :, :], psW[:, :, :])
        v.tensor_scalar(WT[:, 0, :, :], psW[:, :, :], -1.0, 1.0, ALU.mult, ALU.add)
        dve.wait_ge(consts, 2)
        dve.wait_ge(wo_in, 16)
        for c in range(KC):
            d = wo32[:, c, c * PART:(c + 1) * PART]
            last = v.tensor_tensor(d, d, ident[:, :], ALU.add)
        last.then_inc(wo_plus, 1)
        dve.wait_ge(small_in, 16 * (2 + 2 * (PART // DH)))
        v.tensor_scalar(gqk[:, :], gq[:, 0:1], gq[:, 1:2], float(DH) ** -0.5, ALU.mult, ALU.mult)
        dve.wait_ge(emb_done, 1)
        for c in range(KC):
            v.tensor_scalar(modA[:, c, :], psE[:, c, :], bemb[:, c:c + 1], 1.0, ALU.add, ALU.add).then_inc(mod_step, 1)
            v.tensor_scalar(modB[:, c, :], psE[:, KC + c, :], bemb[:, KC + c:KC + c + 1], None, ALU.add)
        dve.wait_ge(mod_step, KC)
        for c in range(KC):
            v.tensor_scalar(modA[:, c, :], modA[:, c, :], gnorm[:, c:c + 1], None, ALU.mult)
        for n, (pair, w32) in enumerate(((Wo, wo32), (Wqkv, wq32))):
            for c in range(KC):
                dve.wait_ge(hi_done, n * KC + c + 1)
                v.scalar_tensor_tensor(out=pair[:, 1, c, :], in0=w32[:, c, :], scalar=WS, in1=pair[:, 0, c, :],
                                       op0=ALU.mult, op1=ALU.subtract)

    @block.tensor
    def _(pe):
        pe.wait_ge(consts, 2)
        pe.wait_ge(cond_in, 16)
        for c in range(KC):
            last = nc.tensor.transpose(psC[:, c, :], condtok[:, c * PART:(c + 1) * PART], ident[0:B, 0:B])
        last.then_inc(cond_T, 1)
        pe.wait_ge(w1_ready, 1)
        for c in range(KC):
            last = nc.tensor.transpose(psW[:, c, :], w1[:, c * PART:(c + 1) * PART], ident[0:B, 0:B])
        last.then_inc(w1_T, 1)
        pe.wait_ge(cond_kept, 1)
        pe.wait_ge(wemb_in, 16)
        for m in range(2 * KC):
            for c in range(KC):
                last = nc.tensor.matmul(psE[:, m, :], we32[:, c, m * PART:(m + 1) * PART], condT[:, c, :],
                                        start=(c == 0), stop=(c == KC - 1))
        last.then_inc(emb_done, 1)


def attention_and_sampling(nc, ctx, XR, ident, keep, x, rows_dram):
    B, T, D = x.shape
    KC = D // PART
    DH = D // HEADS
    NP = B // 2
    Wqkv, Wo, modA, modB = keep["Wqkv"], keep["Wo"], keep["modA"], keep["modB"]
    WT, lidx, gqk, mhalf, Vbd = keep["WT"], keep["lidx"], keep["gqk"], keep["mhalf"], keep["Vbd"]

    def sb(name, shape, dt=F32):
        return ctx.enter_context(nc.sbuf_tensor(name, shape, dt))

    def sem(name):
        return ctx.enter_context(nc.semaphore(name))

    xtok = [sb(f"xtok{u}", [PART, D]) for u in range(2)]
    sqx = sb("sqx", [PART, D])
    ssx = sb("ssx", [PART, 2])
    msx = sb("msx", [PART, 2])
    rx = sb("rx", [PART, 2])
    yt = [sb(f"yt{u}", [PART, D]) for u in range(2)]
    xa = sb("xa", [PART, KC, 2, T])
    xb = sb("xb", [PART, KC, 2, T])
    xn = [sb(f"xn{u}", [PART, 2, KC, PART], F16) for u in range(2)]
    sq = sb("sq", [PART, 2, D])
    ssq = sb("ssq", [PART, 2 * HEADS])
    msq = sb("msq", [PART, 2 * HEADS])
    rqk = sb("rqk", [PART, 2 * HEADS])
    qn = sb("qn", [PART, 2, D])
    qkT = sb("qkT", [PART, 2, 2, KC, PART], F16)
    S = sb("S", [PART, HEADS, T])
    mx = sb("mx", [PART, 4, 4])
    den = sb("den", [PART, HEADS])
    rden = sb("rden", [PART, HEADS])
    PT = sb("PT", [PART, 2, HEADS // 2, PART], F16)
    oT = sb("oT", [PART, 2, KC, PART], F16)
    x1 = sb("x1", [PART, 2, KC, 2, T], F16)
    rows = [sb(f"rows{u}", [PART, D], F16) for u in range(2)]
    E = [sb(f"E{u}", [PART, 2, KC, D], F16) for u in range(2)]
    um = [sb(f"um{u}", [PART, 2, KC, T]) for u in range(2)]
    us = [sb(f"us{u}", [PART, KC, T]) for u in range(2)]

    def ps(name, shape):
        return ctx.enter_context(nc.psum_tensor(name, shape, F32))

    psQ = ps("psQ", [PART, 3, D])
    psS = ps("psS", [PART, 4, D])
    psO = ps("psO", [PART, KC, PART])
    psL = [psQ[:, b, :].rearrange("p (v c t) -> p v c t", v=2, c=KC) for b in range(2)]
    psP = psQ[:, 2, :].rearrange("p (c b t) -> p c b t", c=KC, b=2)

    def turned(j):
        return psS[:, j, :].rearrange("p (c n) -> p c n", c=KC)

    x_in = [sem(f"x_in{u}") for u in range(2)]
    rows_in = [sem(f"rows_in{u}") for u in range(2)]
    ssx_done, msx_done, rx_done, y_done = sem("ssx_done"), sem("msx_done"), sem("rx_done"), sem("y_done")
    xy_T, xT_kept, xa_done, xb_done = sem("xy_T"), sem("xT_kept"), sem("xa_done"), sem("xb_done")
    xn_hi, xn_ready = sem("xn_hi"), sem("xn_ready")
    qkv_done, sq_done, ssq_done = sem("qkv_done"), sem("sq_done"), sem("ssq_done")
    msq_done, rqk_done, qn_done = sem("msq_done"), sem("rqk_done"), sem("qn_done")
    v_hi, v_ready = sem("v_hi"), sem("v_ready")
    qk_T, qk_hi, qk_ready = sem("qk_T"), sem("qk_hi"), sem("qk_ready")
    sc_done, mx_done, sub_done, exp_done = sem("sc_done"), sem("mx_done"), sem("sub_done"), sem("exp_done")
    den_done, rden_done, p_done = sem("den_done"), sem("rden_done"), sem("p_done")
    p_T, pt_hi, pt_ready = sem("p_T"), sem("pt_hi"), sem("pt_ready")
    mix_done, o_hi, o_ready = sem("mix_done"), sem("o_hi"), sem("o_ready")
    proj_done, x1_done, x1_hi, x1_ready = sem("proj_done"), sem("x1_done"), sem("x1_hi"), sem("x1_ready")
    e_built, samp_done, um_done, us_done, x2_done = (sem(n) for n in ("e_built", "samp_done", "um_done", "us_done", "x2_done"))
    passed = sem("passed")
    block = ctx.enter_context(nc.Block())

    FIRST, LAST = -2, NP + 3
    LOOP0, NLOOP = 4, (NP - 3 - 4) // 2

    def run(eng, slot):
        def at(i):
            def pair(d):
                n = i + d
                return Pair(n, n // 2, n % 2) if 0 <= n < NP else None
            return pair
        for i in range(FIRST, LOOP0):
            slot(at(i))
        with eng.Fori(0, NLOOP) as it:
            for j in range(2):
                def pair(d, j=j):
                    c = LOOP0 + j + d
                    return Pair(it * 2 + c, it + c // 2, c % 2)
                slot(pair)
        for i in range(LOOP0 + 2 * NLOOP, LAST):
            slot(at(i))

    @block.sync
    def _(sp):
        def load_x(p):
            need(sp, xy_T, p.n - 1)
            sp.dma_start(xtok[p.u][:, :], x_rows(p)).then_inc(x_in[p.u], 16)

        def x_rows(p):
            return x[bass.ds(p.n * 2, 2), :, :].rearrange("b t d -> (b t) d")

        def load_rows(p):
            for b in range(2):
                need(sp, e_built, p.n * 2 + b - 1)
                sp.dma_start(rows[b][:, :], rows_dram[bass.ds(p.n * 2 + b, 1), :].rearrange("a n -> (a n)")
                             .partition_broadcast(PART)).then_inc(rows_in[b], 16)

        def slot(pair):
            if p := pair(2):
                load_x(p)
            if p := pair(-2):
                load_rows(p)

        run(sp, slot)

    @block.gpsimd
    def _(pool):
        def settled():
            pool.sem_inc(passed, 1)
            return nc.gpsimd

        def norm_x(p):
            pool.wait_ge(ssx_done, p.n + 1)
            settled().tensor_scalar(msx[:, p.u:p.u + 1], ssx[:, p.u:p.u + 1], 1.0 / D, EPS, ALU.mult, ALU.add).then_inc(msx_done, 1)
            pool.wait_ge(msx_done, p.n + 1)
            need(pool, y_done, p.n - 1)
            settled().tensor_tensor(rx[:, p.u:p.u + 1], msx[:, p.u:p.u + 1], mhalf[:, 0:1], ALU.pow).then_inc(rx_done, 1)

        def norm_qk(p):
            pool.wait_ge(ssq_done, p.n * 2 + 2)
            settled().tensor_scalar(msq[:, :], ssq[:, :], 1.0 / DH, EPS * WS * WS, ALU.mult, ALU.add).then_inc(msq_done, 1)
            pool.wait_ge(msq_done, p.n + 1)
            need(pool, qn_done, p.n * 2)
            settled().tensor_tensor(rqk[:, :], msq[:, :], mhalf[:, :], ALU.pow).then_inc(rqk_done, 1)

        def add_taps(p, b):
            pool.wait_ge(um_done, p.n * 2 + b + 1)
            need(pool, x2_done, p.n * 2 + b - 1)
            settled().tensor_tensor(us[b][:, :, :], um[b][:, 0, :, :], um[b][:, 1, :, :], ALU.add).then_inc(us_done, 1)
            pool.wait_ge(us_done, p.n * 2 + b + 1)
            r = XR[:, :, :, bass.ds(p.n * 2 + b, 1)].rearrange("p t c a -> p c (t a)")
            settled().tensor_tensor(r, r, us[b][:, :, :], ALU.add).then_inc(x2_done, 1)

        def norm_p(p):
            pool.wait_ge(rden_done, p.n + 1)
            settled().tensor_tensor(S[:, :, :], S[:, :, :], rden[:, :].unsqueeze(2).broadcast_to([PART, HEADS, T]), ALU.mult)\
                .then_inc(p_done, 1)

        def low_x1(p):
            pool.wait_ge(x1_hi, p.n * 2 + 2)
            need(pool, samp_done, p.n * 2)
            for b in range(2):
                last = settled().tensor_tensor(x1[:, 1, :, b, :], XR[:, :, :, bass.ds(p.n * 2 + b, 1)].rearrange("p t c a -> p c (t a)"),
                                       x1[:, 0, :, b, :], ALU.subtract)
            last.then_inc(x1_ready, 1)

        def shift_x(p):
            pool.wait_ge(xa_done, p.n + 1)
            need(pool, xn_hi, p.n)
            settled().tensor_tensor(xb[:, :, :, :], xa[:, :, :, :],
                            modB[:, :, bass.ds(p.n * 2, 2)].unsqueeze(3).broadcast_to([PART, KC, 2, T]), ALU.add)\
                .then_inc(xb_done, 1)

        def low_x(p):
            pool.wait_ge(xn_hi, p.n + 1)
            settled().tensor_tensor(xn[p.u][:, 1, :, :], xb[:, :, :, :].rearrange("p c b t -> p c (b t)"), xn[p.u][:, 0, :, :],
                            ALU.subtract).then_inc(xn_ready, 1)

        def slot(pair):
            if p := pair(2):
                norm_x(p)
            if p := pair(0):
                norm_qk(p)
            if p := pair(-3):
                add_taps(p, 0)
            if p := pair(-1):
                norm_p(p)
            if p := pair(-3):
                add_taps(p, 1)
            if p := pair(-2):
                low_x1(p)
            if p := pair(2):
                shift_x(p)
                low_x(p)

        run(pool, slot)

    @block.scalar
    def _(act):
        def a(out, in_, f=ACT.Copy, **k):
            return nc.scalar.activation(out, in_, f, **k)

        def squares_x(p):
            act.wait_ge(x_in[p.u], p.half * 16 + 16)
            need(act, msx_done, p.n - 1)
            a(sqx[:, :], xtok[p.u][:, :], ACT.Square, accum_out=ssx[:, p.u:p.u + 1]).then_inc(ssx_done, 1)

        def high_qk(p):
            act.wait_ge(qk_T, p.n + 1)
            need(act, sc_done, p.n)
            a(qkT[:, 0, 0, :, :], turned(0), scale=gqk[:, 0:1]).then_inc(qk_hi, 1)
            a(qkT[:, 0, 1, :, :], turned(1)).then_inc(qk_hi, 1)

        def squares_qk(p, n):
            act.wait_ge(qkv_done, p.n * 3 + n + 1)
            need(act, ssq_done, p.n * 2 + n - 1)
            a(sq[:, n, :], psQ[:, n, :], ACT.Square).then_inc(sq_done, 1)

        def high_v(p):
            act.wait_ge(qkv_done, p.n * 3 + 3)
            need(act, mix_done, p.n - 1)
            for b in range(2):
                for r in range(2):
                    src = psQ[b * T:(b + 1) * T, 2, :].rearrange("p (j r d) -> p j r d", r=2, d=DH)[:, :, r, :]
                    a(Vbd[p.u][r * T:(r + 1) * T, b, 0, :, r * DH:(r + 1) * DH], src).then_inc(v_hi, 1)

        def high_p(p):
            act.wait_ge(p_T, p.n + 1)
            need(act, mix_done, p.n)
            for h in range(2):
                a(PT[:, 0, 4 * h:4 * h + 4, :].rearrange("p (r j) n -> p r (j n)", r=2), psS[:, 2 * h:2 * h + 2, 256:512])\
                    .then_inc(pt_hi, 1)

        def exps(p):
            act.wait_ge(sub_done, p.n + 1)
            a(S[:, :, :], S[:, :, :], ACT.Exp).then_inc(exp_done, 1)

        def high_o(p):
            act.wait_ge(mix_done, p.n + 1)
            need(act, proj_done, p.n)
            a(oT[:, 0, :, :], psO[:, :, :]).then_inc(o_hi, 1)

        def high_x1(p):
            act.wait_ge(x1_done, p.n * 2 + 2)
            need(act, samp_done, p.n * 2)
            for b in range(2):
                a(x1[:, 0, :, b, :], XR[:, :, :, bass.ds(p.n * 2 + b, 1)].rearrange("p t c a -> p c (t a)")).then_inc(x1_hi, 1)

        def keep_xT(p):
            act.wait_ge(xy_T, p.n + 1)
            for b in range(2):
                last = a(XR[:, :, :, bass.ds(p.n * 2 + b, 1)].rearrange("p t c a -> p c (t a)"),
                         psS[:, 2, :].rearrange("p (c b t) -> p c b t", c=KC, b=2)[:, :, b, :])
            last.then_inc(xT_kept, 1)

        def high_x(p):
            act.wait_ge(xb_done, p.n + 1)
            need(act, qkv_done, (p.n - 1) * 3)
            a(xn[p.u][:, 0, :, :], xb[:, :, :, :].rearrange("p c b t -> p c (b t)")).then_inc(xn_hi, 1)

        def slot(pair):
            if p := pair(2):
                squares_x(p)
            if p := pair(0):
                squares_qk(p, 0)
            if p := pair(-2):
                high_p(p)
            if p := pair(0):
                squares_qk(p, 1)
            if p := pair(-1):
                high_qk(p)
            if p := pair(-2):
                high_o(p)
            if p := pair(0):
                high_v(p)
            if p := pair(-1):
                exps(p)
            if p := pair(-2):
                high_x1(p)
            if p := pair(2):
                keep_xT(p)
                high_x(p)

        run(act, slot)

    @block.vector
    def _(dve):
        v = nc.vector

        def low_qk(p):
            for n in range(2):
                dve.wait_ge(qk_hi, p.n * 2 + n + 1)
                need(dve, sc_done, p.n)
                if n == 0:
                    last = v.scalar_tensor_tensor(out=qkT[:, 1, 0, :, :], in0=turned(0), scalar=gqk[:, 0:1],
                                                  in1=qkT[:, 0, 0, :, :], op0=ALU.mult, op1=ALU.subtract)
                else:
                    last = v.tensor_tensor(qkT[:, 1, 1, :, :], turned(1), qkT[:, 0, 1, :, :], ALU.subtract)
            last.then_inc(qk_ready, 1)

        def scale_x(p):
            dve.wait_ge(rx_done, p.n + 1)
            dve.wait_ge(x_in[p.u], p.half * 16 + 16)
            need(dve, xy_T, p.n - 1)
            v.tensor_scalar(yt[p.u][:, :], xtok[p.u][:, :], rx[:, p.u:p.u + 1], None, ALU.mult).then_inc(y_done, 1)

        def build_taps(p, b):
            dve.wait_ge(rows_in[b], p.n * 16 + 16)
            need(dve, samp_done, p.n * 2 + b - 1)
            for t in range(2):
                for c in range(KC):
                    last = v.tensor_scalar(E[b][:, t, c, :], rows[b][:, :], lidx[:, t, c:c + 1], None, ALU.is_equal)
            last.then_inc(e_built, 1)

        def sums_qk(p, n):
            dve.wait_ge(sq_done, p.n * 2 + n + 1)
            need(dve, msq_done, p.n)
            v.tensor_reduce(ssq[:, n * HEADS:(n + 1) * HEADS], sq[:, n, :].rearrange("p (h d) -> p h d", d=DH), AX.X, ALU.add)\
                .then_inc(ssq_done, 1)

        def scale_qk(p):
            dve.wait_ge(rqk_done, p.n + 1)
            need(dve, qk_T, p.n)
            for n in range(2):
                v.tensor_tensor(qn[:, n, :].rearrange("p (h d) -> p h d", d=DH), psQ[:, n, :].rearrange("p (h d) -> p h d", d=DH),
                                rqk[:, n * HEADS:(n + 1) * HEADS].unsqueeze(2).broadcast_to([PART, HEADS, DH]), ALU.mult)\
                    .then_inc(qn_done, 1)

        def low_v(p):
            for b in range(2):
                for r in range(2):
                    dve.wait_ge(v_hi, p.n * 4 + 2 * b + 2)
                    src = psQ[b * T:(b + 1) * T, 2, :].rearrange("p (j r d) -> p j r d", r=2, d=DH)[:, :, r, :]
                    dst = Vbd[p.u][r * T:(r + 1) * T, b, :, :, r * DH:(r + 1) * DH]
                    last = v.tensor_tensor(dst[:, 1, :, :], src, dst[:, 0, :, :], ALU.subtract)
            last.then_inc(v_ready, 1)

        def low_p(p):
            for h in range(2):
                dve.wait_ge(pt_hi, p.n * 2 + h + 1)
                hi, lo = (PT[:, i, 4 * h:4 * h + 4, :].rearrange("p (r j) n -> p r (j n)", r=2) for i in range(2))
                last = v.tensor_tensor(lo, psS[:, 2 * h:2 * h + 2, 256:512], hi, ALU.subtract)
            last.then_inc(pt_ready, 1)

        def subtract_max(p):
            sc = psS[:, :, 0:256].rearrange("p r (c k) -> p r c k", c=4)
            dve.wait_ge(sc_done, p.n + 1)
            v.tensor_reduce(mx[:, :, :], sc, AX.X, ALU.max).then_inc(mx_done, 1)
            dve.wait_ge(mx_done, p.n + 1)
            need(dve, p_T, p.n)
            v.tensor_tensor(S[:, :, :].rearrange("p (c r) k -> p r c k", r=4), sc,
                            mx[:, :, :].unsqueeze(3).broadcast_to([PART, 4, 4, T]), ALU.subtract).then_inc(sub_done, 1)

        def weigh_taps(p, b):
            dve.wait_ge(samp_done, p.n * 2 + b + 1)
            need(dve, us_done, p.n * 2 + b - 1)
            v.tensor_tensor(um[b][:, :, :, :].rearrange("p v c t -> p (v c) t"),
                            psL[b].rearrange("p v c t -> p (v c) t"),
                            WT[:, :, :, bass.ds(p.n * 2 + b, 1)].rearrange("p v c a -> p (v c) a").broadcast_to([PART, 2 * KC, T]),
                            ALU.mult).then_inc(um_done, 1)

        def sum_p(p):
            dve.wait_ge(exp_done, p.n + 1)
            v.tensor_reduce(den[:, :], S[:, :, :], AX.X, ALU.add).then_inc(den_done, 1)
            dve.wait_ge(den_done, p.n + 1)
            need(dve, p_done, p.n)
            v.reciprocal(rden[:, :], den[:, :]).then_inc(rden_done, 1)

        def low_o(p):
            dve.wait_ge(o_hi, p.n + 1)
            v.tensor_tensor(oT[:, 1, :, :], psO[:, :, :], oT[:, 0, :, :], ALU.subtract).then_inc(o_ready, 1)

        def residual(p):
            dve.wait_ge(proj_done, p.n + 1)
            dve.wait_ge(xT_kept, p.n + 1)
            for b in range(2):
                r = XR[:, :, :, bass.ds(p.n * 2 + b, 1)].rearrange("p t c a -> p c (t a)")
                v.scalar_tensor_tensor(out=r, in0=psP[:, :, b, :], scalar=1.0 / (WS * WS), in1=r,
                                       op0=ALU.mult, op1=ALU.add).then_inc(x1_done, 1)

        def modulate(p):
            dve.wait_ge(xy_T, p.n + 1)
            need(dve, xb_done, p.n)
            v.tensor_tensor(xa[:, :, :, :], psS[:, 3, :].rearrange("p (c b t) -> p c b t", c=KC, b=2),
                            modA[:, :, bass.ds(p.n * 2, 2)].unsqueeze(3).broadcast_to([PART, KC, 2, T]), ALU.mult)\
                .then_inc(xa_done, 1)

        def slot(pair):
            if p := pair(2):
                scale_x(p)
            if p := pair(-3):
                build_taps(p, 0)
            if p := pair(0):
                sums_qk(p, 0)
            if p := pair(-2):
                low_p(p)
            if p := pair(-3):
                build_taps(p, 1)
            if p := pair(0):
                sums_qk(p, 1)
            if p := pair(-1):
                low_qk(p)
            if p := pair(0):
                scale_qk(p)
            if p := pair(-2):
                low_o(p)
            if p := pair(0):
                low_v(p)
            if p := pair(-1):
                subtract_max(p)
            if p := pair(-3):
                weigh_taps(p, 0)
            if p := pair(-1):
                sum_p(p)
            if p := pair(-3):
                weigh_taps(p, 1)
            if p := pair(-2):
                residual(p)
            if p := pair(2):
                modulate(p)

        run(dve, slot)

    @block.tensor
    def _(pe):
        mm = nc.tensor.matmul
        TERMS = ((0, 0), (0, 1), (1, 0))

        def turn_qk(p):
            pe.wait_ge(qn_done, p.n * 2 + 2)
            need(pe, sub_done, p.n)
            need(pe, pt_ready, p.n)
            need(pe, qk_ready, p.n)
            for n in range(2):
                for c in range(KC):
                    last = nc.tensor.transpose(turned(n)[:, c, :], qn[:, n, c * PART:(c + 1) * PART], ident[:, :])
            last.then_inc(qk_T, 1)

        def project(p, n):
            if n == 0:
                pe.wait_ge(xn_ready, p.n + 1)
            if n == 0:
                need(pe, qn_done, p.n * 2 - 1)
                need(pe, um_done, p.n * 2 - 7)
            elif n == 1:
                need(pe, qn_done, p.n * 2)
                need(pe, um_done, p.n * 2 - 6)
            else:
                need(pe, v_ready, p.n)
                need(pe, x1_done, p.n * 2 - 4)
            for c in range(KC):
                for t, (i, j) in enumerate(TERMS):
                    last = mm(psQ[:, n, :], xn[p.u][:, i, c, :], Wqkv[:, j, c, n * D:(n + 1) * D],
                              start=(c == 0 and t == 0), stop=(c == KC - 1 and t == 2))
            last.then_inc(qkv_done, 1)

        def turn_p(p):
            pe.wait_ge(p_done, p.n + 1)
            need(pe, pt_ready, p.n)
            late = p.later(3, NP)
            if late is not None:
                need(pe, xT_kept, late + 1)
                need(pe, xa_done, late + 1)
            for j in range(HEADS // 2):
                o = psS[:, j // 2, 256 + (j % 2) * PART:256 + (j % 2 + 1) * PART]
                last = nc.tensor.transpose(o, S[:, 2 * j:2 * j + 2, :].rearrange("p h k -> p (h k)"), ident[:, :])
            last.then_inc(p_T, 1)

        def scores(p):
            pe.wait_ge(qk_ready, p.n + 1)
            late = p.later(2, NP)
            if late is not None:
                need(pe, xT_kept, late + 1)
                need(pe, xa_done, late + 1)
            need(pe, sub_done, p.n)
            need(pe, pt_ready, p.n)
            for c in range(4):
                for b in range(2):
                    for t, (i, j) in enumerate(TERMS):
                        for r in range(4):
                            rows_ = slice(r * DH, (r + 1) * DH)
                            last = mm(psS[b * T:(b + 1) * T, r, c * T:(c + 1) * T],
                                      qkT[rows_, i, 0, c, b * T:(b + 1) * T], qkT[rows_, j, 1, c, b * T:(b + 1) * T],
                                      start=(t == 0), stop=(t == 2))
            last.then_inc(sc_done, 1)

        def sample(p, b):
            pe.wait_ge(e_built, p.n * 2 + b + 1)
            pe.wait_ge(x1_ready, p.n + 1)
            late = p.later(3, NP)
            if late is not None:
                need(pe, qn_done, late * 2 + b + 1)
            need(pe, um_done, p.n * 2 + b - 1)
            o = psL[b]
            for t in range(2):
                for m in range(KC):
                    for c in range(KC):
                        for i in range(2):
                            last = mm(o[:, t, m, :], E[b][:, t, c, m * PART:(m + 1) * PART], x1[:, i, c, b, :],
                                      start=(c == 0 and i == 0), stop=(c == KC - 1 and i == 1))
            last.then_inc(samp_done, 1)

        def mix(p):
            pe.wait_ge(pt_ready, p.n + 1)
            pe.wait_ge(v_ready, p.n + 1)
            need(pe, o_ready, p.n)
            for j in range(HEADS // 2):
                for b in range(2):
                    for t, (i, k) in enumerate(TERMS):
                        last = mm(psO[(j % 2) * 64:(j % 2 + 1) * 64, j // 2, b * T:(b + 1) * T],
                                  Vbd[p.u][:, b, i, j, :], PT[:, k, j, b * T:(b + 1) * T], start=(t == 0), stop=(t == 2))
            last.then_inc(mix_done, 1)

        def proj(p):
            pe.wait_ge(o_ready, p.n + 1)
            late = p.later(2, NP)
            if late is not None:
                need(pe, v_ready, late + 1)
            need(pe, x1_done, p.n * 2)
            for m in range(KC):
                for c in range(KC):
                    for t, (i, j) in enumerate(TERMS):
                        last = mm(psP[:, m, :, :].rearrange("p b t -> p (b t)"), Wo[:, i, c, m * PART:(m + 1) * PART], oT[:, j, c, :],
                                  start=(c == 0 and t == 0), stop=(c == KC - 1 and t == 2))
            last.then_inc(proj_done, 1)

        def turn_x(p):
            pe.wait_ge(y_done, p.n + 1)
            pe.wait_ge(x_in[p.u], p.half * 16 + 16)
            need(pe, sub_done, p.n - 2)
            need(pe, pt_ready, p.n - 3)
            need(pe, xT_kept, p.n)
            need(pe, xa_done, p.n)
            for n, src in ((2, xtok[p.u]), (3, yt[p.u])):
                for c in range(KC):
                    last = nc.tensor.transpose(turned(n)[:, c, :], src[:, c * PART:(c + 1) * PART], ident[:, :])
            last.then_inc(xy_T, 1)

        def slot(pair):
            if p := pair(0):
                project(p, 0)
            if p := pair(-2):
                turn_p(p)
            if p := pair(0):
                project(p, 1)
            if p := pair(-1):
                turn_qk(p)
            if p := pair(-2):
                mix(p)
            if p := pair(0):
                project(p, 2)
            if p := pair(-1):
                scores(p)
            if p := pair(-3):
                sample(p, 0)
                sample(p, 1)
            if p := pair(-2):
                proj(p)
            if p := pair(2):
                turn_x(p)

        run(pe, slot)


def recurrences(nc, ctx, XR, condT, ident, W_ih, W_hh, b_ih, b_hh, coupling, bias, out):
    B, T, D = out.shape
    KC = D // PART
    G3 = W_ih.shape[1]
    GC = G3 // PART
    H2, H1 = DT, DT / 2
    K1, K2 = H1 * EPSILON, H2 * EPSILON

    def sb(name, shape, dt=F32, stack=ctx):
        return stack.enter_context(nc.sbuf_tensor(name, shape, dt))

    def sem(name, stack=ctx):
        return stack.enter_context(nc.semaphore(name))

    Wih = sb("Wih", [PART, 2, KC, G3], F16)
    Whh = sb("Whh", [PART, 2, KC, G3], F16)
    Cp = sb("Cp", [PART, 2, KC, D], F16)
    brow = sb("brow", [PART, G3 + D], F16)
    ones = sb("ones", [PART, B], F16)
    biasT = sb("biasT", [PART, KC])
    biasF = sb("biasF", [PART, KC, B])

    with ExitStack() as s:
        wih32 = sb("wih32", [PART, KC, G3], F32, s)
        whh32 = sb("whh32", [PART, KC, G3], F32, s)
        cp32 = sb("cp32", [PART, KC, D], F32, s)
        brow32 = sb("brow32", [1, G3 + D], F32, s)
        bhh32 = sb("bhh32", [1, G3], F32, s)
        brow_lo = sb("brow_lo", [1, G3 + D], F16, s)
        psC = [s.enter_context(nc.psum_tensor(f"psC{c}", [PART, D], F32)) for c in range(KC)]
        w_in = [sem(f"w_in{n}", s) for n in range(3)]
        bias_in, zeros, sum_done, cT_done, hi_done, brow_done = (
            sem(n, s) for n in ("bias_in", "zeros", "sum_done", "cT_done", "hi_done2", "brow_done"))
        block = s.enter_context(nc.Block())

        @block.sync
        def _(sp):
            sp.dma_start(cp32[:, :, :], coupling.rearrange("(c p) n -> p c n", p=PART)).then_inc(w_in[0], 16)
            sp.dma_start(wih32[:, :, :], W_ih.rearrange("(c p) n -> p c n", p=PART)).then_inc(w_in[1], 16)
            sp.dma_start(whh32[:, :, :], W_hh.rearrange("(c p) n -> p c n", p=PART)).then_inc(w_in[2], 16)

        @block.gpsimd
        def _(pool):
            nc.gpsimd.memset(brow[:, :], 0.0).then_inc(zeros, 1)
            nc.gpsimd.memset(ones[:, :], 1.0)
            nc.gpsimd.memset(biasF[:, :, :], 0.0).then_inc(zeros, 1)

        @block.scalar
        def _(act):
            act.dma_start(brow32[:, 0:G3], b_ih.rearrange("(a n) -> a n", a=1)).then_inc(bias_in, 16)
            act.dma_start(bhh32[:, :], b_hh.rearrange("(a n) -> a n", a=1)).then_inc(bias_in, 16)
            act.dma_start(brow32[:, G3:G3 + D], b_hh[2 * D:3 * D].rearrange("(a n) -> a n", a=1)).then_inc(bias_in, 16)
            with nc.allow_non_contiguous_dma("a small vector, laid along the partitions"):
                act.dma_start(biasT[:, :], bias.rearrange("(c p) -> p c", p=PART)).then_inc(bias_in, 16)
            act.wait_ge(sum_done, 1)
            act.wait_ge(zeros, 1)
            nc.scalar.activation(brow[0:1, :], brow32[:, :], ACT.Copy, scale=WS).then_inc(brow_done, 1)
            for c in range(KC):
                act.wait_ge(cT_done, c + 1)
                nc.scalar.activation(Cp[:, 0, c, :], psC[c][:, :], ACT.Copy, scale=WS).then_inc(hi_done, 1)
            for n, (w, w32) in enumerate(((Wih, wih32), (Whh, whh32))):
                act.wait_ge(w_in[n + 1], 16)
                for c in range(KC):
                    nc.scalar.activation(w[:, 0, c, :], w32[:, c, :], ACT.Copy, scale=WS).then_inc(hi_done, 1)

        @block.vector
        def _(dve):
            v = nc.vector
            dve.wait_ge(bias_in, 64)
            v.tensor_tensor(brow32[:, 0:2 * D], brow32[:, 0:2 * D], bhh32[:, 0:2 * D], ALU.add).then_inc(sum_done, 1)
            dve.wait_ge(zeros, 2)
            for c in range(KC):
                v.tensor_scalar(biasF[:, c, :], biasF[:, c, :], biasT[:, c:c + 1], None, ALU.add)
            dve.wait_ge(brow_done, 1)
            v.scalar_tensor_tensor(out=brow_lo[:, :], in0=brow32[:, :], scalar=WS, in1=brow[0:1, :],
                                   op0=ALU.mult, op1=ALU.subtract).then_inc(brow_done, 1)
            dve.wait_ge(brow_done, 2)
            v.tensor_copy(brow[32:33, :], brow_lo[:, :])
            for c in range(KC):
                dve.wait_ge(hi_done, c + 1)
                v.scalar_tensor_tensor(out=Cp[:, 1, c, :], in0=psC[c][:, :], scalar=WS, in1=Cp[:, 0, c, :],
                                       op0=ALU.mult, op1=ALU.subtract)
            for n, (w, w32) in enumerate(((Wih, wih32), (Whh, whh32))):
                for c in range(KC):
                    dve.wait_ge(hi_done, (n + 1) * KC + c + 1)
                    v.scalar_tensor_tensor(out=w[:, 1, c, :], in0=w32[:, c, :], scalar=WS, in1=w[:, 0, c, :],
                                           op0=ALU.mult, op1=ALU.subtract)

        @block.tensor
        def _(pe):
            pe.wait_ge(w_in[0], 16)
            for c in range(KC):
                for n in range(KC):
                    last = nc.tensor.transpose(psC[c][:, n * PART:(n + 1) * PART], cp32[:, n, c * PART:(c + 1) * PART], ident[:, :])
                last.then_inc(cT_done, 1)

    def two(name, shape, dt=F32):
        return [sb(f"{name}{u}", shape, dt) for u in range(2)]

    F = [PART, KC, B]
    xs = sb("xs", [PART, 2, KC, B], F16)
    hs = sb("hs", [PART, 2, KC, B], F16)
    Hf = two("Hf", F)
    rz = sb("rz", [PART, 2, KC, B])
    an, bn, nn, dn, en = (sb(n, F) for n in ("an", "bn", "nn", "dn", "en"))
    xbias, X3, Dr = two("xbias", F), two("X3", F), two("Dr", F)
    Qs, Ps = two("Qs", F), two("Ps", F)
    qs = [sb(f"qs{s}", F) for s in range(3)]
    th = sb("th", F)
    ts_ = sb("ts", [PART, 2, KC, B], F16)
    sqs, ws, rs = two("sqs", F), two("ws", F), two("rs", F)
    Zp, Gd, Gs, E1, E2 = (sb(n, F) for n in ("Zp", "Gd", "Gs", "Ea", "Eb"))
    yz = two("yz", F)
    ys = [sb(f"ys{s}", F) for s in range(4)]
    e2, e3, gs, aq, bq, cq, hq, qp = (sb(n, F) for n in ("e2", "e3", "gs", "aq", "bq", "cq", "hq", "qp"))
    y23, y14, sy, pp = (sb(n, F) for n in ("y23", "y14", "sy", "pp"))
    ob, ot = two("ob", F), two("ot", F)

    psRZ = [ctx.enter_context(nc.psum_tensor(f"psRZ{u}", [PART, 2, KC, B], F32)) for u in range(2)]
    psN = [ctx.enter_context(nc.psum_tensor(f"psN{u}", [PART, 2, KC, B], F32)) for u in range(2)]
    psF = ctx.enter_context(nc.psum_tensor("psF", [PART, 2, KC, B], F32))

    names = ("xs_hi xs_ready xs_used gi_done rz_done gn_done sig_done an_done bn_done nn_done dn_done en_done h_done hs_hi hs_ready "
             "xbias_done X3_done Dr_done Z_done y1_done G_done Gs_done E_done th_done ts_hi ts_ready sq_done w_done r_done f_done "
             "q_done yz_done y_done e_done gs_done aq_done bq_done cq_done hq_done qp_done Q_done y23_done y14_done sy_done "
             "pp_done P_done ob_done ot_done passed")
    S = {n: sem("s_" + n) for n in names.split()}
    out_sent = [sem(f"out_sent{u}") for u in range(2)]
    block = ctx.enter_context(nc.Block())
    PEEL = 2

    def run(eng, first, step):
        first()
        for t in range(PEEL):
            step(Pair(t, t // 2, t % 2))
        with eng.Fori(0, (T - 2 * PEEL) // 2) as it:
            for u in range(2):
                step(Pair(it * 2 + PEEL + u, it + PEEL // 2, u))
        for t in range(T - PEEL, T):
            step(Pair(t, t // 2, t % 2))

    def has(t, d):
        return not isinstance(t.n, int) or t.n + d < T

    def xr(n):
        return XR[:, bass.ds(n, 1), :, :].rearrange("p a c b -> p (a c b)")

    def flat(ap):
        return ap.rearrange("p c b -> p (c b)")

    @block.tensor
    def _(pe):
        mm = nc.tensor.matmul
        TERMS = ((0, 0), (0, 1), (1, 0))

        def bias_products(u):
            for g in range(8):
                mm(psRZ[u][:, g // KC, g % KC, :], brow[:, g * PART:(g + 1) * PART], ones[:, :], start=(g == 0), stop=False,
                   skip_group_check=True)
            for g in range(8):
                o = G3 + g * PART if g < KC else 2 * D + (g - KC) * PART
                mm(psN[u][:, g // KC, g % KC, :], brow[:, o:o + PART], ones[:, :], start=(g == 0), stop=False,
                   skip_group_check=True)

        def gate_products(u, W, src, part, gates):
            for g in gates:
                o = psRZ[u][:, g // KC, g % KC, :] if g < 2 * KC else psN[u][:, part, g - 2 * KC, :]
                for c in range(KC):
                    for i, j in TERMS:
                        last = mm(o, W[:, i, c, g * PART:(g + 1) * PART], src[:, j, c, :], start=False,
                                  stop=(part == 0 and c == KC - 1 and (i, j) == TERMS[-1]), skip_group_check=True)
            return last

        def gi(n, u, half):
            if half == 0:
                need(pe, S["sig_done"], n - 1)
                need(pe, S["bn_done"], n - 1)
                pe.wait_ge(S["xs_ready"], n + 1)
                bias_products(u)
                gate_products(u, Wih, xs, 1, range(0, GC // 2))
            else:
                gate_products(u, Wih, xs, 1, range(GC // 2, GC)).then_inc(S["gi_done"], 1)

        def gh(n, u, half):
            if half == 0:
                pe.wait_ge(S["hs_ready"], n + 1)
                gate_products(u, Whh, hs, 0, range(0, GC // 2))
            else:
                gate_products(u, Whh, hs, 0, range(GC // 2, 2 * KC)).then_inc(S["rz_done"], 1)
                gate_products(u, Whh, hs, 0, range(2 * KC, GC)).then_inc(S["gn_done"], 1)

        def stage(t, s):
            pe.wait_ge(S["ts_ready"], t.n * 4 + s + 1)
            for c in range(KC):
                for m in range(KC):
                    for i, j in TERMS:
                        last = mm(psF[:, s % 2, m, :], Cp[:, i, c, m * PART:(m + 1) * PART], ts_[:, j, c, :],
                                  start=(c == 0 and m == 0 and (i, j) == TERMS[0]), stop=(c == KC - 1 and (i, j) == TERMS[-1]),
                                  skip_group_check=True)
            last.then_inc(S["f_done"], 1)

        def first():
            gi(0, 0, 0)
            gi(0, 0, 1)
            gh(0, 0, 0)
            gh(0, 0, 1)
            gi(1, 1, 0)
            gi(1, 1, 1)

        def step(t):
            stage(t, 0)
            if has(t, 1):
                gh(t.n + 1, 1 - t.u, 0)
            stage(t, 1)
            if has(t, 1):
                gh(t.n + 1, 1 - t.u, 1)
            stage(t, 2)
            if has(t, 2):
                gi(t.n + 2, t.u, 0)
            stage(t, 3)
            if has(t, 2):
                gi(t.n + 2, t.u, 1)

        run(pe, first, step)

    @block.scalar
    def _(act):
        def a(out, in_, f=ACT.Copy, **k):
            return nc.scalar.activation(out, in_, f, **k)

        def high_xs(n):
            need(act, S["gi_done"], n)
            a(xs[:, 0, :, :].rearrange("p c b -> p (c b)"), xr(n)).then_inc(S["xs_hi"], 1)

        def sigmoids(n, u):
            act.wait_ge(S["rz_done"], n + 1)
            need(act, S["en_done"], n)
            a(rz[:, :, :, :], psRZ[u][:, :, :, :], ACT.Sigmoid, scale=1.0 / WS).then_inc(S["sig_done"], 1)

        def tanh_n(n):
            act.wait_ge(S["bn_done"], n + 1)
            need(act, S["h_done"], n)
            a(nn[:, :, :], bn[:, :, :], ACT.Tanh, scale=1.0 / WS).then_inc(S["nn_done"], 1)

        def high_h(n, u):
            act.wait_ge(S["h_done"], n + 1)
            need(act, S["gn_done"], n + 1)
            a(hs[:, 0, :, :], Hf[u][:, :, :]).then_inc(S["hs_hi"], 1)

        def stage(t, s):
            q = qs[s - 1] if s else Qs[t.u]
            if s:
                act.wait_ge(S["q_done"], t.n * 3 + s)
            else:
                act.wait_ge(S["Q_done"], t.n + 1)
            need(act, S["ts_ready"], t.n * 4 + s)
            a(th[:, :, :], q[:, :, :], ACT.Tanh).then_inc(S["th_done"], 1)
            need(act, S["f_done"], t.n * 4 + s)
            a(ts_[:, 0, :, :], q[:, :, :], ACT.Tanh).then_inc(S["ts_hi"], 1)
            need(act, S["w_done"], t.n * 4 + s - 1)
            a(sqs[s % 2][:, :, :], q[:, :, :], ACT.Square).then_inc(S["sq_done"], 1)

        def first():
            high_xs(0)
            a(hs[:, 0, :, :], condT[:, :, :]).then_inc(S["hs_hi"], 1)
            a(Qs[0][:, :, :], condT[:, :, :]).then_inc(S["Q_done"], 1)
            high_xs(1)
            sigmoids(0, 0)
            tanh_n(0)
            high_h(0, 0)

        def step(t):
            stage(t, 0)
            if has(t, 2):
                high_xs(t.n + 2)
            need(act, S["G_done"], t.n + 1)
            need(act, S["gs_done"], t.n)
            a(Gs[:, :, :], Gd[:, :, :], scale=DT / 6).then_inc(S["Gs_done"], 1)
            stage(t, 1)
            stage(t, 2)
            if has(t, 1):
                sigmoids(t.n + 1, 1 - t.u)
            stage(t, 3)
            if has(t, 1):
                tanh_n(t.n + 1)
                high_h(t.n + 1, 1 - t.u)

        run(act, first, step)

    @block.vector
    def _(dve):
        v = nc.vector

        def stt(out, in0, scalar, in1, op1=ALU.add):
            return v.scalar_tensor_tensor(out=flat(out), in0=flat(in0), scalar=scalar, in1=flat(in1), op0=ALU.mult, op1=op1)

        def gate_n(n, u):
            dve.wait_ge(S["sig_done"], n + 1)
            dve.wait_ge(S["gn_done"], n + 1)
            v.tensor_tensor(an[:, :, :], psN[u][:, 0, :, :], rz[:, 0, :, :], ALU.mult).then_inc(S["an_done"], 1)
            dve.wait_ge(S["an_done"], n + 1)
            need(dve, S["nn_done"], n)
            v.tensor_tensor(bn[:, :, :], psN[u][:, 1, :, :], an[:, :, :], ALU.add).then_inc(S["bn_done"], 1)

        def new_h(n, u, old):
            dve.wait_ge(S["nn_done"], n + 1)
            v.tensor_tensor(dn[:, :, :], old[:, :, :], nn[:, :, :], ALU.subtract).then_inc(S["dn_done"], 1)
            dve.wait_ge(S["dn_done"], n + 1)
            v.tensor_tensor(en[:, :, :], dn[:, :, :], rz[:, 1, :, :], ALU.mult).then_inc(S["en_done"], 1)
            dve.wait_ge(S["en_done"], n + 1)
            need(dve, S["X3_done"], n - 1)
            need(dve, S["Dr_done"], n - 1)
            need(dve, S["hs_ready"], n)
            v.tensor_tensor(Hf[u][:, :, :], nn[:, :, :], en[:, :, :], ALU.add).then_inc(S["h_done"], 1)

        def low_t(t, s):
            dve.wait_ge(S["ts_hi"], t.n * 4 + s + 1)
            v.tensor_tensor(ts_[:, 1, :, :], th[:, :, :], ts_[:, 0, :, :], ALU.subtract).then_inc(S["ts_ready"], 1)

        def cubic(t, s, q):
            dve.wait_ge(S["sq_done"], t.n * 4 + s + 1)
            v.scalar_tensor_tensor(out=flat(ws[s % 2][:, :, :]), in0=flat(sqs[s % 2][:, :, :]), scalar=-3.0, in1=flat(q[:, :, :]),
                                   op0=ALU.add, op1=ALU.mult).then_inc(S["w_done"], 1)
            dve.wait_ge(S["w_done"], t.n * 4 + s + 1)

        def first():
            gate_n(0, 0)
            new_h(0, 0, condT)

        def step(t):
            n = t.n
            Q, P, Qn, Pn = Qs[t.u], Ps[t.u], Qs[1 - t.u], Ps[1 - t.u]
            q2, q3, q4 = qs
            low_t(t, 0)
            dve.wait_ge(S["G_done"], n + 1)
            stt(E1, Gd, H1, Q).then_inc(S["E_done"], 1)
            stt(E2, Gd, H2, Q).then_inc(S["E_done"], 1)
            cubic(t, 0, Q)
            dve.wait_ge(S["E_done"], n * 2 + 1)
            stt(rs[0], ws[0], -H1 / 3, E1).then_inc(S["r_done"], 1)
            dve.wait_ge(S["r_done"], n * 4 + 1)
            dve.wait_ge(S["f_done"], n * 4 + 1)
            stt(q2, psF[:, 0, :, :], H1 / WS, rs[0]).then_inc(S["q_done"], 1)
            dve.wait_ge(S["y1_done"], n + 1)
            stt(e2, ys[0], -H1 * K1, E1).then_inc(S["e_done"], 1)
            low_t(t, 1)
            cubic(t, 1, q2)
            dve.wait_ge(S["e_done"], n * 2 + 1)
            stt(rs[1], ws[1], -H1 / 3, e2).then_inc(S["r_done"], 1)
            dve.wait_ge(S["yz_done"], n * 3 + 1)
            stt(ys[1], ys[0], -BETA * K1, yz[0]).then_inc(S["y_done"], 1)
            dve.wait_ge(S["r_done"], n * 4 + 2)
            dve.wait_ge(S["f_done"], n * 4 + 2)
            stt(q3, psF[:, 1, :, :], H1 / WS, rs[1]).then_inc(S["q_done"], 1)
            dve.wait_ge(S["y_done"], n * 3 + 1)
            dve.wait_ge(S["E_done"], n * 2 + 2)
            stt(e3, ys[1], -H2 * K1, E2).then_inc(S["e_done"], 1)
            low_t(t, 2)
            dve.wait_ge(S["q_done"], n * 3 + 2)
            need(dve, S["cq_done"], n)
            stt(aq, q3, 2.0, q2).then_inc(S["aq_done"], 1)
            cubic(t, 2, q3)
            dve.wait_ge(S["e_done"], n * 2 + 2)
            stt(rs[0], ws[0], -H2 / 3, e3).then_inc(S["r_done"], 1)
            dve.wait_ge(S["yz_done"], n * 3 + 2)
            stt(ys[2], ys[1], -BETA * K1, yz[1]).then_inc(S["y_done"], 1)
            dve.wait_ge(S["r_done"], n * 4 + 3)
            dve.wait_ge(S["f_done"], n * 4 + 3)
            stt(q4, psF[:, 0, :, :], H2 / WS, rs[0]).then_inc(S["q_done"], 1)
            if has(t, 1):
                gate_n(n + 1, 1 - t.u)
            low_t(t, 3)
            dve.wait_ge(S["y_done"], n * 3 + 2)
            dve.wait_ge(S["Gs_done"], n + 1)
            stt(gs, ys[2], -2 * K1 * DT / 6, Gs).then_inc(S["gs_done"], 1)
            cubic(t, 3, q4)
            dve.wait_ge(S["gs_done"], n + 1)
            dve.wait_ge(S["cq_done"], n + 1)
            stt(hq, cq, 1.0 / 3, gs).then_inc(S["hq_done"], 1)
            dve.wait_ge(S["hq_done"], n + 1)
            stt(rs[1], ws[1], -DT / 18, hq).then_inc(S["r_done"], 1)
            dve.wait_ge(S["yz_done"], n * 3 + 3)
            stt(ys[3], ys[2], -BETA * K2, yz[0]).then_inc(S["y_done"], 1)
            if has(t, 1):
                new_h(n + 1, 1 - t.u, Hf[t.u])
            dve.wait_ge(S["r_done"], n * 4 + 4)
            dve.wait_ge(S["f_done"], n * 4 + 4)
            stt(qp, psF[:, 1, :, :], DT / 6 / WS, rs[1]).then_inc(S["qp_done"], 1)
            dve.wait_ge(S["qp_done"], n + 1)
            need(dve, S["ob_done"], n)
            v.tensor_scalar(flat(Qn), flat(qp), CLAMP, -CLAMP, ALU.min, ALU.max).then_inc(S["Q_done"], 1)
            dve.wait_ge(S["y14_done"], n + 1)
            stt(sy, y23, 2.0, y14).then_inc(S["sy_done"], 1)
            dve.wait_ge(S["sy_done"], n + 1)
            stt(pp, sy, DT * EPSILON / 6, P).then_inc(S["pp_done"], 1)
            dve.wait_ge(S["ob_done"], n + 1)
            if has(t, 0):
                need(dve, out_sent[t.u], t.half * (8 * 16))
            v.transpose(flat(ot[t.u]), flat(ob[t.u])).then_inc(S["ot_done"], 1)

        run(dve, first, step)

    @block.gpsimd
    def _(pool):
        def settled():
            pool.sem_inc(S["passed"], 1)
            return nc.gpsimd

        def tt(out, in0, in1, op=ALU.add):
            return settled().tensor_tensor(flat(out), flat(in0), flat(in1), op)

        def low_xs(n):
            pool.wait_ge(S["xs_hi"], n + 1)
            settled().tensor_tensor(xs[:, 1, :, :].rearrange("p c b -> p (c b)"), xr(n), xs[:, 0, :, :].rearrange("p c b -> p (c b)"),
                            ALU.subtract).then_inc(S["xs_ready"], 1)

        def low_h(n, src):
            pool.wait_ge(S["hs_hi"], n + 1)
            tt(hs[:, 1, :, :], src, hs[:, 0, :, :], ALU.subtract).then_inc(S["hs_ready"], 1)

        def with_bias(n, u):
            settled().tensor_tensor(flat(xbias[u]), xr(n), flat(biasF), ALU.add).then_inc(S["xbias_done"], 1)

        def drive(n, u):
            pool.wait_ge(S["h_done"], n + 1)
            pool.wait_ge(S["xbias_done"], n + 1)
            tt(Dr[u], xbias[u], Hf[u]).then_inc(S["Dr_done"], 1)

        def stream(n, u):
            settled().tensor_tensor(flat(X3[u]), xr(n), flat(Hf[u]), ALU.add).then_inc(S["X3_done"], 1)

        def p_parts(n, u):
            settled().tensor_scalar(flat(Zp), flat(Ps[u]), -BETA, ALPHA, ALU.mult, ALU.add).then_inc(S["Z_done"], 1)
            need(pool, S["Dr_done"], n + 1)
            tt(Gd, Dr[u], Ps[u], ALU.subtract).then_inc(S["G_done"], 1)
            need(pool, S["Q_done"], n + 1)
            pool.wait_ge(S["Z_done"], n + 1)
            tt(ys[0], Qs[u], Zp).then_inc(S["y1_done"], 1)

        def q_plus_z(n, s):
            pool.wait_ge(S["q_done"], n * 3 + s + 1)
            tt(yz[s % 2], qs[s], Zp).then_inc(S["yz_done"], 1)

        def first():
            settled().tensor_copy(flat(Ps[0]), flat(condT)).then_inc(S["P_done"], 1)
            with_bias(0, 0)
            low_xs(0)
            low_h(0, condT)
            low_xs(1)
            drive(0, 0)
            low_h(1, Hf[0])

        def step(t):
            n, u = t.n, t.u
            pool.wait_ge(S["P_done"], n + 1)
            p_parts(n, u)
            stream(n, u)
            q_plus_z(n, 0)
            if has(t, 2):
                low_xs(n + 2)
            if has(t, 1):
                with_bias(n + 1, 1 - u)
            q_plus_z(n, 1)
            pool.wait_ge(S["y_done"], n * 3 + 2)
            tt(y23, ys[1], ys[2]).then_inc(S["y23_done"], 1)
            pool.wait_ge(S["q_done"], n * 3 + 3)
            tt(bq, qs[2], Qs[u], ALU.subtract).then_inc(S["bq_done"], 1)
            pool.wait_ge(S["bq_done"], n + 1)
            pool.wait_ge(S["aq_done"], n + 1)
            tt(cq, aq, bq).then_inc(S["cq_done"], 1)
            q_plus_z(n, 2)
            pool.wait_ge(S["y_done"], n * 3 + 3)
            tt(y14, ys[0], ys[3]).then_inc(S["y14_done"], 1)
            if has(t, 1):
                drive(n + 1, 1 - u)
                low_h(n + 2, Hf[1 - u])
            pool.wait_ge(S["Q_done"], n + 2)
            pool.wait_ge(S["X3_done"], n + 1)
            need(pool, S["ot_done"], n - 1)
            tt(ob[u], X3[u], Qs[1 - u]).then_inc(S["ob_done"], 1)
            pool.wait_ge(S["pp_done"], n + 1)
            settled().tensor_scalar(flat(Ps[1 - u]), flat(pp), CLAMP, -CLAMP, ALU.min, ALU.max).then_inc(S["P_done"], 1)

        run(pool, first, step)

    @block.sync
    def _(sp):
        def step(t):
            sp.wait_ge(S["ot_done"], t.n + 1)
            for q in range(4):
                for h in range(2):
                    dst = out[h * 32:(h + 1) * 32, bass.ds(t.n, 1), :].rearrange("b a (c q f) -> b (a c) q f", q=4, f=32)[:, :, q, :]
                    src = ot[t.u][q * 32:(q + 1) * 32, :, :].rearrange("p c (h f) -> p c h f", h=2)[:, :, h, :]
                    sp.dma_start(dst, src).then_inc(out_sent[t.u], 16)

        run(sp, lambda: None, step)
        for s in out_sent:
            sp.wait_ge(s, (T // 2) * 8 * 16)


_INS = ["x", "cond_2048", "L0_cond_W_emb", "L0_cond_b_emb", "L0_cond_g_norm", "L0_cond_W_qkv", "L0_cond_g_q", "L0_cond_g_k",
        "L0_cond_W_out", "L2_cond_W_ih", "L2_cond_W_hh", "L2_cond_b_ih", "L2_cond_b_hh", "L3_cond_coupling", "L3_cond_bias"]


def kernel(**inputs):
    import numpy as np
    import concourse.bacc as bacc
    from concourse.bass_utils import run_bass_kernel_spmd

    nc = bacc.Bacc("TRN2", target_bir_lowering=False, num_devices=1)
    arrays, args = {}, []
    for name in _INS:
        a = np.ascontiguousarray(inputs[name])
        arrays[f"in_{name}"] = a
        args.append(nc.dram_tensor(f"in_{name}", a.shape, mybir.dt.from_np(a.dtype), kind="ExternalInput").ap())
    shape = inputs["x"].shape
    out = nc.dram_tensor("out", shape, F32, kind="ExternalOutput").ap()
    rows = nc.dram_tensor("rows_dram", (shape[0], shape[2]), F16, kind="Internal").ap()
    program(nc, *args, out, rows)
    r = run_bass_kernel_spmd(nc, [arrays], core_ids=[0])
    return r.results[0]["out"]
```

```python
from contextlib import ExitStack

import concourse.bass as bass
from concourse import mybir

ALU = mybir.AluOpType
ACT = mybir.ActivationFunctionType
AX = mybir.AxisListType
F32 = mybir.dt.float32
F16 = mybir.dt.float16
I32 = mybir.dt.int32

WS = 64.0
PART = 128
EPS = 1e-6
HEADS = 16
DT, EPSILON, ALPHA, BETA, CLAMP = 0.01, 0.08, 0.7, 0.8, 20.0


class Pair:

    def __init__(self, n, half, u):
        self.n, self.half, self.u = n, half, u
        self.before = half - 1 if u == 0 else half

    def later(self, d, count):
        n = self.n + d
        return None if isinstance(n, int) and n >= count else n


def need(eng, sem, value):
    if isinstance(value, int) and value <= 0:
        return
    eng.wait_ge(sem, value)


def program(nc, x, cond, W_emb, b_emb, g_norm, W_qkv, g_q, g_k, W_out, W_ih, W_hh, b_ih, b_hh,
            coupling, bias, out, rows_dram):
    B, T, D = x.shape
    KC = D // PART
    G3 = W_ih.shape[1]
    DH = D // HEADS
    NPAIR = B // 2
    TOK = 2 * T
    assert TOK == PART and KC == 4 and B == 64 and T == 64

    with ExitStack() as ctx:
        def sb(name, shape, dt=F32, stack=ctx):
            return stack.enter_context(nc.sbuf_tensor(name, shape, dt))

        def sem(name, stack=ctx):
            return stack.enter_context(nc.semaphore(name))

        XR = sb("XR", [PART, T, KC, B])
        condT = sb("condT", [PART, KC, B])
        ident = sb("ident", [PART, PART])
        with ExitStack() as attn:
            keep = dict(
                Wqkv=sb("Wqkv", [PART, 2, KC, G3], F16, attn), Wo=sb("Wo", [PART, 2, KC, D], F16, attn),
                modA=sb("modA", [PART, KC, B], F32, attn), modB=sb("modB", [PART, KC, B], F32, attn),
                WT=sb("WT", [PART, 2, KC, B], F32, attn), lidx=sb("lidx", [PART, 2, KC], F32, attn),
                gqk=sb("gqk", [PART, 1], F32, attn),
                Vbd=[sb(f"Vbd{u}", [PART, 2, 2, HEADS // 2, 64], F16, attn) for u in range(2)])
            with ExitStack() as s:
                setup(nc, s, XR, condT, ident, keep, cond, W_emb, b_emb, g_norm, W_qkv, g_q, g_k, W_out, rows_dram)
            with ExitStack() as s:
                attention_and_sampling(nc, s, XR, ident, keep, x, rows_dram)
        with ExitStack() as s:
            recurrences(nc, s, XR, condT, ident, W_ih, W_hh, b_ih, b_hh, coupling, bias, out)


def setup(nc, ctx, XR, condT, ident, keep, cond, W_emb, b_emb, g_norm, W_qkv, g_q, g_k, W_out, rows_dram):
    B, D = cond.shape
    KC = D // PART
    G3 = W_qkv.shape[1]
    DH = g_q.shape[0]
    Wqkv, Wo, modA, modB = keep["Wqkv"], keep["Wo"], keep["modA"], keep["modB"]
    WT, lidx, gqk, Vbd = keep["WT"], keep["lidx"], keep["gqk"], keep["Vbd"]

    def sb(name, shape, dt=F32):
        return ctx.enter_context(nc.sbuf_tensor(name, shape, dt))

    def sem(name):
        return ctx.enter_context(nc.semaphore(name))

    room = XR[:, :, :, :].rearrange("p t c b -> p (t c b)")
    wq32 = room[:, 0:KC * G3].rearrange("p (c n) -> p c n", c=KC)
    wo32 = room[:, KC * G3:KC * (G3 + D)].rearrange("p (c n) -> p c n", c=KC)
    we32 = room[:, KC * (G3 + D):KC * (G3 + 3 * D)].rearrange("p (c n) -> p c n", c=KC)
    condtok = sb("condtok", [B, D])
    bemb = sb("bemb", [PART, 2 * KC])
    gnorm = sb("gnorm", [PART, KC])
    gq = sb("gq", [PART, 2])
    ix = sb("ix", [B, D])
    iint = sb("iint", [B, D], I32)
    ir = sb("ir", [B, D])
    igt = sb("igt", [B, D])
    i0 = sb("i0", [B, D])
    i0h = sb("i0h", [B, D], F16)
    w1 = sb("w1", [B, D])
    psC = ctx.enter_context(nc.psum_tensor("psC", [PART, KC, B], F32))
    psW = ctx.enter_context(nc.psum_tensor("psW", [PART, KC, B], F32))
    psE = ctx.enter_context(nc.psum_tensor("psE", [PART, 2 * KC, B], F32))

    cond_in, small_in, wemb_in, wqkv_in, wo_in = (sem(n) for n in ("cond_in", "small_in", "wemb_in", "wqkv_in", "wo_in"))
    rows_out = sem("rows_out")
    consts = sem("consts")
    grid_step = sem("grid_step")
    rows_ready, w1_ready = sem("rows_ready"), sem("w1_ready")
    cond_T, cond_kept, w1_T, emb_done = sem("cond_T"), sem("cond_kept"), sem("w1_T"), sem("emb_done")
    wo_plus, hi_done, mod_step, fold = sem("wo_plus"), sem("hi_done"), sem("mod_step"), sem("fold")
    block = ctx.enter_context(nc.Block())

    @block.sync
    def _(sp):
        sp.dma_start(condtok[:, :], cond).then_inc(cond_in, 16)
        sp.dma_start(we32, W_emb.rearrange("(c p) n -> p c n", p=PART)).then_inc(wemb_in, 16)
        sp.dma_start(wo32, W_out.rearrange("(c p) n -> p c n", p=PART)).then_inc(wo_in, 16)
        sp.dma_start(wq32, W_qkv.rearrange("(c p) n -> p c n", p=PART)).then_inc(wqkv_in, 16)
        sp.wait_ge(rows_ready, 1)
        sp.dma_start(rows_dram, i0h[:, :]).then_inc(rows_out, 16)
        sp.wait_ge(rows_out, 16)

    @block.gpsimd
    def _(pool):
        nc.gpsimd.memset(ident[:, :], 0.0).then_inc(consts, 1)
        pool.wait_ge(consts, 1)
        nc.gpsimd.affine_select(out=ident[:, :], in_=ident[:, :], compare_op=ALU.not_equal, fill=1.0, base=0,
                                pattern=[[-1, PART]], channel_multiplier=1).then_inc(consts, 1)
        nc.gpsimd.iota(lidx[:, :, :], pattern=[[-1, 2], [PART, KC]], base=0, channel_multiplier=1,
                       allow_small_or_imprecise_dtypes=True).then_inc(consts, 1)
        for v in Vbd:
            nc.gpsimd.memset(v[:, :, :, :, :], 0.0).then_inc(consts, 1)

    @block.scalar
    def _(act):
        with nc.allow_non_contiguous_dma("small vectors, laid along the partitions"):
            act.dma_start(bemb[:, :], b_emb.rearrange("(c p) -> p c", p=PART)).then_inc(small_in, 16)
            act.dma_start(gnorm[:, :], g_norm.rearrange("(c p) -> p c", p=PART)).then_inc(small_in, 16)
            for n, g in enumerate((g_q, g_k)):
                for q in range(PART // DH):
                    act.dma_start(gq[q * DH:(q + 1) * DH, n:n + 1], g.rearrange("(p a) -> p a", a=1)).then_inc(small_in, 16)
        act.wait_ge(cond_T, 1)
        nc.scalar.activation(condT[:, :, :], psC[:, :, :], ACT.Copy).then_inc(cond_kept, 1)
        act.wait_ge(wo_plus, 1)
        for c in range(KC):
            nc.scalar.activation(Wo[:, 0, c, :], wo32[:, c, :], ACT.Copy, scale=WS).then_inc(hi_done, 1)
        act.wait_ge(wqkv_in, 16)
        for c in range(KC):
            nc.scalar.activation(Wqkv[:, 0, c, :], wq32[:, c, :], ACT.Copy, scale=WS).then_inc(hi_done, 1)

    @block.vector
    def _(dve):
        v = nc.vector
        dve.wait_ge(cond_in, 16)
        v.tensor_scalar(ix[:, :], condtok[:, :], 1.0, 0.5, ALU.add, ALU.mult).then_inc(grid_step, 1)
        dve.wait_ge(grid_step, 1)
        v.tensor_scalar(ix[:, :], ix[:, :], float(D - 1), 0.0, ALU.mult, ALU.max).then_inc(grid_step, 1)
        dve.wait_ge(grid_step, 2)
        v.tensor_scalar(ix[:, :], ix[:, :], float(D - 1), None, ALU.min).then_inc(grid_step, 1)
        dve.wait_ge(grid_step, 3)
        v.tensor_copy(iint[:, :], ix[:, :]).then_inc(grid_step, 1)
        dve.wait_ge(grid_step, 4)
        v.tensor_copy(ir[:, :], iint[:, :]).then_inc(grid_step, 1)
        dve.wait_ge(grid_step, 5)
        v.tensor_tensor(igt[:, :], ir[:, :], ix[:, :], ALU.is_gt).then_inc(grid_step, 1)
        dve.wait_ge(grid_step, 6)
        v.tensor_tensor(i0[:, :], ir[:, :], igt[:, :], ALU.subtract).then_inc(grid_step, 1)
        dve.wait_ge(grid_step, 7)
        v.tensor_copy(i0h[:, :], i0[:, :]).then_inc(rows_ready, 1)
        v.tensor_tensor(w1[:, :], ix[:, :], i0[:, :], ALU.subtract).then_inc(w1_ready, 1)
        dve.wait_ge(w1_T, 1)
        v.tensor_copy(WT[:, 1, :, :], psW[:, :, :])
        v.tensor_scalar(WT[:, 0, :, :], psW[:, :, :], -1.0, 1.0, ALU.mult, ALU.add)
        dve.wait_ge(consts, 2)
        dve.wait_ge(wo_in, 16)
        for c in range(KC):
            d = wo32[:, c, c * PART:(c + 1) * PART]
            last = v.tensor_tensor(d, d, ident[:, :], ALU.add)
        last.then_inc(wo_plus, 1)
        dve.wait_ge(small_in, 16 * (2 + 2 * (PART // DH)))
        v.tensor_scalar(gqk[:, :], gq[:, 0:1], gq[:, 1:2], float(DH) ** -0.5, ALU.mult, ALU.mult)
        dve.wait_ge(emb_done, 1)
        for c in range(KC):
            v.tensor_scalar(modA[:, c, :], psE[:, c, :], bemb[:, c:c + 1], 1.0, ALU.add, ALU.add).then_inc(mod_step, 1)
            v.tensor_scalar(modB[:, c, :], psE[:, KC + c, :], bemb[:, KC + c:KC + c + 1], None, ALU.add)
        dve.wait_ge(mod_step, KC)
        for c in range(KC):
            v.tensor_scalar(modA[:, c, :], modA[:, c, :], gnorm[:, c:c + 1], None, ALU.mult)
        for n, (pair, w32) in enumerate(((Wo, wo32), (Wqkv, wq32))):
            for c in range(KC):
                dve.wait_ge(hi_done, n * KC + c + 1)
                v.scalar_tensor_tensor(out=pair[:, 1, c, :], in0=w32[:, c, :], scalar=WS, in1=pair[:, 0, c, :],
                                       op0=ALU.mult, op1=ALU.subtract)

    @block.tensor
    def _(pe):
        pe.wait_ge(consts, 2)
        pe.wait_ge(cond_in, 16)
        for c in range(KC):
            last = nc.tensor.transpose(psC[:, c, :], condtok[:, c * PART:(c + 1) * PART], ident[0:B, 0:B])
        last.then_inc(cond_T, 1)
        pe.wait_ge(w1_ready, 1)
        for c in range(KC):
            last = nc.tensor.transpose(psW[:, c, :], w1[:, c * PART:(c + 1) * PART], ident[0:B, 0:B])
        last.then_inc(w1_T, 1)
        pe.wait_ge(cond_kept, 1)
        pe.wait_ge(wemb_in, 16)
        for m in range(2 * KC):
            for c in range(KC):
                last = nc.tensor.matmul(psE[:, m, :], we32[:, c, m * PART:(m + 1) * PART], condT[:, c, :],
                                        start=(c == 0), stop=(c == KC - 1))
        last.then_inc(emb_done, 1)


def attention_and_sampling(nc, ctx, XR, ident, keep, x, rows_dram):
    B, T, D = x.shape
    KC = D // PART
    DH = D // HEADS
    NP = B // 2
    Wqkv, Wo, modA, modB = keep["Wqkv"], keep["Wo"], keep["modA"], keep["modB"]
    WT, lidx, gqk, Vbd = keep["WT"], keep["lidx"], keep["gqk"], keep["Vbd"]

    def sb(name, shape, dt=F32):
        return ctx.enter_context(nc.sbuf_tensor(name, shape, dt))

    def sem(name):
        return ctx.enter_context(nc.semaphore(name))

    xtok = [sb(f"xtok{u}", [PART, D]) for u in range(2)]
    sqx = sb("sqx", [PART, D])
    yt = [sb(f"yt{u}", [PART, D]) for u in range(2)]
    xa = sb("xa", [PART, KC, 2, T])
    xb = sb("xb", [PART, KC, 2, T])
    xn = [sb(f"xn{u}", [PART, 2, KC, PART], F16) for u in range(2)]
    sq = sb("sq", [PART, 2, D])
    QK, X = slice(0, 2 * HEADS), slice(2 * HEADS, 2 * HEADS + 1)
    ss, ms, rs, rt = (sb(n, [PART, 2 * HEADS + 1]) for n in ("ss", "ms", "rs", "rt"))
    qn = sb("qn", [PART, 2, D])
    qkT = sb("qkT", [PART, 2, 2, KC, PART], F16)
    S = sb("S", [PART, HEADS, T])
    mx = sb("mx", [PART, 4, 4])
    den = sb("den", [PART, HEADS])
    rden = sb("rden", [PART, HEADS])
    PT = sb("PT", [PART, 2, HEADS // 2, PART], F16)
    oT = sb("oT", [PART, 2, KC, PART], F16)
    x1 = sb("x1", [PART, 2, KC, 2, T], F16)
    rows = [sb(f"rows{u}", [PART, D], F16) for u in range(2)]
    E = [sb(f"E{u}", [PART, 2, KC, D], F16) for u in range(2)]
    um = [sb(f"um{u}", [PART, 2, KC, T]) for u in range(2)]
    us = [sb(f"us{u}", [PART, KC, T]) for u in range(2)]

    def ps(name, shape):
        return ctx.enter_context(nc.psum_tensor(name, shape, F32))

    psQ = ps("psQ", [PART, 3, D])
    psS = ps("psS", [PART, 4, D])
    psO = ps("psO", [PART, KC, PART])
    psL = [psQ[:, b, :].rearrange("p (v c t) -> p v c t", v=2, c=KC) for b in range(2)]
    psP = psQ[:, 2, :].rearrange("p (c b t) -> p c b t", c=KC, b=2)

    def turned(j):
        return psS[:, j, :].rearrange("p (c n) -> p c n", c=KC)

    x_in = [sem(f"x_in{u}") for u in range(2)]
    rows_in = [sem(f"rows_in{u}") for u in range(2)]
    ssx_done, ms_done, rs_step, y_done = sem("ssx_done"), sem("ms_done"), sem("rs_step"), sem("y_done")
    xy_T, xT_kept, xa_done, xb_done = sem("xy_T"), sem("xT_kept"), sem("xa_done"), sem("xb_done")
    xn_hi, xn_ready = sem("xn_hi"), sem("xn_ready")
    qkv_done, sq_done, ssq_done, qn_done = sem("qkv_done"), sem("sq_done"), sem("ssq_done"), sem("qn_done")
    v_hi, v_ready = sem("v_hi"), sem("v_ready")
    qk_T, qk_hi, qk_ready = sem("qk_T"), sem("qk_hi"), sem("qk_ready")
    sc_done, mx_done, sub_done, exp_done = sem("sc_done"), sem("mx_done"), sem("sub_done"), sem("exp_done")
    den_done, rden_done, p_done = sem("den_done"), sem("rden_done"), sem("p_done")
    p_T, pt_hi, pt_ready = sem("p_T"), sem("pt_hi"), sem("pt_ready")
    mix_done, o_hi, o_ready = sem("mix_done"), sem("o_hi"), sem("o_ready")
    proj_done, x1_done, x1_hi, x1_ready = sem("proj_done"), sem("x1_done"), sem("x1_hi"), sem("x1_ready")
    e_built, samp_done, um_done, us_done, x2_done = (sem(n) for n in ("e_built", "samp_done", "um_done", "us_done", "x2_done"))
    passed = sem("passed")
    block = ctx.enter_context(nc.Block())

    FIRST, LAST = -2, NP + 3
    LOOP0, NLOOP = 4, (NP - 3 - 4) // 2

    def run(eng, slot):
        def at(i):
            def pair(d):
                n = i + d
                return Pair(n, n // 2, n % 2) if 0 <= n < NP else None
            return pair
        for i in range(FIRST, LOOP0):
            slot(at(i))
        with eng.Fori(0, NLOOP) as it:
            for j in range(2):
                def pair(d, j=j):
                    c = LOOP0 + j + d
                    return Pair(it * 2 + c, it + c // 2, c % 2)
                slot(pair)
        for i in range(LOOP0 + 2 * NLOOP, LAST):
            slot(at(i))

    @block.sync
    def _(sp):
        def load_x(p):
            need(sp, xy_T, p.n - 1)
            sp.dma_start(xtok[p.u][:, :], x_rows(p)).then_inc(x_in[p.u], 16)

        def x_rows(p):
            return x[bass.ds(p.n * 2, 2), :, :].rearrange("b t d -> (b t) d")

        def load_rows(p):
            for b in range(2):
                need(sp, e_built, p.n * 2 + b - 1)
                sp.dma_start(rows[b][:, :], rows_dram[bass.ds(p.n * 2 + b, 1), :].rearrange("a n -> (a n)")
                             .partition_broadcast(PART)).then_inc(rows_in[b], 16)

        def slot(pair):
            if p := pair(2):
                load_x(p)
            if p := pair(-2):
                load_rows(p)

        run(sp, slot)

    @block.gpsimd
    def _(pool):
        def settled():
            pool.sem_inc(passed, 1)
            return nc.gpsimd

        def add_taps(p, b):
            pool.wait_ge(um_done, p.n * 2 + b + 1)
            need(pool, x2_done, p.n * 2 + b - 1)
            settled().tensor_tensor(us[b][:, :, :], um[b][:, 0, :, :], um[b][:, 1, :, :], ALU.add).then_inc(us_done, 1)
            pool.wait_ge(us_done, p.n * 2 + b + 1)
            r = XR[:, :, :, bass.ds(p.n * 2 + b, 1)].rearrange("p t c a -> p c (t a)")
            settled().tensor_tensor(r, r, us[b][:, :, :], ALU.add).then_inc(x2_done, 1)

        def norm_p(p):
            pool.wait_ge(rden_done, p.n + 1)
            settled().tensor_tensor(S[:, :, :], S[:, :, :], rden[:, :].unsqueeze(2).broadcast_to([PART, HEADS, T]), ALU.mult)\
                .then_inc(p_done, 1)

        def low_x1(p):
            pool.wait_ge(x1_hi, p.n * 2 + 2)
            need(pool, samp_done, p.n * 2)
            for b in range(2):
                last = settled().tensor_tensor(x1[:, 1, :, b, :], XR[:, :, :, bass.ds(p.n * 2 + b, 1)].rearrange("p t c a -> p c (t a)"),
                                       x1[:, 0, :, b, :], ALU.subtract)
            last.then_inc(x1_ready, 1)

        def shift_x(p):
            pool.wait_ge(xa_done, p.n + 1)
            need(pool, xn_hi, p.n)
            need(pool, xn_ready, p.n)
            settled().tensor_tensor(xb[:, :, :, :], xa[:, :, :, :],
                            modB[:, :, bass.ds(p.n * 2, 2)].unsqueeze(3).broadcast_to([PART, KC, 2, T]), ALU.add)\
                .then_inc(xb_done, 1)

        def low_x(p):
            pool.wait_ge(xn_hi, p.n + 1)
            settled().tensor_tensor(xn[p.u][:, 1, :, :], xb[:, :, :, :].rearrange("p c b t -> p c (b t)"), xn[p.u][:, 0, :, :],
                            ALU.subtract).then_inc(xn_ready, 1)

        def slot(pair):
            if p := pair(1):
                low_x(p)
            if p := pair(-3):
                add_taps(p, 0)
            if p := pair(-1):
                norm_p(p)
            if p := pair(-3):
                add_taps(p, 1)
            if p := pair(-2):
                low_x1(p)
            if p := pair(2):
                shift_x(p)

        run(pool, slot)

    @block.scalar
    def _(act):
        def a(out, in_, f=ACT.Copy, **k):
            return nc.scalar.activation(out, in_, f, **k)

        def squares_x(p):
            act.wait_ge(x_in[p.u], p.half * 16 + 16)
            need(act, ms_done, p.n)
            a(sqx[:, :], xtok[p.u][:, :], ACT.Square, accum_out=ss[:, X]).then_inc(ssx_done, 1)

        def high_qk(p):
            act.wait_ge(qk_T, p.n + 1)
            need(act, sc_done, p.n)
            a(qkT[:, 0, 0, :, :], turned(0), scale=gqk[:, 0:1]).then_inc(qk_hi, 1)
            a(qkT[:, 0, 1, :, :], turned(1)).then_inc(qk_hi, 1)

        def squares_qk(p, n):
            act.wait_ge(qkv_done, p.n * 3 + n + 1)
            need(act, ssq_done, p.n * 2 + n - 1)
            a(sq[:, n, :], psQ[:, n, :], ACT.Square).then_inc(sq_done, 1)

        def high_v(p):
            act.wait_ge(qkv_done, p.n * 3 + 3)
            need(act, mix_done, p.n - 1)
            for b in range(2):
                for r in range(2):
                    src = psQ[b * T:(b + 1) * T, 2, :].rearrange("p (j r d) -> p j r d", r=2, d=DH)[:, :, r, :]
                    a(Vbd[p.u][r * T:(r + 1) * T, b, 0, :, r * DH:(r + 1) * DH], src).then_inc(v_hi, 1)

        def high_p(p):
            act.wait_ge(p_T, p.n + 1)
            need(act, mix_done, p.n)
            for h in range(2):
                a(PT[:, 0, 4 * h:4 * h + 4, :].rearrange("p (r j) n -> p r (j n)", r=2), psS[:, 2 * h:2 * h + 2, 256:512])\
                    .then_inc(pt_hi, 1)

        def exps(p):
            act.wait_ge(sub_done, p.n + 1)
            a(S[:, :, :], S[:, :, :], ACT.Exp).then_inc(exp_done, 1)

        def high_o(p):
            act.wait_ge(mix_done, p.n + 1)
            need(act, proj_done, p.n)
            a(oT[:, 0, :, :], psO[:, :, :]).then_inc(o_hi, 1)

        def high_x1(p):
            act.wait_ge(x1_done, p.n * 2 + 2)
            need(act, samp_done, p.n * 2)
            for b in range(2):
                a(x1[:, 0, :, b, :], XR[:, :, :, bass.ds(p.n * 2 + b, 1)].rearrange("p t c a -> p c (t a)")).then_inc(x1_hi, 1)

        def keep_xT(p):
            act.wait_ge(xy_T, p.n + 1)
            for b in range(2):
                last = a(XR[:, :, :, bass.ds(p.n * 2 + b, 1)].rearrange("p t c a -> p c (t a)"),
                         psS[:, 2, :].rearrange("p (c b t) -> p c b t", c=KC, b=2)[:, :, b, :])
            last.then_inc(xT_kept, 1)

        def high_x(p):
            act.wait_ge(xb_done, p.n + 1)
            need(act, qkv_done, (p.n - 1) * 3)
            a(xn[p.u][:, 0, :, :], xb[:, :, :, :].rearrange("p c b t -> p c (b t)")).then_inc(xn_hi, 1)

        def slot(pair):
            if p := pair(0):
                squares_qk(p, 0)
            if p := pair(-2):
                high_p(p)
            if p := pair(2):
                squares_x(p)
            if p := pair(0):
                squares_qk(p, 1)
            if p := pair(-1):
                high_qk(p)
            if p := pair(1):
                high_x(p)
            if p := pair(-2):
                high_o(p)
            if p := pair(0):
                high_v(p)
            if p := pair(-1):
                exps(p)
            if p := pair(2):
                keep_xT(p)
            if p := pair(-2):
                high_x1(p)

        run(act, slot)

    @block.vector
    def _(dve):
        v = nc.vector

        STEPS = 11
        LOWS = (4, 6)
        EARLY = 4

        def low_qk(p, n):
            dve.wait_ge(qk_hi, p.n * 2 + n + 1)
            need(dve, sc_done, p.n)
            if n == 0:
                v.scalar_tensor_tensor(out=qkT[:, 1, 0, :, :], in0=turned(0), scalar=gqk[:, 0:1],
                                       in1=qkT[:, 0, 0, :, :], op0=ALU.mult, op1=ALU.subtract)
            else:
                v.tensor_tensor(qkT[:, 1, 1, :, :], turned(1), qkT[:, 0, 1, :, :], ALU.subtract).then_inc(qk_ready, 1)

        def scale_x(p):
            dve.wait_ge(rs_step, p.n * STEPS + STEPS)
            dve.wait_ge(x_in[p.u], p.half * 16 + 16)
            need(dve, xy_T, p.n - 1)
            v.tensor_scalar(yt[p.u][:, :], xtok[p.u][:, :], rs[:, X], None, ALU.mult).then_inc(y_done, 1)

        def build_tap(p, b, k):
            if k == 0:
                dve.wait_ge(rows_in[b], p.n * 16 + 16)
                need(dve, samp_done, p.n * 2 + b - 1)
            t, c = k // KC, k % KC
            e = v.tensor_scalar(E[b][:, t, c, :], rows[b][:, :], lidx[:, t, c:c + 1], None, ALU.is_equal)
            if k == 2 * KC - 1:
                e.then_inc(e_built, 1)

        def means(n, qk, x):
            if x:
                dve.wait_ge(ssx_done, x.n + 1)
                last = v.tensor_scalar(ms[:, X], ss[:, X], 1.0 / D, EPS, ALU.mult, ALU.add)
            if qk:
                dve.wait_ge(ssq_done, qk.n * 2 + 2)
                last = v.tensor_scalar(ms[:, QK], ss[:, QK], 1.0 / DH, EPS * WS * WS, ALU.mult, ALU.add)
            last.then_inc(ms_done, 1)

        def rsqrt_step(n, cols, k):
            m, r, t = ms[:, cols], rs[:, cols], rt[:, cols]
            if k == 0:
                dve.wait_ge(ms_done, n + 1)
                o = v.tensor_scalar(t.bitcast(I32), m.bitcast(I32), 1, None, ALU.logical_shift_right)
            else:
                dve.wait_ge(rs_step, n * STEPS + k)
                if k == 1:
                    o = v.tensor_scalar(r.bitcast(I32), t.bitcast(I32), -1, 0x5F3759DF, ALU.mult, ALU.add)
                elif k % 3 == 2:
                    o = v.tensor_tensor(t, r, r, ALU.mult)
                elif k % 3 == 0:
                    o = v.scalar_tensor_tensor(out=t, in0=t, scalar=-0.5, in1=m, op0=ALU.mult, op1=ALU.mult)
                else:
                    o = v.scalar_tensor_tensor(out=r, in0=t, scalar=1.5, in1=r, op0=ALU.add, op1=ALU.mult)
            o.then_inc(rs_step, 1)

        def sums_qk(p, n):
            dve.wait_ge(sq_done, p.n * 2 + n + 1)
            v.tensor_reduce(ss[:, n * HEADS:(n + 1) * HEADS], sq[:, n, :].rearrange("p (h d) -> p h d", d=DH), AX.X, ALU.add)\
                .then_inc(ssq_done, 1)

        def scale_qk(p):
            dve.wait_ge(rs_step, p.n * STEPS + 3 * STEPS)
            need(dve, qk_T, p.n)
            for n in range(2):
                v.tensor_tensor(qn[:, n, :].rearrange("p (h d) -> p h d", d=DH), psQ[:, n, :].rearrange("p (h d) -> p h d", d=DH),
                                rs[:, n * HEADS:(n + 1) * HEADS].unsqueeze(2).broadcast_to([PART, HEADS, DH]), ALU.mult)\
                    .then_inc(qn_done, 1)

        def low_v(p):
            for b in range(2):
                for r in range(2):
                    dve.wait_ge(v_hi, p.n * 4 + 2 * b + 2)
                    src = psQ[b * T:(b + 1) * T, 2, :].rearrange("p (j r d) -> p j r d", r=2, d=DH)[:, :, r, :]
                    dst = Vbd[p.u][r * T:(r + 1) * T, b, :, :, r * DH:(r + 1) * DH]
                    last = v.tensor_tensor(dst[:, 1, :, :], src, dst[:, 0, :, :], ALU.subtract)
            last.then_inc(v_ready, 1)

        def low_p(p):
            for h in range(2):
                dve.wait_ge(pt_hi, p.n * 2 + h + 1)
                hi, lo = (PT[:, i, 4 * h:4 * h + 4, :].rearrange("p (r j) n -> p r (j n)", r=2) for i in range(2))
                last = v.tensor_tensor(lo, psS[:, 2 * h:2 * h + 2, 256:512], hi, ALU.subtract)
            last.then_inc(pt_ready, 1)

        def subtract_max(p):
            sc = psS[:, :, 0:256].rearrange("p r (c k) -> p r c k", c=4)
            dve.wait_ge(sc_done, p.n + 1)
            v.tensor_reduce(mx[:, :, :], sc, AX.X, ALU.max).then_inc(mx_done, 1)
            dve.wait_ge(mx_done, p.n + 1)
            need(dve, p_T, p.n)
            v.tensor_tensor(S[:, :, :].rearrange("p (c r) k -> p r c k", r=4), sc,
                            mx[:, :, :].unsqueeze(3).broadcast_to([PART, 4, 4, T]), ALU.subtract).then_inc(sub_done, 1)

        def weigh_taps(p, b):
            dve.wait_ge(samp_done, p.n * 2 + b + 1)
            need(dve, us_done, p.n * 2 + b - 1)
            v.tensor_tensor(um[b][:, :, :, :].rearrange("p v c t -> p (v c) t"),
                            psL[b].rearrange("p v c t -> p (v c) t"),
                            WT[:, :, :, bass.ds(p.n * 2 + b, 1)].rearrange("p v c a -> p (v c) a").broadcast_to([PART, 2 * KC, T]),
                            ALU.mult).then_inc(um_done, 1)

        def sum_p(p):
            dve.wait_ge(exp_done, p.n + 1)
            v.tensor_reduce(den[:, :], S[:, :, :], AX.X, ALU.add).then_inc(den_done, 1)
            dve.wait_ge(den_done, p.n + 1)
            need(dve, p_done, p.n)
            v.reciprocal(rden[:, :], den[:, :]).then_inc(rden_done, 1)

        def low_o(p):
            dve.wait_ge(o_hi, p.n + 1)
            v.tensor_tensor(oT[:, 1, :, :], psO[:, :, :], oT[:, 0, :, :], ALU.subtract).then_inc(o_ready, 1)

        def residual(p):
            dve.wait_ge(proj_done, p.n + 1)
            dve.wait_ge(xT_kept, p.n + 1)
            for b in range(2):
                r = XR[:, :, :, bass.ds(p.n * 2 + b, 1)].rearrange("p t c a -> p c (t a)")
                v.scalar_tensor_tensor(out=r, in0=psP[:, :, b, :], scalar=1.0 / (WS * WS), in1=r,
                                       op0=ALU.mult, op1=ALU.add).then_inc(x1_done, 1)

        def modulate(p):
            dve.wait_ge(xy_T, p.n + 1)
            need(dve, xb_done, p.n)
            v.tensor_tensor(xa[:, :, :, :], psS[:, 3, :].rearrange("p (c b t) -> p c b t", c=KC, b=2),
                            modA[:, :, bass.ds(p.n * 2, 2)].unsqueeze(3).broadcast_to([PART, KC, 2, T]), ALU.mult)\
                .then_inc(xa_done, 1)

        def slot(pair):
            x, qk, tap = pair(2), pair(0), pair(-3)
            n = x.n if x else qk.n + 2 if qk else None
            cols = slice(QK.start if qk else X.start, X.stop if x else QK.stop)
            for k in range(EARLY):
                if tap:
                    build_tap(tap, 1, k)
            if qk:
                sums_qk(qk, 0)
            if p := pair(-2):
                low_p(p)
            if qk:
                sums_qk(qk, 1)
            if x or qk:
                means(n, qk, x)
            for k in range(STEPS):
                if tap and k + EARLY < 2 * KC:
                    build_tap(tap, 1, k + EARLY)
                if x or qk:
                    rsqrt_step(n, cols, k)
                if (p := pair(-1)) and k in LOWS:
                    low_qk(p, LOWS.index(k))
            if qk:
                scale_qk(qk)
            if x:
                scale_x(x)
            if p := pair(-2):
                low_o(p)
            if qk:
                low_v(qk)
            if p := pair(-1):
                subtract_max(p)
            if tap:
                weigh_taps(tap, 0)
            if p := pair(-1):
                sum_p(p)
            if tap:
                weigh_taps(tap, 1)
            if p := pair(-2):
                for k in range(2 * KC):
                    build_tap(p, 0, k)
            if x:
                modulate(x)
            if p := pair(-2):
                residual(p)

        run(dve, slot)

    @block.tensor
    def _(pe):
        mm = nc.tensor.matmul
        TERMS = ((0, 0), (0, 1), (1, 0))

        def turn_qk(p):
            pe.wait_ge(qn_done, p.n * 2 + 2)
            need(pe, sub_done, p.n)
            need(pe, pt_ready, p.n)
            need(pe, qk_ready, p.n)
            for n in range(2):
                for c in range(KC):
                    last = nc.tensor.transpose(turned(n)[:, c, :], qn[:, n, c * PART:(c + 1) * PART], ident[:, :])
            last.then_inc(qk_T, 1)

        def project(p, n):
            if n == 0:
                pe.wait_ge(xn_ready, p.n + 1)
            if n == 0:
                need(pe, qn_done, p.n * 2 - 1)
                need(pe, um_done, p.n * 2 - 7)
            elif n == 1:
                need(pe, qn_done, p.n * 2)
                need(pe, um_done, p.n * 2 - 6)
            else:
                need(pe, v_ready, p.n)
                need(pe, x1_done, p.n * 2 - 4)
            for c in range(KC):
                for t, (i, j) in enumerate(TERMS):
                    last = mm(psQ[:, n, :], xn[p.u][:, i, c, :], Wqkv[:, j, c, n * D:(n + 1) * D],
                              start=(c == 0 and t == 0), stop=(c == KC - 1 and t == 2))
            last.then_inc(qkv_done, 1)

        def turn_p(p):
            pe.wait_ge(p_done, p.n + 1)
            need(pe, pt_ready, p.n)
            late = p.later(3, NP)
            if late is not None:
                need(pe, xT_kept, late + 1)
                need(pe, xa_done, late + 1)
            for j in range(HEADS // 2):
                o = psS[:, j // 2, 256 + (j % 2) * PART:256 + (j % 2 + 1) * PART]
                last = nc.tensor.transpose(o, S[:, 2 * j:2 * j + 2, :].rearrange("p h k -> p (h k)"), ident[:, :])
            last.then_inc(p_T, 1)

        def scores(p):
            pe.wait_ge(qk_ready, p.n + 1)
            late = p.later(2, NP)
            if late is not None:
                need(pe, xT_kept, late + 1)
                need(pe, xa_done, late + 1)
            need(pe, sub_done, p.n)
            need(pe, pt_ready, p.n)
            for c in range(4):
                for b in range(2):
                    for t, (i, j) in enumerate(TERMS):
                        for r in range(4):
                            rows_ = slice(r * DH, (r + 1) * DH)
                            last = mm(psS[b * T:(b + 1) * T, r, c * T:(c + 1) * T],
                                      qkT[rows_, i, 0, c, b * T:(b + 1) * T], qkT[rows_, j, 1, c, b * T:(b + 1) * T],
                                      start=(t == 0), stop=(t == 2))
            last.then_inc(sc_done, 1)

        def sample(p, b):
            pe.wait_ge(e_built, p.n * 2 + b + 1)
            pe.wait_ge(x1_ready, p.n + 1)
            late = p.later(3, NP)
            if late is not None:
                need(pe, qn_done, late * 2 + b + 1)
            need(pe, um_done, p.n * 2 + b - 1)
            o = psL[b]
            for t in range(2):
                for m in range(KC):
                    for c in range(KC):
                        for i in range(2):
                            last = mm(o[:, t, m, :], E[b][:, t, c, m * PART:(m + 1) * PART], x1[:, i, c, b, :],
                                      start=(c == 0 and i == 0), stop=(c == KC - 1 and i == 1))
            last.then_inc(samp_done, 1)

        def mix(p):
            pe.wait_ge(pt_ready, p.n + 1)
            pe.wait_ge(v_ready, p.n + 1)
            need(pe, o_ready, p.n)
            for j in range(HEADS // 2):
                for b in range(2):
                    for t, (i, k) in enumerate(TERMS):
                        last = mm(psO[(j % 2) * 64:(j % 2 + 1) * 64, j // 2, b * T:(b + 1) * T],
                                  Vbd[p.u][:, b, i, j, :], PT[:, k, j, b * T:(b + 1) * T], start=(t == 0), stop=(t == 2))
            last.then_inc(mix_done, 1)

        def proj(p):
            pe.wait_ge(o_ready, p.n + 1)
            late = p.later(2, NP)
            if late is not None:
                need(pe, v_ready, late + 1)
            need(pe, x1_done, p.n * 2)
            for m in range(KC):
                for c in range(KC):
                    for t, (i, j) in enumerate(TERMS):
                        last = mm(psP[:, m, :, :].rearrange("p b t -> p (b t)"), Wo[:, i, c, m * PART:(m + 1) * PART], oT[:, j, c, :],
                                  start=(c == 0 and t == 0), stop=(c == KC - 1 and t == 2))
            last.then_inc(proj_done, 1)

        def turn_x(p):
            pe.wait_ge(y_done, p.n + 1)
            pe.wait_ge(x_in[p.u], p.half * 16 + 16)
            need(pe, sub_done, p.n - 2)
            need(pe, pt_ready, p.n - 3)
            need(pe, xT_kept, p.n)
            need(pe, xa_done, p.n)
            for n, src in ((2, xtok[p.u]), (3, yt[p.u])):
                for c in range(KC):
                    last = nc.tensor.transpose(turned(n)[:, c, :], src[:, c * PART:(c + 1) * PART], ident[:, :])
            last.then_inc(xy_T, 1)

        def slot(pair):
            if p := pair(0):
                project(p, 0)
            if p := pair(-2):
                turn_p(p)
            if p := pair(0):
                project(p, 1)
            if p := pair(-1):
                turn_qk(p)
            if p := pair(-2):
                mix(p)
            if p := pair(0):
                project(p, 2)
            if p := pair(-1):
                scores(p)
            if p := pair(-3):
                sample(p, 0)
                sample(p, 1)
            if p := pair(-2):
                proj(p)
            if p := pair(2):
                turn_x(p)

        run(pe, slot)


def recurrences(nc, ctx, XR, condT, ident, W_ih, W_hh, b_ih, b_hh, coupling, bias, out):
    B, T, D = out.shape
    KC = D // PART
    G3 = W_ih.shape[1]
    GC = G3 // PART
    H2, H1 = DT, DT / 2
    K1, K2 = H1 * EPSILON, H2 * EPSILON

    def sb(name, shape, dt=F32, stack=ctx):
        return stack.enter_context(nc.sbuf_tensor(name, shape, dt))

    def sem(name, stack=ctx):
        return stack.enter_context(nc.semaphore(name))

    Wih = sb("Wih", [PART, 2, KC, G3], F16)
    Whh = sb("Whh", [PART, 2, KC, G3], F16)
    Cp = sb("Cp", [PART, 2, KC, D], F16)
    brow = sb("brow", [PART, G3 + D], F16)
    ones = sb("ones", [PART, B], F16)
    biasT = sb("biasT", [PART, KC])
    alphas = sb("alphas", [PART, 1])

    with ExitStack() as s:
        wih32 = sb("wih32", [PART, KC, G3], F32, s)
        whh32 = sb("whh32", [PART, KC, G3], F32, s)
        cp32 = sb("cp32", [PART, KC, D], F32, s)
        brow32 = sb("brow32", [1, G3 + D], F32, s)
        bhh32 = sb("bhh32", [1, G3], F32, s)
        brow_lo = sb("brow_lo", [1, G3 + D], F16, s)
        psC = [s.enter_context(nc.psum_tensor(f"psC{c}", [PART, D], F32)) for c in range(KC)]
        w_in = [sem(f"w_in{n}", s) for n in range(3)]
        bias_in, zeros, sum_done, cT_done, hi_done, brow_done = (
            sem(n, s) for n in ("bias_in", "zeros", "sum_done", "cT_done", "hi_done2", "brow_done"))
        block = s.enter_context(nc.Block())

        @block.sync
        def _(sp):
            sp.dma_start(cp32[:, :, :], coupling.rearrange("(c p) n -> p c n", p=PART)).then_inc(w_in[0], 16)
            sp.dma_start(wih32[:, :, :], W_ih.rearrange("(c p) n -> p c n", p=PART)).then_inc(w_in[1], 16)
            sp.dma_start(whh32[:, :, :], W_hh.rearrange("(c p) n -> p c n", p=PART)).then_inc(w_in[2], 16)

        @block.gpsimd
        def _(pool):
            nc.gpsimd.memset(brow[:, :], 0.0).then_inc(zeros, 1)
            nc.gpsimd.memset(ones[:, :], 1.0)
            nc.gpsimd.memset(alphas[:, :], ALPHA)

        @block.scalar
        def _(act):
            act.dma_start(brow32[:, 0:G3], b_ih.rearrange("(a n) -> a n", a=1)).then_inc(bias_in, 16)
            act.dma_start(bhh32[:, :], b_hh.rearrange("(a n) -> a n", a=1)).then_inc(bias_in, 16)
            act.dma_start(brow32[:, G3:G3 + D], b_hh[2 * D:3 * D].rearrange("(a n) -> a n", a=1)).then_inc(bias_in, 16)
            with nc.allow_non_contiguous_dma("a small vector, laid along the partitions"):
                act.dma_start(biasT[:, :], bias.rearrange("(c p) -> p c", p=PART)).then_inc(bias_in, 16)
            act.wait_ge(sum_done, 1)
            act.wait_ge(zeros, 1)
            nc.scalar.activation(brow[0:1, :], brow32[:, :], ACT.Copy, scale=WS).then_inc(brow_done, 1)
            for c in range(KC):
                act.wait_ge(cT_done, c + 1)
                nc.scalar.activation(Cp[:, 0, c, :], psC[c][:, :], ACT.Copy, scale=WS).then_inc(hi_done, 1)
            for n, (w, w32) in enumerate(((Wih, wih32), (Whh, whh32))):
                act.wait_ge(w_in[n + 1], 16)
                for c in range(KC):
                    nc.scalar.activation(w[:, 0, c, :], w32[:, c, :], ACT.Copy, scale=WS).then_inc(hi_done, 1)

        @block.vector
        def _(dve):
            v = nc.vector
            dve.wait_ge(bias_in, 64)
            v.tensor_tensor(brow32[:, 0:2 * D], brow32[:, 0:2 * D], bhh32[:, 0:2 * D], ALU.add).then_inc(sum_done, 1)
            dve.wait_ge(brow_done, 1)
            v.scalar_tensor_tensor(out=brow_lo[:, :], in0=brow32[:, :], scalar=WS, in1=brow[0:1, :],
                                   op0=ALU.mult, op1=ALU.subtract).then_inc(brow_done, 1)
            dve.wait_ge(brow_done, 2)
            v.tensor_copy(brow[32:33, :], brow_lo[:, :])
            for c in range(KC):
                dve.wait_ge(hi_done, c + 1)
                v.scalar_tensor_tensor(out=Cp[:, 1, c, :], in0=psC[c][:, :], scalar=WS, in1=Cp[:, 0, c, :],
                                       op0=ALU.mult, op1=ALU.subtract)
            for n, (w, w32) in enumerate(((Wih, wih32), (Whh, whh32))):
                for c in range(KC):
                    dve.wait_ge(hi_done, (n + 1) * KC + c + 1)
                    v.scalar_tensor_tensor(out=w[:, 1, c, :], in0=w32[:, c, :], scalar=WS, in1=w[:, 0, c, :],
                                           op0=ALU.mult, op1=ALU.subtract)

        @block.tensor
        def _(pe):
            pe.wait_ge(w_in[0], 16)
            for c in range(KC):
                for n in range(KC):
                    last = nc.tensor.transpose(psC[c][:, n * PART:(n + 1) * PART], cp32[:, n, c * PART:(c + 1) * PART], ident[:, :])
                last.then_inc(cT_done, 1)

    def two(name, shape, dt=F32):
        return [sb(f"{name}{u}", shape, dt) for u in range(2)]

    F = [PART, KC, B]
    xs = sb("xs", [PART, 2, KC, B], F16)
    hs = sb("hs", [PART, 2, KC, B], F16)
    Hf = two("Hf", F)
    rz = sb("rz", [PART, 3, KC, B])
    an, bn, nn, dn, en = (sb(n, F) for n in ("an", "bn", "nn", "dn", "en"))
    xbias, X3, Dr = two("xbias", F), two("X3", F), two("Dr", F)
    Qs, Ps = two("Qs", F), two("Ps", F)
    qs = [sb(f"qs{s}", F) for s in range(3)]
    th = sb("th", F)
    ts_ = sb("ts", [PART, 2, KC, B], F16)
    sqs, ws, rs = two("sqs", F), two("ws", F), two("rs", F)
    Zp, Gd, Gs, Ea, Eb = (sb(n, F) for n in ("Zp", "Gd", "Gs", "Ea", "Eb"))
    yz = two("yz", F)
    ys = [sb(f"ys{s}", F) for s in range(4)]
    e2, e3, gs, aq, cq, hq, hr, qp = (sb(n, F) for n in ("e2", "e3", "gs", "aq", "cq", "hq", "hr", "qp"))
    y23, y14, sy, pp = (sb(n, F) for n in ("y23", "y14", "sy", "pp"))
    ob, ot = two("ob", F), two("ot", F)

    psRZ = [ctx.enter_context(nc.psum_tensor(f"psRZ{u}", [PART, 2, KC, B], F32)) for u in range(2)]
    psN = [ctx.enter_context(nc.psum_tensor(f"psN{u}", [PART, 2, KC, B], F32)) for u in range(2)]
    psF = ctx.enter_context(nc.psum_tensor("psF", [PART, 2, KC, B], F32))

    names = ("xs_hi xs_ready xs_used gi_done rz_done gn_done sig_done an_done bn_done nn_done nz_done zh_done rz_sig h_done hs_hi hs_ready "
             "xbias_done X3_done Dr_done Z_done y1_done G_done Gs_done E_done th_done ts_hi ts_ready sq_done w_done r_done f_done "
             "q_done yz_done y_done e_done gs_done aq_done cq_done hq_done qp_done Q_done y23_done y14_done sy_done "
             "pp_done P_done ob_done ot_done passed act_passed")
    S = {n: sem("s_" + n) for n in names.split()}
    out_sent = [sem(f"out_sent{u}") for u in range(2)]
    block = ctx.enter_context(nc.Block())
    PEEL = 2

    def run(eng, first, step):
        first()
        for t in range(PEEL):
            step(Pair(t, t // 2, t % 2))
        with eng.Fori(0, (T - 2 * PEEL) // 2) as it:
            for u in range(2):
                step(Pair(it * 2 + PEEL + u, it + PEEL // 2, u))
        for t in range(T - PEEL, T):
            step(Pair(t, t // 2, t % 2))

    def has(t, d):
        return not isinstance(t.n, int) or t.n + d < T

    def xr(n):
        return XR[:, bass.ds(n, 1), :, :].rearrange("p a c b -> p (a c b)")

    def flat(ap):
        return ap.rearrange("p c b -> p (c b)")

    @block.tensor
    def _(pe):
        mm = nc.tensor.matmul
        TERMS = ((0, 0), (0, 1), (1, 0))

        def bias_products(u):
            for g in range(8):
                mm(psRZ[u][:, g // KC, g % KC, :], brow[:, g * PART:(g + 1) * PART], ones[:, :], start=(g == 0), stop=False,
                   skip_group_check=True)
            for g in range(8):
                o = G3 + g * PART if g < KC else 2 * D + (g - KC) * PART
                mm(psN[u][:, g // KC, g % KC, :], brow[:, o:o + PART], ones[:, :], start=(g == 0), stop=False,
                   skip_group_check=True)

        def gate_products(u, W, src, part, gates):
            for g in gates:
                o = psRZ[u][:, g // KC, g % KC, :] if g < 2 * KC else psN[u][:, part, g - 2 * KC, :]
                for c in range(KC):
                    for i, j in TERMS:
                        last = mm(o, W[:, i, c, g * PART:(g + 1) * PART], src[:, j, c, :], start=False,
                                  stop=(part == 0 and c == KC - 1 and (i, j) == TERMS[-1]), skip_group_check=True)
            return last

        def gi(n, u, half):
            if half == 0:
                need(pe, S["sig_done"], n - 1)
                need(pe, S["bn_done"], n - 1)
                pe.wait_ge(S["xs_ready"], n + 1)
                bias_products(u)
                gate_products(u, Wih, xs, 1, range(0, GC // 2))
            else:
                gate_products(u, Wih, xs, 1, range(GC // 2, GC)).then_inc(S["gi_done"], 1)

        def gh(n, u, half):
            if half == 0:
                pe.wait_ge(S["hs_ready"], n + 1)
                gate_products(u, Whh, hs, 0, range(0, GC // 2))
            else:
                gate_products(u, Whh, hs, 0, range(GC // 2, 2 * KC)).then_inc(S["rz_done"], 1)
                gate_products(u, Whh, hs, 0, range(2 * KC, GC)).then_inc(S["gn_done"], 1)

        def stage(t, s):
            pe.wait_ge(S["ts_hi"], t.n * 4 + s + 1)
            for c in range(KC):
                for m in range(KC):
                    for i in range(2):
                        mm(psF[:, s % 2, m, :], Cp[:, i, c, m * PART:(m + 1) * PART], ts_[:, 0, c, :],
                           start=(c == 0 and m == 0 and i == 0), stop=False, skip_group_check=True)
            pe.wait_ge(S["ts_ready"], t.n * 4 + s + 1)
            for c in range(KC):
                for m in range(KC):
                    last = mm(psF[:, s % 2, m, :], Cp[:, 0, c, m * PART:(m + 1) * PART], ts_[:, 1, c, :],
                              start=False, stop=(c == KC - 1), skip_group_check=True)
            last.then_inc(S["f_done"], 1)

        def first():
            gi(0, 0, 0)
            gi(0, 0, 1)
            gh(0, 0, 0)
            gh(0, 0, 1)
            gi(1, 1, 0)
            gi(1, 1, 1)

        def step(t):
            stage(t, 0)
            if has(t, 1):
                gh(t.n + 1, 1 - t.u, 0)
            stage(t, 1)
            if has(t, 1):
                gh(t.n + 1, 1 - t.u, 1)
            stage(t, 2)
            if has(t, 2):
                gi(t.n + 2, t.u, 0)
            stage(t, 3)
            if has(t, 2):
                gi(t.n + 2, t.u, 1)

        run(pe, first, step)

    @block.scalar
    def _(act):
        def a(out, in_, f=ACT.Copy, **k):
            return nc.scalar.activation(out, in_, f, **k)

        def high_xs(n):
            need(act, S["gi_done"], n)
            a(xs[:, 0, :, :].rearrange("p c b -> p (c b)"), xr(n)).then_inc(S["xs_hi"], 1)

        def sigmoids(n, u):
            act.wait_ge(S["rz_done"], n + 1)
            need(act, S["h_done"], n)
            need(act, S["zh_done"], n)
            a(rz[:, 0:2, :, :], psRZ[u][:, :, :, :], ACT.Sigmoid, scale=1.0 / WS).then_inc(S["rz_sig"], 1)
            need(act, S["nz_done"], n)
            a(rz[:, 2, :, :], psRZ[u][:, 1, :, :], ACT.Sigmoid, scale=-1.0 / WS).then_inc(S["sig_done"], 1)

        def tanh_n(n):
            act.wait_ge(S["bn_done"], n + 1)
            need(act, S["nz_done"], n)
            a(nn[:, :, :], bn[:, :, :], ACT.Tanh, scale=1.0 / WS).then_inc(S["nn_done"], 1)

        def high_h(n, u):
            act.wait_ge(S["h_done"], n + 1)
            need(act, S["gn_done"], n + 1)
            a(hs[:, 0, :, :], Hf[u][:, :, :]).then_inc(S["hs_hi"], 1)

        def stage(t, s):
            q = qs[s - 1] if s else Qs[t.u]
            if s:
                act.wait_ge(S["q_done"], t.n * 3 + s)
            else:
                act.wait_ge(S["Q_done"], t.n + 1)
            need(act, S["f_done"], t.n * 4 + s)
            a(ts_[:, 0, :, :], q[:, :, :], ACT.Tanh).then_inc(S["ts_hi"], 1)
            need(act, S["ts_ready"], t.n * 4 + s)
            a(th[:, :, :], q[:, :, :], ACT.Tanh).then_inc(S["th_done"], 1)
            need(act, S["w_done"], t.n * 4 + s - 1)
            a(sqs[s % 2][:, :, :], q[:, :, :], ACT.Square).then_inc(S["sq_done"], 1)

        def first():
            high_xs(0)
            a(hs[:, 0, :, :], condT[:, :, :]).then_inc(S["hs_hi"], 1)
            a(Qs[0][:, :, :], condT[:, :, :]).then_inc(S["Q_done"], 1)
            high_xs(1)
            with_bias(0, 0)
            sigmoids(0, 0)
            tanh_n(0)
            high_h(0, 0)

        def with_bias(n, u):
            need(act, S["Dr_done"], n - 1)
            act.sem_inc(S["act_passed"], 1)
            for c in range(KC):
                last = a(xbias[u][:, c, :], XR[:, bass.ds(n, 1), c, :].rearrange("p a b -> p (a b)"), ACT.Identity,
                         bias=biasT[:, c:c + 1])
            last.then_inc(S["xbias_done"], 1)

        def step(t):
            stage(t, 0)
            act.wait_ge(S["P_done"], t.n + 1)
            need(act, S["yz_done"], t.n * 3)
            a(Zp[:, :, :], Ps[t.u][:, :, :], ACT.Identity, scale=-BETA, bias=alphas[:, 0:1]).then_inc(S["Z_done"], 1)
            if has(t, 2):
                high_xs(t.n + 2)
            act.wait_ge(S["G_done"], t.n + 1)
            need(act, S["gs_done"], t.n)
            a(Gs[:, :, :], Gd[:, :, :], scale=DT / 6).then_inc(S["Gs_done"], 1)
            stage(t, 1)
            if has(t, 1):
                with_bias(t.n + 1, 1 - t.u)
            stage(t, 2)
            if has(t, 1):
                sigmoids(t.n + 1, 1 - t.u)
                tanh_n(t.n + 1)
            stage(t, 3)
            if has(t, 1):
                high_h(t.n + 1, 1 - t.u)

        run(act, first, step)

    @block.vector
    def _(dve):
        v = nc.vector

        def stt(out, in0, scalar, in1, op1=ALU.add):
            return v.scalar_tensor_tensor(out=flat(out), in0=flat(in0), scalar=scalar, in1=flat(in1), op0=ALU.mult, op1=op1)

        def gate_n(n, u):
            dve.wait_ge(S["rz_sig"], n + 1)
            dve.wait_ge(S["gn_done"], n + 1)
            v.tensor_tensor(an[:, :, :], psN[u][:, 0, :, :], rz[:, 0, :, :], ALU.mult).then_inc(S["an_done"], 1)
            dve.wait_ge(S["an_done"], n + 1)
            need(dve, S["nn_done"], n)
            v.tensor_tensor(bn[:, :, :], psN[u][:, 1, :, :], an[:, :, :], ALU.add).then_inc(S["bn_done"], 1)

        def new_h(n, u):
            dve.wait_ge(S["nn_done"], n + 1)
            dve.wait_ge(S["sig_done"], n + 1)
            v.tensor_tensor(dn[:, :, :], rz[:, 2, :, :], nn[:, :, :], ALU.mult).then_inc(S["nz_done"], 1)
            dve.wait_ge(S["nz_done"], n + 1)
            dve.wait_ge(S["zh_done"], n + 1)
            need(dve, S["X3_done"], n - 1)
            need(dve, S["Dr_done"], n - 1)
            need(dve, S["hs_ready"], n)
            v.tensor_tensor(Hf[u][:, :, :], dn[:, :, :], en[:, :, :], ALU.add).then_inc(S["h_done"], 1)

        def low_t(t, s):
            dve.wait_ge(S["th_done"], t.n * 4 + s + 1)
            v.tensor_tensor(ts_[:, 1, :, :], th[:, :, :], ts_[:, 0, :, :], ALU.subtract).then_inc(S["ts_ready"], 1)

        def cubic(t, s, q):
            dve.wait_ge(S["sq_done"], t.n * 4 + s + 1)
            v.scalar_tensor_tensor(out=flat(ws[s % 2][:, :, :]), in0=flat(sqs[s % 2][:, :, :]), scalar=-3.0, in1=flat(q[:, :, :]),
                                   op0=ALU.add, op1=ALU.mult).then_inc(S["w_done"], 1)

        def turn_out(n, u, half):
            dve.wait_ge(S["ob_done"], n + 1)
            need(dve, out_sent[u], half * (8 * 16))
            v.transpose(flat(ot[u]), flat(ob[u])).then_inc(S["ot_done"], 1)

        def first():
            gate_n(0, 0)
            new_h(0, 0)

        def step(t):
            n = t.n
            Q, P, Qn, Pn = Qs[t.u], Ps[t.u], Qs[1 - t.u], Ps[1 - t.u]
            q2, q3, q4 = qs
            low_t(t, 0)
            cubic(t, 0, Q)
            dve.wait_ge(S["G_done"], n + 1)
            stt(Ea, Gd, H1, Q).then_inc(S["E_done"], 1)
            dve.wait_ge(S["w_done"], n * 4 + 1)
            dve.wait_ge(S["E_done"], n * 2 + 1)
            stt(rs[0], ws[0], -H1 / 3, Ea).then_inc(S["r_done"], 1)
            stt(Eb, Gd, H2, Q).then_inc(S["E_done"], 1)
            dve.wait_ge(S["r_done"], n * 4 + 1)
            dve.wait_ge(S["f_done"], n * 4 + 1)
            stt(q2, psF[:, 0, :, :], H1 / WS, rs[0]).then_inc(S["q_done"], 1)
            dve.wait_ge(S["y1_done"], n + 1)
            stt(e2, ys[0], -H1 * K1, Ea).then_inc(S["e_done"], 1)
            if has(t, 0) and not (isinstance(n, int) and n == 0):
                turn_out(n - 1, 1 - t.u, t.before)
            low_t(t, 1)
            cubic(t, 1, q2)
            dve.wait_ge(S["yz_done"], n * 3 + 1)
            stt(ys[1], ys[0], -BETA * K1, yz[0]).then_inc(S["y_done"], 1)
            dve.wait_ge(S["w_done"], n * 4 + 2)
            dve.wait_ge(S["e_done"], n * 2 + 1)
            stt(rs[1], ws[1], -H1 / 3, e2).then_inc(S["r_done"], 1)
            dve.wait_ge(S["y_done"], n * 3 + 1)
            dve.wait_ge(S["E_done"], n * 2 + 2)
            stt(e3, ys[1], -H2 * K1, Eb).then_inc(S["e_done"], 1)
            dve.wait_ge(S["r_done"], n * 4 + 2)
            dve.wait_ge(S["f_done"], n * 4 + 2)
            stt(q3, psF[:, 1, :, :], H1 / WS, rs[1]).then_inc(S["q_done"], 1)
            dve.wait_ge(S["q_done"], n * 3 + 2)
            need(dve, S["cq_done"], n)
            stt(aq, q3, 2.0, q2).then_inc(S["aq_done"], 1)
            low_t(t, 2)
            cubic(t, 2, q3)
            dve.wait_ge(S["yz_done"], n * 3 + 2)
            stt(ys[2], ys[1], -BETA * K1, yz[1]).then_inc(S["y_done"], 1)
            dve.wait_ge(S["w_done"], n * 4 + 3)
            dve.wait_ge(S["e_done"], n * 2 + 2)
            stt(rs[0], ws[0], -H2 / 3, e3).then_inc(S["r_done"], 1)
            dve.wait_ge(S["y_done"], n * 3 + 2)
            dve.wait_ge(S["Gs_done"], n + 1)
            stt(gs, ys[2], -2 * K1 * DT / 6, Gs).then_inc(S["gs_done"], 1)
            if has(t, 1):
                gate_n(n + 1, 1 - t.u)
            dve.wait_ge(S["r_done"], n * 4 + 3)
            dve.wait_ge(S["f_done"], n * 4 + 3)
            stt(q4, psF[:, 0, :, :], H2 / WS, rs[0]).then_inc(S["q_done"], 1)
            dve.wait_ge(S["gs_done"], n + 1)
            dve.wait_ge(S["cq_done"], n + 1)
            stt(hq, cq, 1.0 / 3, gs).then_inc(S["hq_done"], 1)
            if has(t, 1):
                new_h(n + 1, 1 - t.u)
            low_t(t, 3)
            cubic(t, 3, q4)
            dve.wait_ge(S["hq_done"], n * 2 + 1)
            dve.wait_ge(S["q_done"], n * 3 + 3)
            stt(hr, q4, 1.0 / 3, hq).then_inc(S["hq_done"], 1)
            dve.wait_ge(S["yz_done"], n * 3 + 3)
            stt(ys[3], ys[2], -BETA * K2, yz[0]).then_inc(S["y_done"], 1)
            dve.wait_ge(S["w_done"], n * 4 + 4)
            dve.wait_ge(S["hq_done"], n * 2 + 2)
            stt(rs[1], ws[1], -DT / 18, hr).then_inc(S["r_done"], 1)
            dve.wait_ge(S["y14_done"], n + 1)
            dve.wait_ge(S["y23_done"], n + 1)
            stt(sy, y23, 2.0, y14).then_inc(S["sy_done"], 1)
            dve.wait_ge(S["r_done"], n * 4 + 4)
            dve.wait_ge(S["f_done"], n * 4 + 4)
            stt(qp, psF[:, 1, :, :], DT / 6 / WS, rs[1]).then_inc(S["qp_done"], 1)
            dve.wait_ge(S["sy_done"], n + 1)
            stt(pp, sy, DT * EPSILON / 6, P).then_inc(S["pp_done"], 1)
            dve.wait_ge(S["qp_done"], n + 1)
            need(dve, S["ob_done"], n)
            v.tensor_scalar(flat(Qn), flat(qp), CLAMP, -CLAMP, ALU.min, ALU.max).then_inc(S["Q_done"], 1)
            dve.wait_ge(S["pp_done"], n + 1)
            need(dve, S["G_done"], n)
            need(dve, S["Z_done"], n)
            v.tensor_scalar(flat(Pn), flat(pp), CLAMP, -CLAMP, ALU.min, ALU.max).then_inc(S["P_done"], 1)
            if isinstance(n, int) and n == T - 1:
                turn_out(n, t.u, t.half)

        run(dve, first, step)

    @block.gpsimd
    def _(pool):
        def settled():
            pool.sem_inc(S["passed"], 1)
            return nc.gpsimd

        def tt(out, in0, in1, op=ALU.add):
            return settled().tensor_tensor(flat(out), flat(in0), flat(in1), op)

        def low_xs(n):
            pool.wait_ge(S["xs_hi"], n + 1)
            settled().tensor_tensor(xs[:, 1, :, :].rearrange("p c b -> p (c b)"), xr(n), xs[:, 0, :, :].rearrange("p c b -> p (c b)"),
                            ALU.subtract).then_inc(S["xs_ready"], 1)

        def low_h(n, src):
            pool.wait_ge(S["hs_hi"], n + 1)
            tt(hs[:, 1, :, :], src, hs[:, 0, :, :], ALU.subtract).then_inc(S["hs_ready"], 1)

        def drive(n, u):
            pool.wait_ge(S["h_done"], n + 1)
            pool.wait_ge(S["xbias_done"], n + 1)
            tt(Dr[u], xbias[u], Hf[u]).then_inc(S["Dr_done"], 1)

        def stream(n, u):
            settled().tensor_tensor(flat(X3[u]), xr(n), flat(Hf[u]), ALU.add).then_inc(S["X3_done"], 1)

        def less_p(n, u):
            pool.wait_ge(S["P_done"], n + 1)
            pool.wait_ge(S["Dr_done"], n + 1)
            need(pool, S["gs_done"], n)
            need(pool, S["Gs_done"], n)
            tt(Gd, Dr[u], Ps[u], ALU.subtract).then_inc(S["G_done"], 1)
            pool.wait_ge(S["Z_done"], n + 1)
            tt(ys[0], Qs[u], Zp).then_inc(S["y1_done"], 1)

        def add_q(n, u):
            pool.wait_ge(S["Q_done"], n + 2)
            need(pool, S["ot_done"], n - 1)
            tt(ob[u], X3[u], Qs[1 - u]).then_inc(S["ob_done"], 1)

        def keep_zh(n, u, old):
            pool.wait_ge(S["rz_sig"], n + 1)
            need(pool, S["h_done"], n)
            settled().tensor_tensor(flat(en), rz[:, 1, :, :].rearrange("p c b -> p (c b)"), flat(old), ALU.mult)\
                .then_inc(S["zh_done"], 1)

        def q_plus_z(n, s):
            pool.wait_ge(S["q_done"], n * 3 + s + 1)
            tt(yz[s % 2], qs[s], Zp).then_inc(S["yz_done"], 1)

        def first():
            settled().tensor_copy(flat(Ps[0]), flat(condT)).then_inc(S["P_done"], 1)
            low_xs(0)
            low_h(0, condT)
            low_xs(1)
            keep_zh(0, 0, condT)
            drive(0, 0)
            low_h(1, Hf[0])

        def step(t):
            n, u = t.n, t.u
            less_p(n, u)
            if not (isinstance(n, int) and n == 0):
                add_q(n - 1, 1 - u)
            q_plus_z(n, 0)
            stream(n, u)
            if has(t, 2):
                low_xs(n + 2)
            q_plus_z(n, 1)
            pool.wait_ge(S["aq_done"], n + 1)
            need(pool, S["hq_done"], n * 2 - 1)
            tt(cq, aq, Qs[u], ALU.subtract).then_inc(S["cq_done"], 1)
            if has(t, 1):
                keep_zh(n + 1, 1 - u, Hf[u])
            pool.wait_ge(S["y_done"], n * 3 + 2)
            tt(y23, ys[1], ys[2]).then_inc(S["y23_done"], 1)
            q_plus_z(n, 2)
            if has(t, 1):
                drive(n + 1, 1 - u)
            pool.wait_ge(S["y_done"], n * 3 + 3)
            tt(y14, ys[0], ys[3]).then_inc(S["y14_done"], 1)
            if has(t, 1):
                low_h(n + 2, Hf[1 - u])
            if isinstance(n, int) and n == T - 1:
                add_q(n, u)

        run(pool, first, step)

    @block.sync
    def _(sp):
        def step(t):
            sp.wait_ge(S["ot_done"], t.n + 1)
            for q in range(4):
                for h in range(2):
                    dst = out[h * 32:(h + 1) * 32, bass.ds(t.n, 1), :].rearrange("b a (c q f) -> b (a c) q f", q=4, f=32)[:, :, q, :]
                    src = ot[t.u][q * 32:(q + 1) * 32, :, :].rearrange("p c (h f) -> p c h f", h=2)[:, :, h, :]
                    sp.dma_start(dst, src).then_inc(out_sent[t.u], 16)

        run(sp, lambda: None, step)
        for s in out_sent:
            sp.wait_ge(s, (T // 2) * 8 * 16)


_INS = ["x", "cond_2048", "L0_cond_W_emb", "L0_cond_b_emb", "L0_cond_g_norm", "L0_cond_W_qkv", "L0_cond_g_q", "L0_cond_g_k",
        "L0_cond_W_out", "L2_cond_W_ih", "L2_cond_W_hh", "L2_cond_b_ih", "L2_cond_b_hh", "L3_cond_coupling", "L3_cond_bias"]


def kernel(**inputs):
    import numpy as np
    import concourse.bacc as bacc
    from concourse.bass_utils import run_bass_kernel_spmd

    nc = bacc.Bacc("TRN2", target_bir_lowering=False, num_devices=1)
    arrays, args = {}, []
    for name in _INS:
        a = np.ascontiguousarray(inputs[name])
        arrays[f"in_{name}"] = a
        args.append(nc.dram_tensor(f"in_{name}", a.shape, mybir.dt.from_np(a.dtype), kind="ExternalInput").ap())
    shape = inputs["x"].shape
    out = nc.dram_tensor("out", shape, F32, kind="ExternalOutput").ap()
    rows = nc.dram_tensor("rows_dram", (shape[0], shape[2]), F16, kind="Internal").ap()
    program(nc, *args, out, rows)
    r = run_bass_kernel_spmd(nc, [arrays], core_ids=[0])
    return r.results[0]["out"]
```

```python
from contextlib import ExitStack

import concourse.bass as bass
from concourse import mybir

ALU = mybir.AluOpType
ACT = mybir.ActivationFunctionType
AX = mybir.AxisListType
F32 = mybir.dt.float32
F16 = mybir.dt.float16
I32 = mybir.dt.int32

WS = 64.0
PART = 128
EPS = 1e-6
HEADS = 16
DT, EPSILON, ALPHA, BETA, CLAMP = 0.01, 0.08, 0.7, 0.8, 20.0


class Pair:

    def __init__(self, n, half, u):
        self.n, self.half, self.u = n, half, u
        self.before = half - 1 if u == 0 else half

    def later(self, d, count):
        n = self.n + d
        return None if isinstance(n, int) and n >= count else n


def need(eng, sem, value):
    if isinstance(value, int) and value <= 0:
        return
    eng.wait_ge(sem, value)


def program(nc, x, cond, W_emb, b_emb, g_norm, W_qkv, g_q, g_k, W_out, W_ih, W_hh, b_ih, b_hh,
            coupling, bias, out, rows_dram):
    B, T, D = x.shape
    KC = D // PART
    G3 = W_ih.shape[1]
    DH = D // HEADS
    NPAIR = B // 2
    TOK = 2 * T
    assert TOK == PART and KC == 4 and B == 64 and T == 64

    with ExitStack() as ctx:
        def sb(name, shape, dt=F32, stack=ctx):
            return stack.enter_context(nc.sbuf_tensor(name, shape, dt))

        def sem(name, stack=ctx):
            return stack.enter_context(nc.semaphore(name))

        XR = sb("XR", [PART, T, KC, B])
        condT = sb("condT", [PART, KC, B])
        ident = sb("ident", [PART, PART])
        Wx = sb("Wx", [PART, 2, KC, G3], F16)
        later = dict(
            Wih=Wx, Whh=sb("Whh", [PART, 2, KC, G3], F16), Cp=sb("Cp", [PART, 2, KC, D], F16),
            brow=sb("brow", [PART, 2 * D], F16),
            brz=sb("brz", [PART, 2 * KC]),
            ones=sb("ones", [PART, B], F16), unit=sb("unit", [PART, 1]), biasT=sb("biasT", [PART, KC]), alphas=sb("alphas", [PART, 1]))
        with ExitStack() as attn:
            keep = dict(
                front=sb("front", [PART, 9, D], F32, attn), x_in=[sem(f"x_in{u}", attn) for u in range(2)],
                Wqkv=Wx, Wo=sb("Wo", [PART, 2, KC, D], F16, attn),
                modA=sb("modA", [PART, KC, B], F32, attn), modB=sb("modB", [PART, KC, B], F32, attn),
                WT=sb("WT", [PART, 2, KC, B], F32, attn), lidx=sb("lidx", [PART, 2, KC], F32, attn),
                gqk=sb("gqk", [PART, 1], F32, attn),
                Vbd=[sb(f"Vbd{u}", [PART, 2, 2, HEADS // 2, 64], F16, attn) for u in range(2)])
            with ExitStack() as s:
                setup(nc, s, XR, condT, ident, keep, later, cond, W_emb, b_emb, g_norm, W_qkv, g_q, g_k, b_ih, b_hh, bias, x, rows_dram)
            with ExitStack() as s:
                attention_and_sampling(nc, s, XR, ident, keep, later, x, rows_dram, W_out, coupling, W_hh, W_ih)
        with ExitStack() as s:
            recurrences(nc, s, XR, condT, later, out)


def setup(nc, ctx, XR, condT, ident, keep, later, cond, W_emb, b_emb, g_norm, W_qkv, g_q, g_k, b_ih, b_hh, bias, x, rows_dram):
    B, D = cond.shape
    KC = D // PART
    G3 = W_qkv.shape[1]
    DH = g_q.shape[0]
    Wqkv, modA, modB = keep["Wqkv"], keep["modA"], keep["modB"]
    WT, lidx, gqk, Vbd = keep["WT"], keep["lidx"], keep["gqk"], keep["Vbd"]
    brow, brz, ones, biasT, alphas = (later[n] for n in ("brow", "brz", "ones", "biasT", "alphas"))

    def sb(name, shape, dt=F32):
        return ctx.enter_context(nc.sbuf_tensor(name, shape, dt))

    def sem(name):
        return ctx.enter_context(nc.semaphore(name))

    room = XR[:, :, :, :].rearrange("p t c b -> p (t c b)")
    wq32 = room[:, 0:KC * G3].rearrange("p (c n) -> p c n", c=KC)
    we32 = room[:, KC * G3:KC * (G3 + 2 * D)].rearrange("p (c n) -> p c n", c=KC)
    brow32 = sb("brow32", [1, 2 * D])
    brow_lo = sb("brow_lo", [1, 2 * D], F16)
    bhrz = sb("bhrz", [PART, 2 * KC])
    condtok = sb("condtok", [B, D])
    bemb = sb("bemb", [PART, 2 * KC])
    gnorm = sb("gnorm", [PART, KC])
    gq = sb("gq", [PART, 2])
    ix = sb("ix", [B, D])
    iint = sb("iint", [B, D], I32)
    ir = sb("ir", [B, D])
    igt = sb("igt", [B, D])
    i0 = sb("i0", [B, D])
    i0h = sb("i0h", [B, D], F16)
    w1 = sb("w1", [B, D])
    psC = ctx.enter_context(nc.psum_tensor("psC", [PART, KC, B], F32))
    psW = ctx.enter_context(nc.psum_tensor("psW", [PART, KC, B], F32))
    psE = ctx.enter_context(nc.psum_tensor("psE", [PART, 2 * KC, B], F32))

    cond_in, small_in, wemb_in, bias_in = (sem(n) for n in ("cond_in", "small_in", "wemb_in", "bias_in"))
    wqkv_in = [sem(f"wqkv_in{c}") for c in range(KC)]
    zeros, brow_done = sem("zeros"), sem("brow_done")
    rows_out = sem("rows_out")
    consts = sem("consts")
    grid_step = sem("grid_step")
    rows_ready, w1_ready = sem("rows_ready"), sem("w1_ready")
    cond_T, cond_kept, w1_T, emb_done = sem("cond_T"), sem("cond_kept"), sem("w1_T"), sem("emb_done")
    hi_done, mod_step = sem("hi_done"), sem("mod_step")
    block = ctx.enter_context(nc.Block())

    @block.sync
    def _(sp):
        sp.dma_start(condtok[:, :], cond).then_inc(cond_in, 16)
        sp.dma_start(we32, W_emb.rearrange("(c p) n -> p c n", p=PART)).then_inc(wemb_in, 16)
        sp.dma_start(brow32[:, 0:D], b_ih[2 * D:3 * D].rearrange("(a n) -> a n", a=1)).then_inc(bias_in, 16)
        sp.dma_start(brow32[:, D:2 * D], b_hh[2 * D:3 * D].rearrange("(a n) -> a n", a=1)).then_inc(bias_in, 16)
        for c in range(KC):
            sp.dma_start(wq32[:, c, :], W_qkv[c * PART:(c + 1) * PART, :]).then_inc(wqkv_in[c], 16)
        for u in range(2):
            sp.dma_start(keep["front"][:, u, :], x[2 * u:2 * u + 2, :, :].rearrange("b t d -> (b t) d")).then_inc(keep["x_in"][u], 16)
        sp.wait_ge(rows_ready, 1)
        sp.dma_start(rows_dram, i0h[:, :]).then_inc(rows_out, 16)
        sp.wait_ge(rows_out, 16)

    @block.gpsimd
    def _(pool):
        nc.gpsimd.memset(ident[:, :], 0.0).then_inc(consts, 1)
        pool.wait_ge(consts, 1)
        nc.gpsimd.affine_select(out=ident[:, :], in_=ident[:, :], compare_op=ALU.not_equal, fill=1.0, base=0,
                                pattern=[[-1, PART]], channel_multiplier=1).then_inc(consts, 1)
        nc.gpsimd.iota(lidx[:, :, :], pattern=[[-1, 2], [PART, KC]], base=0, channel_multiplier=1,
                       allow_small_or_imprecise_dtypes=True).then_inc(consts, 1)
        for v in Vbd:
            nc.gpsimd.memset(v[:, :, :, :, :], 0.0).then_inc(consts, 1)
        nc.gpsimd.memset(brow[:, :], 0.0).then_inc(zeros, 1)
        nc.gpsimd.memset(ones[:, :], 1.0)
        nc.gpsimd.memset(alphas[:, :], ALPHA)
        nc.gpsimd.memset(later["unit"][:, :], 1.0)
        with nc.allow_non_contiguous_dma("small vectors, laid along the partitions"):
            pool.dma_start(bemb[:, :], b_emb.rearrange("(c p) -> p c", p=PART)).then_inc(small_in, 16)
            pool.dma_start(gnorm[:, :], g_norm.rearrange("(c p) -> p c", p=PART)).then_inc(small_in, 16)
            for n, g in enumerate((g_q, g_k)):
                for q in range(PART // DH):
                    pool.dma_start(gq[q * DH:(q + 1) * DH, n:n + 1], g.rearrange("(p a) -> p a", a=1)).then_inc(small_in, 16)
            pool.dma_start(brz[:, :], b_ih[0:2 * D].rearrange("(c p) -> p c", p=PART)).then_inc(small_in, 16)
            pool.dma_start(bhrz[:, :], b_hh[0:2 * D].rearrange("(c p) -> p c", p=PART)).then_inc(small_in, 16)
            pool.dma_start(biasT[:, :], bias.rearrange("(c p) -> p c", p=PART)).then_inc(small_in, 16)

    @block.scalar
    def _(act):
        act.wait_ge(cond_T, 1)
        nc.scalar.activation(condT[:, :, :], psC[:, :, :], ACT.Copy).then_inc(cond_kept, 1)
        act.wait_ge(bias_in, 32)
        act.wait_ge(zeros, 1)
        nc.scalar.activation(brow[0:1, :], brow32[:, :], ACT.Copy, scale=WS).then_inc(brow_done, 1)
        for c in range(KC):
            act.wait_ge(wqkv_in[c], 16)
            nc.scalar.activation(Wqkv[:, 0, c, :], wq32[:, c, :], ACT.Copy, scale=WS).then_inc(hi_done, 1)

    @block.vector
    def _(dve):
        v = nc.vector
        dve.wait_ge(cond_in, 16)
        v.tensor_scalar(ix[:, :], condtok[:, :], 1.0, 0.5, ALU.add, ALU.mult).then_inc(grid_step, 1)
        dve.wait_ge(grid_step, 1)
        v.tensor_scalar(ix[:, :], ix[:, :], float(D - 1), 0.0, ALU.mult, ALU.max).then_inc(grid_step, 1)
        dve.wait_ge(grid_step, 2)
        v.tensor_scalar(ix[:, :], ix[:, :], float(D - 1), None, ALU.min).then_inc(grid_step, 1)
        dve.wait_ge(grid_step, 3)
        v.tensor_copy(iint[:, :], ix[:, :]).then_inc(grid_step, 1)
        dve.wait_ge(grid_step, 4)
        v.tensor_copy(ir[:, :], iint[:, :]).then_inc(grid_step, 1)
        dve.wait_ge(grid_step, 5)
        v.tensor_tensor(igt[:, :], ir[:, :], ix[:, :], ALU.is_gt).then_inc(grid_step, 1)
        dve.wait_ge(grid_step, 6)
        v.tensor_tensor(i0[:, :], ir[:, :], igt[:, :], ALU.subtract).then_inc(grid_step, 1)
        dve.wait_ge(grid_step, 7)
        v.tensor_copy(i0h[:, :], i0[:, :]).then_inc(rows_ready, 1)
        v.tensor_tensor(w1[:, :], ix[:, :], i0[:, :], ALU.subtract).then_inc(w1_ready, 1)
        dve.wait_ge(w1_T, 1)
        v.tensor_copy(WT[:, 1, :, :], psW[:, :, :])
        v.tensor_scalar(WT[:, 0, :, :], psW[:, :, :], -1.0, 1.0, ALU.mult, ALU.add)
        dve.wait_ge(brow_done, 1)
        v.scalar_tensor_tensor(out=brow_lo[:, :], in0=brow32[:, :], scalar=WS, in1=brow[0:1, :],
                               op0=ALU.mult, op1=ALU.subtract).then_inc(brow_done, 1)
        dve.wait_ge(brow_done, 2)
        v.tensor_copy(brow[32:33, :], brow_lo[:, :])
        for c in range(KC):
            dve.wait_ge(hi_done, c + 1)
            v.scalar_tensor_tensor(out=Wqkv[:, 1, c, :], in0=wq32[:, c, :], scalar=WS, in1=Wqkv[:, 0, c, :],
                                   op0=ALU.mult, op1=ALU.subtract)
        dve.wait_ge(small_in, 16 * (5 + 2 * (PART // DH)))
        v.tensor_tensor(brz[:, :], brz[:, :], bhrz[:, :], ALU.add)
        v.tensor_scalar(gqk[:, :], gq[:, 0:1], gq[:, 1:2], float(DH) ** -0.5, ALU.mult, ALU.mult)
        dve.wait_ge(emb_done, 1)
        for c in range(KC):
            v.tensor_scalar(modA[:, c, :], psE[:, c, :], bemb[:, c:c + 1], 1.0, ALU.add, ALU.add).then_inc(mod_step, 1)
            v.tensor_scalar(modB[:, c, :], psE[:, KC + c, :], bemb[:, KC + c:KC + c + 1], None, ALU.add)
        dve.wait_ge(mod_step, KC)
        for c in range(KC):
            v.tensor_scalar(modA[:, c, :], modA[:, c, :], gnorm[:, c:c + 1], None, ALU.mult)

    @block.tensor
    def _(pe):
        pe.wait_ge(consts, 2)
        pe.wait_ge(cond_in, 16)
        for c in range(KC):
            last = nc.tensor.transpose(psC[:, c, :], condtok[:, c * PART:(c + 1) * PART], ident[0:B, 0:B])
        last.then_inc(cond_T, 1)
        pe.wait_ge(w1_ready, 1)
        for c in range(KC):
            last = nc.tensor.transpose(psW[:, c, :], w1[:, c * PART:(c + 1) * PART], ident[0:B, 0:B])
        last.then_inc(w1_T, 1)
        pe.wait_ge(cond_kept, 1)
        pe.wait_ge(wemb_in, 16)
        for m in range(2 * KC):
            for c in range(KC):
                last = nc.tensor.matmul(psE[:, m, :], we32[:, c, m * PART:(m + 1) * PART], condT[:, c, :],
                                        start=(c == 0), stop=(c == KC - 1))
        last.then_inc(emb_done, 1)


def attention_and_sampling(nc, ctx, XR, ident, keep, later, x, rows_dram, W_out, coupling, W_hh, W_ih):
    B, T, D = x.shape
    KC = D // PART
    G3 = W_ih.shape[1]
    DH = D // HEADS
    NP = B // 2
    Whh, Cp, Wih = later["Whh"], later["Cp"], later["Wih"]
    Wqkv, Wo, modA, modB = keep["Wqkv"], keep["Wo"], keep["modA"], keep["modB"]
    WT, lidx, gqk, Vbd = keep["WT"], keep["lidx"], keep["gqk"], keep["Vbd"]

    def sb(name, shape, dt=F32):
        return ctx.enter_context(nc.sbuf_tensor(name, shape, dt))

    def sem(name):
        return ctx.enter_context(nc.semaphore(name))

    front = keep["front"]
    xtok = [front[:, u, :] for u in range(2)]
    yt = [front[:, 2 + u, :] for u in range(2)]
    xa = front[:, 4, :].rearrange("p (c b t) -> p c b t", c=KC, b=2)
    sq = front[:, 5:7, :]
    xn = [front[:, 7 + u, :].bitcast(F16).rearrange("p (i c n) -> p i c n", i=2, c=KC) for u in range(2)]
    wih32 = [front[:, 3 * j:3 * j + 3, :].rearrange("p a n -> p (a n)") for j in range(3)]
    QK, X = slice(0, 2 * HEADS), slice(2 * HEADS, 2 * HEADS + 1)
    ss, ms, rs, rt = (sb(n, [PART, 2 * HEADS + 1]) for n in ("ss", "ms", "rs", "rt"))
    qn = sb("qn", [PART, 2, D])
    qkT = sb("qkT", [PART, 2, 2, KC, PART], F16)
    S = sb("S", [PART, HEADS, T])
    mx = sb("mx", [PART, 4, 4])
    den = sb("den", [PART, HEADS])
    rden = sb("rden", [PART, HEADS])
    PT = sb("PT", [PART, 2, HEADS // 2, PART], F16)
    oT = sb("oT", [PART, 2, KC, PART], F16)
    x1 = sb("x1", [PART, 2, KC, 2, T], F16)
    rows = [sb(f"rows{u}", [PART, D], F16) for u in range(2)]
    E = [sb(f"E{u}", [PART, 2, KC, D], F16) for u in range(2)]
    um = [sb(f"um{u}", [PART, 2, KC, T]) for u in range(2)]
    room = [E[u][:, :, :, :].rearrange("p t c n -> p (t c n)").bitcast(F32) for u in range(2)]
    wo32, cp32 = (r.rearrange("p (c n) -> p c n", c=KC) for r in room)

    def ps(name, shape):
        return ctx.enter_context(nc.psum_tensor(name, shape, F32))

    psQ = ps("psQ", [PART, 3, D])
    psS = ps("psS", [PART, 4, D])
    psO = ps("psO", [PART, KC, PART])
    psL = [psQ[:, b, :].rearrange("p (v c t) -> p v c t", v=2, c=KC) for b in range(2)]
    psP = psQ[:, 2, :].rearrange("p (c b t) -> p c b t", c=KC, b=2)

    def turned(j):
        return psS[:, j, :].rearrange("p (c n) -> p c n", c=KC)

    x_in = keep["x_in"]
    rows_in = [sem(f"rows_in{u}") for u in range(2)]
    ssx_done, ms_done, rs_step, y_done = sem("ssx_done"), sem("ms_done"), sem("rs_step"), sem("y_done")
    xy_T, xT_kept, xa_done, xb_done = sem("xy_T"), sem("xT_kept"), sem("xa_done"), sem("xb_done")
    xn_hi, xn_ready = sem("xn_hi"), sem("xn_ready")
    qkv_done, sq_done, ssq_done, qn_done = sem("qkv_done"), sem("sq_done"), sem("ssq_done"), sem("qn_done")
    v_hi, v_ready = sem("v_hi"), sem("v_ready")
    qk_T, qk_hi, qk_ready = sem("qk_T"), sem("qk_hi"), sem("qk_ready")
    sc_done, mx_done, sub_done, exp_done = sem("sc_done"), sem("mx_done"), sem("sub_done"), sem("exp_done")
    den_done, rden_done, p_done = sem("den_done"), sem("rden_done"), sem("p_done")
    p_T, pt_hi, pt_ready = sem("p_T"), sem("pt_hi"), sem("pt_ready")
    mix_done, o_hi, o_ready = sem("mix_done"), sem("o_hi"), sem("o_ready")
    proj_done, x1_done, x1_hi, x1_ready = sem("proj_done"), sem("x1_done"), sem("x1_hi"), sem("x1_ready")
    e_built, samp_done, um_done, us_done, x2_done = (sem(n) for n in ("e_built", "samp_done", "um_done", "us_done", "x2_done"))
    passed = sem("passed")
    room_in = [sem(f"room_in{u}") for u in range(2)]
    wo_plus, wo_hi, wo_lo, cT_done, cp_hi, cp_lo, whh_hi, whh_lo, wih_hi, wih_lo = (
        sem(n) for n in ("wo_plus", "wo_hi", "wo_lo", "cT_done", "cp_hi", "cp_lo", "whh_hi", "whh_lo", "wih_hi", "wih_lo"))
    scaled = sem("scaled")
    wih_in = [sem(f"wih_in{j}") for j in range(3)]
    block = ctx.enter_context(nc.Block())

    def turned_coupling(c):
        return (psS[:, 0, :], psS[:, 1, :], psO[:, :, :].rearrange("p c n -> p (c n)"), psQ[:, 2, :])[c]

    LOAD_WHH = {0: (0,), 1: (1, 2), 2: (3,)}

    FIRST, LAST = -2, NP + 3
    LOOP0, NLOOP = 4, (NP - 3 - 4) // 2

    def run(eng, slot):
        def at(i):
            def pair(d):
                n = i + d
                return Pair(n, n // 2, n % 2) if 0 <= n < NP else None
            return pair
        for i in range(FIRST, LOOP0):
            slot(at(i), i)
        with eng.Fori(0, NLOOP) as it:
            for j in range(2):
                def pair(d, j=j):
                    c = LOOP0 + j + d
                    return Pair(it * 2 + c, it + c // 2, c % 2)
                slot(pair, None)
        for i in range(LOOP0 + 2 * NLOOP, LAST):
            slot(at(i), i)

    @block.sync
    def _(sp):
        def load_x(p):
            if isinstance(p.n, int) and p.n < 2:
                return
            need(sp, xy_T, p.n - 1)
            sp.dma_start(xtok[p.u][:, :], x_rows(p)).then_inc(x_in[p.u], 16)

        def x_rows(p):
            return x[bass.ds(p.n * 2, 2), :, :].rearrange("b t d -> (b t) d")

        def load_rows(p):
            for b in range(2):
                need(sp, e_built, p.n * 2 + b - 1)
                sp.dma_start(rows[b][:, :], rows_dram[bass.ds(p.n * 2 + b, 1), :].rearrange("a n -> (a n)")
                             .partition_broadcast(PART)).then_inc(rows_in[b], 16)

        def load_whh(c):
            if c == 0:
                sp.wait_ge(cT_done, KC)
            elif c == 1:
                sp.wait_ge(wo_lo, 1)
            else:
                sp.wait_ge(whh_lo, c - 1)
            sp.dma_start(room[1 - c % 2][:, 0:G3], W_hh[c * PART:(c + 1) * PART, :]).then_inc(room_in[1 - c % 2], 16)

        def load_wih(c):
            if c == 0:
                sp.wait_ge(qkv_done, NP * 3)
                sp.wait_ge(ssq_done, NP * 2)
                sp.wait_ge(xy_T, NP)
                sp.wait_ge(xn_ready, NP)
            if c == 3:
                sp.wait_ge(wih_lo, 1)
            sp.dma_start(wih32[c % 3], W_ih[c * PART:(c + 1) * PART, :]).then_inc(wih_in[c % 3], 16)

        def slot(pair, i):
            if p := pair(2):
                load_x(p)
            if i == FIRST:
                sp.dma_start(cp32, coupling.rearrange("(c p) n -> p c n", p=PART)).then_inc(room_in[1], 16)
                sp.dma_start(wo32, W_out.rearrange("(c p) n -> p c n", p=PART)).then_inc(room_in[0], 16)
            if p := pair(-2):
                load_rows(p)
            if i in LOAD_WHH:
                for c in LOAD_WHH[i]:
                    load_whh(c)
            if i == NP:
                for c in range(KC):
                    load_wih(c)

        run(sp, slot)

    @block.gpsimd
    def _(pool):
        def settled():
            pool.sem_inc(passed, 1)
            return nc.gpsimd

        def low_w(w, c, w32, hi, done):
            pool.wait_ge(hi, c + 1)
            settled().tensor_tensor(w[:, 1, c, :], w32, w[:, 0, c, :], ALU.subtract).then_inc(done, 1)

        def add_taps(p, b):
            pool.wait_ge(um_done, p.n * 2 + b + 1)
            us = um[b][:, 0, :, :]
            settled().tensor_tensor(us, us, um[b][:, 1, :, :], ALU.add).then_inc(us_done, 1)
            pool.wait_ge(us_done, p.n * 2 + b + 1)
            r = XR[:, :, :, bass.ds(p.n * 2 + b, 1)].rearrange("p t c a -> p c (t a)")
            settled().tensor_tensor(r, r, us, ALU.add).then_inc(x2_done, 1)

        def norm_p(p):
            pool.wait_ge(rden_done, p.n + 1)
            settled().tensor_tensor(S[:, :, :], S[:, :, :], rden[:, :].unsqueeze(2).broadcast_to([PART, HEADS, T]), ALU.mult)\
                .then_inc(p_done, 1)

        def low_x1(p):
            pool.wait_ge(x1_hi, p.n * 2 + 2)
            need(pool, samp_done, p.n * 2)
            for b in range(2):
                last = settled().tensor_tensor(x1[:, 1, :, b, :], XR[:, :, :, bass.ds(p.n * 2 + b, 1)].rearrange("p t c a -> p c (t a)"),
                                       x1[:, 0, :, b, :], ALU.subtract)
            last.then_inc(x1_ready, 1)

        def shift_x(p):
            pool.wait_ge(xa_done, p.n + 1)
            settled().tensor_tensor(xa[:, :, :, :], xa[:, :, :, :],
                            modB[:, :, bass.ds(p.n * 2, 2)].unsqueeze(3).broadcast_to([PART, KC, 2, T]), ALU.add)\
                .then_inc(xb_done, 1)

        def low_x(p):
            pool.wait_ge(xn_hi, p.n + 1)
            settled().tensor_tensor(xn[p.u][:, 1, :, :], xa[:, :, :, :].rearrange("p c b t -> p c (b t)"), xn[p.u][:, 0, :, :],
                            ALU.subtract).then_inc(xn_ready, 1)

        def slot(pair, i):
            if p := pair(1):
                low_x(p)
            for c in {1: (1,), 2: (2, 3)}.get(i, ()):
                low_w(Whh, c, room[1 - c % 2][:, 0:G3], whh_hi, whh_lo)
            for c in {NP: (0, 1), NP + 1: (2,), NP + 2: (3,)}.get(i, ()):
                low_w(Wih, c, wih32[c % 3], wih_hi, wih_lo)
            if p := pair(-3):
                add_taps(p, 0)
            if p := pair(-1):
                norm_p(p)
            if p := pair(-3):
                add_taps(p, 1)
            if p := pair(-2):
                low_x1(p)
            if p := pair(2):
                shift_x(p)
            if i == 0:
                pool.wait_ge(wo_hi, 1)
                settled().tensor_tensor(Wo[:, 1, :, :], wo32, Wo[:, 0, :, :], ALU.subtract).then_inc(wo_lo, 1)
                low_w(Whh, 0, room[1][:, 0:G3], whh_hi, whh_lo)

        run(pool, slot)

    @block.scalar
    def _(act):
        def a(out, in_, f=ACT.Copy, **k):
            return nc.scalar.activation(out, in_, f, **k)

        def squares_x(p):
            act.wait_ge(x_in[p.u], p.half * 16 + 16)
            need(act, ms_done, p.n)
            need(act, xy_T, p.n - 1)
            a(yt[p.u][:, :], xtok[p.u][:, :], ACT.Square, accum_out=ss[:, X]).then_inc(ssx_done, 1)

        def high_qk(p):
            act.wait_ge(qk_T, p.n + 1)
            need(act, sc_done, p.n)
            a(qkT[:, 0, 0, :, :], turned(0), scale=gqk[:, 0:1]).then_inc(qk_hi, 1)
            a(qkT[:, 0, 1, :, :], turned(1)).then_inc(qk_hi, 1)

        def high_whh(c):
            act.wait_ge(room_in[1 - c % 2], 32 if c < 2 else 48)
            w = room[1 - c % 2][:, 0:G3]
            a(w, w, scale=WS).then_inc(scaled, 1)
            act.wait_ge(scaled, c + 2)
            a(Whh[:, 0, c, :], w).then_inc(whh_hi, 1)

        def high_wih(c):
            act.wait_ge(wih_in[c % 3], 16 if c < 3 else 32)
            a(wih32[c % 3], wih32[c % 3], scale=WS).then_inc(scaled, 1)
            act.wait_ge(scaled, KC + c + 2)
            a(Wih[:, 0, c, :], wih32[c % 3]).then_inc(wih_hi, 1)

        def squares_qk(p, n):
            act.wait_ge(qkv_done, p.n * 3 + n + 1)
            need(act, ssq_done, p.n * 2 + n - 1)
            a(sq[:, n, :], psQ[:, n, :], ACT.Square).then_inc(sq_done, 1)

        def high_v(p):
            act.wait_ge(qkv_done, p.n * 3 + 3)
            need(act, mix_done, p.n - 1)
            for b in range(2):
                for r in range(2):
                    src = psQ[b * T:(b + 1) * T, 2, :].rearrange("p (j r d) -> p j r d", r=2, d=DH)[:, :, r, :]
                    a(Vbd[p.u][r * T:(r + 1) * T, b, 0, :, r * DH:(r + 1) * DH], src).then_inc(v_hi, 1)

        def high_p(p):
            act.wait_ge(p_T, p.n + 1)
            need(act, mix_done, p.n)
            for h in range(2):
                a(PT[:, 0, 4 * h:4 * h + 4, :].rearrange("p (r j) n -> p r (j n)", r=2), psS[:, 2 * h:2 * h + 2, 256:512])\
                    .then_inc(pt_hi, 1)

        def exps(p):
            act.wait_ge(sub_done, p.n + 1)
            a(S[:, :, :], S[:, :, :], ACT.Exp).then_inc(exp_done, 1)

        def high_o(p):
            act.wait_ge(mix_done, p.n + 1)
            need(act, proj_done, p.n)
            a(oT[:, 0, :, :], psO[:, :, :]).then_inc(o_hi, 1)

        def high_x1(p):
            act.wait_ge(x1_done, p.n * 2 + 2)
            need(act, samp_done, p.n * 2)
            for b in range(2):
                a(x1[:, 0, :, b, :], XR[:, :, :, bass.ds(p.n * 2 + b, 1)].rearrange("p t c a -> p c (t a)")).then_inc(x1_hi, 1)

        def keep_xT(p):
            act.wait_ge(xy_T, p.n + 1)
            for b in range(2):
                last = a(XR[:, :, :, bass.ds(p.n * 2 + b, 1)].rearrange("p t c a -> p c (t a)"),
                         psS[:, 2, :].rearrange("p (c b t) -> p c b t", c=KC, b=2)[:, :, b, :])
            last.then_inc(xT_kept, 1)

        def high_x(p):
            act.wait_ge(xb_done, p.n + 1)
            need(act, qkv_done, (p.n - 1) * 3)
            a(xn[p.u][:, 0, :, :], xa[:, :, :, :].rearrange("p c b t -> p c (b t)")).then_inc(xn_hi, 1)

        def slot(pair, i):
            if p := pair(0):
                squares_qk(p, 0)
            if p := pair(-2):
                high_p(p)
            if i == NP + 1:
                high_wih(2)
            if p := pair(2):
                squares_x(p)
            if p := pair(0):
                squares_qk(p, 1)
            if p := pair(-1):
                high_qk(p)
            if i == NP:
                high_wih(0)
            if p := pair(1):
                high_x(p)
            if p := pair(-2):
                high_o(p)
            if p := pair(0):
                high_v(p)
            if i == 0:
                act.wait_ge(wo_plus, 1)
                a(wo32, wo32, scale=WS).then_inc(scaled, 1)
                act.wait_ge(scaled, 1)
                a(Wo[:, 0, :, :], wo32).then_inc(wo_hi, 1)
            if i in (1, 2):
                high_whh(2 * i - 1)
            if i == NP:
                high_wih(1)
            if p := pair(-1):
                exps(p)
            if i == NP + 1:
                high_wih(3)
            if p := pair(2):
                keep_xT(p)
            if p := pair(-2):
                high_x1(p)
            if i == -1:
                for c in range(KC):
                    act.wait_ge(cT_done, c + 1)
                    a(Cp[:, 0, c, :], turned_coupling(c), scale=WS).then_inc(cp_hi, 1)
            if i in (0, 1):
                high_whh(2 * i)

        run(act, slot)

    @block.vector
    def _(dve):
        v = nc.vector

        STEPS = 11
        LOWS = (4, 6)
        EARLY = 4

        def low_qk(p, n):
            dve.wait_ge(qk_hi, p.n * 2 + n + 1)
            need(dve, sc_done, p.n)
            if n == 0:
                v.scalar_tensor_tensor(out=qkT[:, 1, 0, :, :], in0=turned(0), scalar=gqk[:, 0:1],
                                       in1=qkT[:, 0, 0, :, :], op0=ALU.mult, op1=ALU.subtract)
            else:
                v.tensor_tensor(qkT[:, 1, 1, :, :], turned(1), qkT[:, 0, 1, :, :], ALU.subtract).then_inc(qk_ready, 1)

        def scale_x(p):
            dve.wait_ge(rs_step, p.n * STEPS + STEPS)
            dve.wait_ge(x_in[p.u], p.half * 16 + 16)
            need(dve, xy_T, p.n - 1)
            v.tensor_scalar(yt[p.u][:, :], xtok[p.u][:, :], rs[:, X], None, ALU.mult).then_inc(y_done, 1)

        def build_tap(p, b, k):
            if k == 0:
                dve.wait_ge(rows_in[b], p.n * 16 + 16)
                need(dve, samp_done, p.n * 2 + b - 1)
                if isinstance(p.n, int) and p.n == 0:
                    dve.wait_ge(whh_lo, KC)
            t, c = k // KC, k % KC
            e = v.tensor_scalar(E[b][:, t, c, :], rows[b][:, :], lidx[:, t, c:c + 1], None, ALU.is_equal)
            if k == 2 * KC - 1:
                e.then_inc(e_built, 1)

        def means(n, qk, x):
            if x:
                dve.wait_ge(ssx_done, x.n + 1)
                last = v.tensor_scalar(ms[:, X], ss[:, X], 1.0 / D, EPS, ALU.mult, ALU.add)
            if qk:
                dve.wait_ge(ssq_done, qk.n * 2 + 2)
                last = v.tensor_scalar(ms[:, QK], ss[:, QK], 1.0 / DH, EPS * WS * WS, ALU.mult, ALU.add)
            last.then_inc(ms_done, 1)

        def rsqrt_step(n, cols, k):
            m, r, t = ms[:, cols], rs[:, cols], rt[:, cols]
            if k == 0:
                dve.wait_ge(ms_done, n + 1)
                o = v.tensor_scalar(t.bitcast(I32), m.bitcast(I32), 1, None, ALU.logical_shift_right)
            else:
                dve.wait_ge(rs_step, n * STEPS + k)
                if k == 1:
                    o = v.tensor_scalar(r.bitcast(I32), t.bitcast(I32), -1, 0x5F3759DF, ALU.mult, ALU.add)
                elif k % 3 == 2:
                    o = v.tensor_tensor(t, r, r, ALU.mult)
                elif k % 3 == 0:
                    o = v.scalar_tensor_tensor(out=t, in0=t, scalar=-0.5, in1=m, op0=ALU.mult, op1=ALU.mult)
                else:
                    o = v.scalar_tensor_tensor(out=r, in0=t, scalar=1.5, in1=r, op0=ALU.add, op1=ALU.mult)
            o.then_inc(rs_step, 1)

        def sums_qk(p, n):
            dve.wait_ge(sq_done, p.n * 2 + n + 1)
            v.tensor_reduce(ss[:, n * HEADS:(n + 1) * HEADS], sq[:, n, :].rearrange("p (h d) -> p h d", d=DH), AX.X, ALU.add)\
                .then_inc(ssq_done, 1)

        def scale_qk(p):
            dve.wait_ge(rs_step, p.n * STEPS + 3 * STEPS)
            need(dve, qk_T, p.n)
            for n in range(2):
                v.tensor_tensor(qn[:, n, :].rearrange("p (h d) -> p h d", d=DH), psQ[:, n, :].rearrange("p (h d) -> p h d", d=DH),
                                rs[:, n * HEADS:(n + 1) * HEADS].unsqueeze(2).broadcast_to([PART, HEADS, DH]), ALU.mult)\
                    .then_inc(qn_done, 1)

        def low_v(p):
            for b in range(2):
                for r in range(2):
                    dve.wait_ge(v_hi, p.n * 4 + 2 * b + 2)
                    src = psQ[b * T:(b + 1) * T, 2, :].rearrange("p (j r d) -> p j r d", r=2, d=DH)[:, :, r, :]
                    dst = Vbd[p.u][r * T:(r + 1) * T, b, :, :, r * DH:(r + 1) * DH]
                    last = v.tensor_tensor(dst[:, 1, :, :], src, dst[:, 0, :, :], ALU.subtract)
            last.then_inc(v_ready, 1)

        def low_p(p):
            for h in range(2):
                dve.wait_ge(pt_hi, p.n * 2 + h + 1)
                hi, lo = (PT[:, i, 4 * h:4 * h + 4, :].rearrange("p (r j) n -> p r (j n)", r=2) for i in range(2))
                last = v.tensor_tensor(lo, psS[:, 2 * h:2 * h + 2, 256:512], hi, ALU.subtract)
            last.then_inc(pt_ready, 1)

        def subtract_max(p):
            sc = psS[:, :, 0:256].rearrange("p r (c k) -> p r c k", c=4)
            dve.wait_ge(sc_done, p.n + 1)
            v.tensor_reduce(mx[:, :, :], sc, AX.X, ALU.max).then_inc(mx_done, 1)
            dve.wait_ge(mx_done, p.n + 1)
            need(dve, p_T, p.n)
            v.tensor_tensor(S[:, :, :].rearrange("p (c r) k -> p r c k", r=4), sc,
                            mx[:, :, :].unsqueeze(3).broadcast_to([PART, 4, 4, T]), ALU.subtract).then_inc(sub_done, 1)

        def weigh_taps(p, b):
            dve.wait_ge(samp_done, p.n * 2 + b + 1)
            need(dve, x2_done, p.n * 2 + b - 1)
            v.tensor_tensor(um[b][:, :, :, :].rearrange("p v c t -> p (v c) t"),
                            psL[b].rearrange("p v c t -> p (v c) t"),
                            WT[:, :, :, bass.ds(p.n * 2 + b, 1)].rearrange("p v c a -> p (v c) a").broadcast_to([PART, 2 * KC, T]),
                            ALU.mult).then_inc(um_done, 1)

        def sum_p(p):
            dve.wait_ge(exp_done, p.n + 1)
            v.tensor_reduce(den[:, :], S[:, :, :], AX.X, ALU.add).then_inc(den_done, 1)
            dve.wait_ge(den_done, p.n + 1)
            need(dve, p_done, p.n)
            v.reciprocal(rden[:, :], den[:, :]).then_inc(rden_done, 1)

        def low_o(p):
            dve.wait_ge(o_hi, p.n + 1)
            v.tensor_tensor(oT[:, 1, :, :], psO[:, :, :], oT[:, 0, :, :], ALU.subtract).then_inc(o_ready, 1)

        def residual(p):
            dve.wait_ge(proj_done, p.n + 1)
            dve.wait_ge(xT_kept, p.n + 1)
            for b in range(2):
                r = XR[:, :, :, bass.ds(p.n * 2 + b, 1)].rearrange("p t c a -> p c (t a)")
                v.scalar_tensor_tensor(out=r, in0=psP[:, :, b, :], scalar=1.0 / (WS * WS), in1=r,
                                       op0=ALU.mult, op1=ALU.add).then_inc(x1_done, 1)

        def modulate(p):
            dve.wait_ge(xy_T, p.n + 1)
            need(dve, xn_ready, p.n)
            v.tensor_tensor(xa[:, :, :, :], psS[:, 3, :].rearrange("p (c b t) -> p c b t", c=KC, b=2),
                            modA[:, :, bass.ds(p.n * 2, 2)].unsqueeze(3).broadcast_to([PART, KC, 2, T]), ALU.mult)\
                .then_inc(xa_done, 1)

        def slot(pair, i):
            x, qk, tap = pair(2), pair(0), pair(-3)
            n = x.n if x else qk.n + 2 if qk else None
            cols = slice(QK.start if qk else X.start, X.stop if x else QK.stop)
            for k in range(EARLY):
                if tap:
                    build_tap(tap, 1, k)
            if qk:
                sums_qk(qk, 0)
            if p := pair(-2):
                low_p(p)
            if qk:
                sums_qk(qk, 1)
            if x or qk:
                means(n, qk, x)
            for k in range(STEPS):
                if tap and k + EARLY < 2 * KC:
                    build_tap(tap, 1, k + EARLY)
                if x or qk:
                    rsqrt_step(n, cols, k)
                if (p := pair(-1)) and k in LOWS:
                    low_qk(p, LOWS.index(k))
            if qk:
                scale_qk(qk)
            if x:
                scale_x(x)
            if p := pair(-2):
                low_o(p)
            if qk:
                low_v(qk)
            if p := pair(-1):
                subtract_max(p)
            if tap:
                weigh_taps(tap, 0)
            if p := pair(-1):
                sum_p(p)
            if tap:
                weigh_taps(tap, 1)
            if p := pair(-2):
                for k in range(2 * KC):
                    build_tap(p, 0, k)
            if x:
                modulate(x)
            if p := pair(-2):
                residual(p)
            if i == -1:
                for c in range(KC):
                    dve.wait_ge(cp_hi, c + 1)
                    v.scalar_tensor_tensor(out=Cp[:, 1, c, :], in0=turned_coupling(c), scalar=WS, in1=Cp[:, 0, c, :],
                                           op0=ALU.mult, op1=ALU.subtract).then_inc(cp_lo, 1)
                dve.wait_ge(room_in[0], 16)
                for c in range(KC):
                    d = wo32[:, c, c * PART:(c + 1) * PART]
                    last = v.tensor_tensor(d, d, ident[:, :], ALU.add)
                last.then_inc(wo_plus, 1)

        run(dve, slot)

    @block.tensor
    def _(pe):
        mm = nc.tensor.matmul
        TERMS = ((0, 0), (0, 1), (1, 0))

        def turn_qk(p):
            pe.wait_ge(qn_done, p.n * 2 + 2)
            need(pe, sub_done, p.n)
            need(pe, pt_ready, p.n)
            need(pe, qk_ready, p.n)
            for n in range(2):
                for c in range(KC):
                    last = nc.tensor.transpose(turned(n)[:, c, :], qn[:, n, c * PART:(c + 1) * PART], ident[:, :])
            last.then_inc(qk_T, 1)

        def project(p, n):
            if n == 0:
                pe.wait_ge(xn_ready, p.n + 1)
            if n == 2 and isinstance(p.n, int) and p.n == 0:
                pe.wait_ge(cp_lo, KC)
            if n == 0:
                need(pe, qn_done, p.n * 2 - 1)
                need(pe, um_done, p.n * 2 - 7)
            elif n == 1:
                need(pe, qn_done, p.n * 2)
                need(pe, um_done, p.n * 2 - 6)
            else:
                need(pe, v_ready, p.n)
                need(pe, x1_done, p.n * 2 - 4)
            for c in range(KC):
                for t, (i, j) in enumerate(TERMS):
                    last = mm(psQ[:, n, :], xn[p.u][:, i, c, :], Wqkv[:, j, c, n * D:(n + 1) * D],
                              start=(c == 0 and t == 0), stop=(c == KC - 1 and t == 2))
            last.then_inc(qkv_done, 1)

        def turn_p(p):
            pe.wait_ge(p_done, p.n + 1)
            need(pe, pt_ready, p.n)
            late = p.later(3, NP)
            if late is not None:
                need(pe, xT_kept, late + 1)
                need(pe, xa_done, late + 1)
            for j in range(HEADS // 2):
                o = psS[:, j // 2, 256 + (j % 2) * PART:256 + (j % 2 + 1) * PART]
                last = nc.tensor.transpose(o, S[:, 2 * j:2 * j + 2, :].rearrange("p h k -> p (h k)"), ident[:, :])
            last.then_inc(p_T, 1)

        def scores(p):
            pe.wait_ge(qk_ready, p.n + 1)
            late = p.later(2, NP)
            if late is not None:
                need(pe, xT_kept, late + 1)
                need(pe, xa_done, late + 1)
            need(pe, sub_done, p.n)
            need(pe, pt_ready, p.n)
            for c in range(4):
                for b in range(2):
                    for t, (i, j) in enumerate(TERMS):
                        for r in range(4):
                            rows_ = slice(r * DH, (r + 1) * DH)
                            last = mm(psS[b * T:(b + 1) * T, r, c * T:(c + 1) * T],
                                      qkT[rows_, i, 0, c, b * T:(b + 1) * T], qkT[rows_, j, 1, c, b * T:(b + 1) * T],
                                      start=(t == 0), stop=(t == 2))
            last.then_inc(sc_done, 1)

        def sample(p, b):
            pe.wait_ge(e_built, p.n * 2 + b + 1)
            pe.wait_ge(x1_ready, p.n + 1)
            late = p.later(3, NP)
            need(pe, qn_done, NP * 2 if late is None else late * 2 + b + 1)
            need(pe, um_done, p.n * 2 + b - 1)
            o = psL[b]
            for t in range(2):
                for m in range(KC):
                    for c in range(KC):
                        for i in range(2):
                            last = mm(o[:, t, m, :], E[b][:, t, c, m * PART:(m + 1) * PART], x1[:, i, c, b, :],
                                      start=(c == 0 and i == 0), stop=(c == KC - 1 and i == 1))
            last.then_inc(samp_done, 1)

        def mix(p):
            pe.wait_ge(pt_ready, p.n + 1)
            pe.wait_ge(v_ready, p.n + 1)
            need(pe, o_ready, p.n)
            for j in range(HEADS // 2):
                for b in range(2):
                    for t, (i, k) in enumerate(TERMS):
                        last = mm(psO[(j % 2) * 64:(j % 2 + 1) * 64, j // 2, b * T:(b + 1) * T],
                                  Vbd[p.u][:, b, i, j, :], PT[:, k, j, b * T:(b + 1) * T], start=(t == 0), stop=(t == 2))
            last.then_inc(mix_done, 1)

        def proj(p):
            pe.wait_ge(o_ready, p.n + 1)
            late = p.later(2, NP)
            if late is not None:
                need(pe, v_ready, late + 1)
            need(pe, x1_done, p.n * 2)
            for m in range(KC):
                for c in range(KC):
                    for t, (i, j) in enumerate(TERMS):
                        last = mm(psP[:, m, :, :].rearrange("p b t -> p (b t)"), Wo[:, i, c, m * PART:(m + 1) * PART], oT[:, j, c, :],
                                  start=(c == 0 and t == 0), stop=(c == KC - 1 and t == 2))
            last.then_inc(proj_done, 1)

        def turn_x(p):
            pe.wait_ge(y_done, p.n + 1)
            pe.wait_ge(x_in[p.u], p.half * 16 + 16)
            need(pe, sub_done, p.n - 2)
            need(pe, pt_ready, p.n - 3)
            need(pe, xT_kept, p.n)
            need(pe, xa_done, p.n)
            for n, src in ((2, xtok[p.u]), (3, yt[p.u])):
                for c in range(KC):
                    last = nc.tensor.transpose(turned(n)[:, c, :], src[:, c * PART:(c + 1) * PART], ident[:, :])
            last.then_inc(xy_T, 1)

        def slot(pair, i):
            if p := pair(0):
                project(p, 0)
            if p := pair(-2):
                turn_p(p)
            if p := pair(0):
                project(p, 1)
            if i == NP:
                sample(pair(-3), 0)
                sample(pair(-3), 1)
            if p := pair(-1):
                turn_qk(p)
            if p := pair(-2):
                mix(p)
            if p := pair(0):
                project(p, 2)
            if p := pair(-1):
                scores(p)
            if (p := pair(-3)) and i != NP:
                sample(p, 0)
                sample(p, 1)
            if p := pair(-2):
                proj(p)
            if p := pair(2):
                turn_x(p)
            if i == -1:
                pe.wait_ge(room_in[1], 16)
                for c in range(KC):
                    for n in range(KC):
                        last = nc.tensor.transpose(turned_coupling(c)[:, n * PART:(n + 1) * PART],
                                                   cp32[:, n, c * PART:(c + 1) * PART], ident[:, :])
                    last.then_inc(cT_done, 1)

        run(pe, slot)


def recurrences(nc, ctx, XR, condT, later, out):
    B, T, D = out.shape
    KC = D // PART
    G3 = 3 * D
    GC = G3 // PART
    H2, H1 = DT, DT / 2
    K1, K2 = H1 * EPSILON, H2 * EPSILON

    def sb(name, shape, dt=F32, stack=ctx):
        return stack.enter_context(nc.sbuf_tensor(name, shape, dt))

    def sem(name, stack=ctx):
        return stack.enter_context(nc.semaphore(name))

    Wih, Whh, Cp, brow, brz, ones, biasT, alphas, unit = (later[n] for n in ("Wih", "Whh", "Cp", "brow", "brz", "ones", "biasT", "alphas", "unit"))

    def two(name, shape, dt=F32):
        return [sb(f"{name}{u}", shape, dt) for u in range(2)]

    F = [PART, KC, B]
    xs = sb("xs", [PART, 2, KC, B], F16)
    hs = sb("hs", [PART, 2, KC, B], F16)
    Hf = two("Hf", F)
    rz = sb("rz", [PART, 3, KC, B])
    an, bn, nn, dn, en = (sb(n, F) for n in ("an", "bn", "nn", "dn", "en"))
    xbias, X3, Dr = two("xbias", F), two("X3", F), two("Dr", F)
    Qs, Ps = two("Qs", F), two("Ps", F)
    qs = [sb(f"qs{s}", F) for s in range(3)]
    th = sb("th", F)
    ts_ = sb("ts", [PART, 2, KC, B], F16)
    sqs, ws, rs = two("sqs", F), two("ws", F), two("rs", F)
    Zp, Gd, Gs, Ea, Eb = (sb(n, F) for n in ("Zp", "Gd", "Gs", "Ea", "Eb"))
    yz = two("yz", F)
    ys = [sb(f"ys{s}", F) for s in range(4)]
    e2, e3, gs, aq, cq, hq, hr, qp = (sb(n, F) for n in ("e2", "e3", "gs", "aq", "cq", "hq", "hr", "qp"))
    y23, y14, sy, pp = (sb(n, F) for n in ("y23", "y14", "sy", "pp"))
    ob, ot = two("ob", F), two("ot", F)

    psRZ = [ctx.enter_context(nc.psum_tensor(f"psRZ{u}", [PART, 2, KC, B], F32)) for u in range(2)]
    psN = [ctx.enter_context(nc.psum_tensor(f"psN{u}", [PART, 2, KC, B], F32)) for u in range(2)]
    psF = ctx.enter_context(nc.psum_tensor("psF", [PART, 2, KC, B], F32))

    names = ("xs_hi xs_ready gi_done rz_done gn_done sig_done an_done bn_done nn_done nz_done zh_done rz_sig h_done hs_hi hs_ready "
             "xbias_done X3_done Dr_done Z_done y1_done G_done Gs_done E_done th_done ts_hi ts_ready sq_done w_done r_done f_done "
             "q_done yz_done y_done e_done gs_done aq_done cq_done hq_done qp_done Q_done y23_done y14_done sy_done "
             "pp_done P_done ob_done ot_done passed act_passed")
    S = {n: sem("s_" + n) for n in names.split()}
    out_sent = [sem(f"out_sent{u}") for u in range(2)]
    block = ctx.enter_context(nc.Block())
    PEEL = 2

    def run(eng, first, step):
        first()
        for t in range(PEEL):
            step(Pair(t, t // 2, t % 2))
        with eng.Fori(0, (T - 2 * PEEL) // 2) as it:
            for u in range(2):
                step(Pair(it * 2 + PEEL + u, it + PEEL // 2, u))
        for t in range(T - PEEL, T):
            step(Pair(t, t // 2, t % 2))

    def has(t, d):
        return not isinstance(t.n, int) or t.n + d < T

    def xr(n):
        return XR[:, bass.ds(n, 1), :, :].rearrange("p a c b -> p (a c b)")

    def flat(ap):
        return ap.rearrange("p c b -> p (c b)")

    @block.tensor
    def _(pe):
        mm = nc.tensor.matmul
        TERMS = ((0, 0), (0, 1), (1, 0))

        def bias_products(u):
            for g in range(2 * KC):
                mm(psN[u][:, 1 - g // KC, g % KC, :], brow[:, g * PART:(g + 1) * PART], ones[:, :], start=(g == 0), stop=False,
                   skip_group_check=True)

        def gate_products(u, W, src, part, gates):
            for g in gates:
                o = psRZ[u][:, g // KC, g % KC, :] if g < 2 * KC else psN[u][:, part, g - 2 * KC, :]
                for c in range(KC):
                    for i, j in TERMS:
                        last = mm(o, W[:, i, c, g * PART:(g + 1) * PART], src[:, j, c, :],
                                  start=(part == 1 and g == 0 and c == 0 and (i, j) == TERMS[0]),
                                  stop=(part == 0 and c == KC - 1 and (i, j) == TERMS[-1]), skip_group_check=True)
            return last

        def gi(n, u, half):
            if half == 0:
                need(pe, S["sig_done"], n - 1)
                need(pe, S["bn_done"], n - 1)
                pe.wait_ge(S["xs_ready"], n + 1)
                gate_products(u, Wih, xs, 1, range(0, GC // 2))
            else:
                bias_products(u)
                gate_products(u, Wih, xs, 1, range(GC // 2, GC)).then_inc(S["gi_done"], 1)

        def gh(n, u, half):
            if half == 0:
                pe.wait_ge(S["hs_ready"], n + 1)
                gate_products(u, Whh, hs, 0, range(0, GC // 2))
            else:
                gate_products(u, Whh, hs, 0, range(GC // 2, 2 * KC)).then_inc(S["rz_done"], 1)
                gate_products(u, Whh, hs, 0, range(2 * KC, GC)).then_inc(S["gn_done"], 1)

        def stage(t, s):
            pe.wait_ge(S["ts_hi"], t.n * 4 + s + 1)
            for c in range(KC):
                for m in range(KC):
                    for i in range(2):
                        mm(psF[:, s % 2, m, :], Cp[:, i, c, m * PART:(m + 1) * PART], ts_[:, 0, c, :],
                           start=(c == 0 and m == 0 and i == 0), stop=False, skip_group_check=True)
            pe.wait_ge(S["ts_ready"], t.n * 4 + s + 1)
            for c in range(KC):
                for m in range(KC):
                    last = mm(psF[:, s % 2, m, :], Cp[:, 0, c, m * PART:(m + 1) * PART], ts_[:, 1, c, :],
                              start=False, stop=(c == KC - 1), skip_group_check=True)
            last.then_inc(S["f_done"], 1)

        def first():
            gi(0, 0, 0)
            gi(0, 0, 1)
            gh(0, 0, 0)
            gh(0, 0, 1)
            gi(1, 1, 0)
            gi(1, 1, 1)

        def step(t):
            stage(t, 0)
            if has(t, 1):
                gh(t.n + 1, 1 - t.u, 0)
            stage(t, 1)
            if has(t, 1):
                gh(t.n + 1, 1 - t.u, 1)
            stage(t, 2)
            if has(t, 2):
                gi(t.n + 2, t.u, 0)
            stage(t, 3)
            if has(t, 2):
                gi(t.n + 2, t.u, 1)

        run(pe, first, step)

    @block.scalar
    def _(act):
        def a(out, in_, f=ACT.Copy, **k):
            return nc.scalar.activation(out, in_, f, **k)

        def high_xs(n):
            need(act, S["gi_done"], n)
            a(xs[:, 0, :, :].rearrange("p c b -> p (c b)"), xr(n)).then_inc(S["xs_hi"], 1)

        def sigmoids(n, u):
            act.wait_ge(S["rz_done"], n + 1)
            need(act, S["h_done"], n)
            need(act, S["zh_done"], n)
            for g in range(2 * KC):
                i, c = g // KC, g % KC
                last = a(rz[:, i, c, :], psRZ[u][:, i, c, :], ACT.Sigmoid, scale=1.0 / WS, bias=brz[:, g:g + 1])
                if c == KC - 1:
                    last.then_inc(S["rz_sig"], 1)
            need(act, S["nz_done"], n)
            act.wait_ge(S["rz_sig"], n * 2 + 2)
            a(rz[:, 2, :, :], rz[:, 1, :, :], ACT.Identity, scale=-1.0, bias=unit[:, 0:1]).then_inc(S["sig_done"], 1)

        def tanh_n(n):
            act.wait_ge(S["bn_done"], n + 1)
            need(act, S["nz_done"], n)
            a(nn[:, :, :], bn[:, :, :], ACT.Tanh, scale=1.0 / WS).then_inc(S["nn_done"], 1)

        def high_h(n, u):
            act.wait_ge(S["h_done"], n + 1)
            need(act, S["gn_done"], n + 1)
            a(hs[:, 0, :, :], Hf[u][:, :, :]).then_inc(S["hs_hi"], 1)

        def stage(t, s):
            q = qs[s - 1] if s else Qs[t.u]
            if s:
                act.wait_ge(S["q_done"], t.n * 3 + s)
            else:
                act.wait_ge(S["Q_done"], t.n + 1)
            need(act, S["f_done"], t.n * 4 + s)
            a(ts_[:, 0, :, :], q[:, :, :], ACT.Tanh).then_inc(S["ts_hi"], 1)
            need(act, S["ts_ready"], t.n * 4 + s)
            a(th[:, :, :], q[:, :, :], ACT.Tanh).then_inc(S["th_done"], 1)
            need(act, S["w_done"], t.n * 4 + s - 1)
            a(sqs[s % 2][:, :, :], q[:, :, :], ACT.Square).then_inc(S["sq_done"], 1)

        def first():
            high_xs(0)
            a(hs[:, 0, :, :], condT[:, :, :]).then_inc(S["hs_hi"], 1)
            a(Qs[0][:, :, :], condT[:, :, :]).then_inc(S["Q_done"], 1)
            high_xs(1)
            with_bias(0, 0)
            sigmoids(0, 0)
            tanh_n(0)
            high_h(0, 0)

        def with_bias(n, u):
            need(act, S["Dr_done"], n - 1)
            act.sem_inc(S["act_passed"], 1)
            for c in range(KC):
                last = a(xbias[u][:, c, :], XR[:, bass.ds(n, 1), c, :].rearrange("p a b -> p (a b)"), ACT.Identity,
                         bias=biasT[:, c:c + 1])
            last.then_inc(S["xbias_done"], 1)

        def step(t):
            stage(t, 0)
            act.wait_ge(S["P_done"], t.n + 1)
            need(act, S["yz_done"], t.n * 3)
            a(Zp[:, :, :], Ps[t.u][:, :, :], ACT.Identity, scale=-BETA, bias=alphas[:, 0:1]).then_inc(S["Z_done"], 1)
            if has(t, 2):
                high_xs(t.n + 2)
            act.wait_ge(S["G_done"], t.n + 1)
            need(act, S["gs_done"], t.n)
            a(Gs[:, :, :], Gd[:, :, :], scale=DT / 6).then_inc(S["Gs_done"], 1)
            stage(t, 1)
            if has(t, 1):
                with_bias(t.n + 1, 1 - t.u)
            stage(t, 2)
            if has(t, 1):
                sigmoids(t.n + 1, 1 - t.u)
                tanh_n(t.n + 1)
            stage(t, 3)
            if has(t, 1):
                high_h(t.n + 1, 1 - t.u)

        run(act, first, step)

    @block.vector
    def _(dve):
        v = nc.vector

        def stt(out, in0, scalar, in1, op1=ALU.add):
            return v.scalar_tensor_tensor(out=flat(out), in0=flat(in0), scalar=scalar, in1=flat(in1), op0=ALU.mult, op1=op1)

        def gate_n(n, u):
            dve.wait_ge(S["rz_sig"], n * 2 + 1)
            dve.wait_ge(S["gn_done"], n + 1)
            v.tensor_tensor(an[:, :, :], psN[u][:, 0, :, :], rz[:, 0, :, :], ALU.mult).then_inc(S["an_done"], 1)
            dve.wait_ge(S["an_done"], n + 1)
            need(dve, S["nn_done"], n)
            v.tensor_tensor(bn[:, :, :], psN[u][:, 1, :, :], an[:, :, :], ALU.add).then_inc(S["bn_done"], 1)

        def new_h(n, u):
            dve.wait_ge(S["nn_done"], n + 1)
            dve.wait_ge(S["sig_done"], n + 1)
            v.tensor_tensor(dn[:, :, :], rz[:, 2, :, :], nn[:, :, :], ALU.mult).then_inc(S["nz_done"], 1)
            dve.wait_ge(S["nz_done"], n + 1)
            dve.wait_ge(S["zh_done"], n + 1)
            need(dve, S["X3_done"], n - 1)
            need(dve, S["Dr_done"], n - 1)
            need(dve, S["hs_ready"], n)
            v.tensor_tensor(Hf[u][:, :, :], dn[:, :, :], en[:, :, :], ALU.add).then_inc(S["h_done"], 1)

        def low_t(t, s):
            dve.wait_ge(S["th_done"], t.n * 4 + s + 1)
            v.tensor_tensor(ts_[:, 1, :, :], th[:, :, :], ts_[:, 0, :, :], ALU.subtract).then_inc(S["ts_ready"], 1)

        def cubic(t, s, q):
            dve.wait_ge(S["sq_done"], t.n * 4 + s + 1)
            v.scalar_tensor_tensor(out=flat(ws[s % 2][:, :, :]), in0=flat(sqs[s % 2][:, :, :]), scalar=-3.0, in1=flat(q[:, :, :]),
                                   op0=ALU.add, op1=ALU.mult).then_inc(S["w_done"], 1)

        def turn_out(n, u, half):
            dve.wait_ge(S["ob_done"], n + 1)
            need(dve, out_sent[u], half * (8 * 16))
            v.transpose(flat(ot[u]), flat(ob[u])).then_inc(S["ot_done"], 1)

        def first():
            gate_n(0, 0)
            new_h(0, 0)

        def step(t):
            n = t.n
            Q, P, Qn, Pn = Qs[t.u], Ps[t.u], Qs[1 - t.u], Ps[1 - t.u]
            q2, q3, q4 = qs
            low_t(t, 0)
            cubic(t, 0, Q)
            dve.wait_ge(S["G_done"], n + 1)
            stt(Ea, Gd, H1, Q).then_inc(S["E_done"], 1)
            dve.wait_ge(S["w_done"], n * 4 + 1)
            dve.wait_ge(S["E_done"], n * 2 + 1)
            stt(rs[0], ws[0], -H1 / 3, Ea).then_inc(S["r_done"], 1)
            stt(Eb, Gd, H2, Q).then_inc(S["E_done"], 1)
            dve.wait_ge(S["r_done"], n * 4 + 1)
            dve.wait_ge(S["f_done"], n * 4 + 1)
            stt(q2, psF[:, 0, :, :], H1 / WS, rs[0]).then_inc(S["q_done"], 1)
            dve.wait_ge(S["y1_done"], n + 1)
            stt(e2, ys[0], -H1 * K1, Ea).then_inc(S["e_done"], 1)
            if has(t, 0) and not (isinstance(n, int) and n == 0):
                turn_out(n - 1, 1 - t.u, t.before)
            low_t(t, 1)
            cubic(t, 1, q2)
            dve.wait_ge(S["yz_done"], n * 3 + 1)
            stt(ys[1], ys[0], -BETA * K1, yz[0]).then_inc(S["y_done"], 1)
            dve.wait_ge(S["w_done"], n * 4 + 2)
            dve.wait_ge(S["e_done"], n * 2 + 1)
            stt(rs[1], ws[1], -H1 / 3, e2).then_inc(S["r_done"], 1)
            dve.wait_ge(S["y_done"], n * 3 + 1)
            dve.wait_ge(S["E_done"], n * 2 + 2)
            stt(e3, ys[1], -H2 * K1, Eb).then_inc(S["e_done"], 1)
            dve.wait_ge(S["r_done"], n * 4 + 2)
            dve.wait_ge(S["f_done"], n * 4 + 2)
            stt(q3, psF[:, 1, :, :], H1 / WS, rs[1]).then_inc(S["q_done"], 1)
            dve.wait_ge(S["q_done"], n * 3 + 2)
            need(dve, S["cq_done"], n)
            stt(aq, q3, 2.0, q2).then_inc(S["aq_done"], 1)
            low_t(t, 2)
            cubic(t, 2, q3)
            dve.wait_ge(S["yz_done"], n * 3 + 2)
            stt(ys[2], ys[1], -BETA * K1, yz[1]).then_inc(S["y_done"], 1)
            dve.wait_ge(S["w_done"], n * 4 + 3)
            dve.wait_ge(S["e_done"], n * 2 + 2)
            stt(rs[0], ws[0], -H2 / 3, e3).then_inc(S["r_done"], 1)
            dve.wait_ge(S["y_done"], n * 3 + 2)
            dve.wait_ge(S["Gs_done"], n + 1)
            stt(gs, ys[2], -2 * K1 * DT / 6, Gs).then_inc(S["gs_done"], 1)
            if has(t, 1):
                gate_n(n + 1, 1 - t.u)
            dve.wait_ge(S["r_done"], n * 4 + 3)
            dve.wait_ge(S["f_done"], n * 4 + 3)
            stt(q4, psF[:, 0, :, :], H2 / WS, rs[0]).then_inc(S["q_done"], 1)
            dve.wait_ge(S["gs_done"], n + 1)
            dve.wait_ge(S["cq_done"], n + 1)
            stt(hq, cq, 1.0 / 3, gs).then_inc(S["hq_done"], 1)
            if has(t, 1):
                new_h(n + 1, 1 - t.u)
            low_t(t, 3)
            cubic(t, 3, q4)
            dve.wait_ge(S["hq_done"], n * 2 + 1)
            dve.wait_ge(S["q_done"], n * 3 + 3)
            stt(hr, q4, 1.0 / 3, hq).then_inc(S["hq_done"], 1)
            dve.wait_ge(S["yz_done"], n * 3 + 3)
            stt(ys[3], ys[2], -BETA * K2, yz[0]).then_inc(S["y_done"], 1)
            dve.wait_ge(S["w_done"], n * 4 + 4)
            dve.wait_ge(S["hq_done"], n * 2 + 2)
            stt(rs[1], ws[1], -DT / 18, hr).then_inc(S["r_done"], 1)
            dve.wait_ge(S["r_done"], n * 4 + 4)
            dve.wait_ge(S["f_done"], n * 4 + 4)
            stt(qp, psF[:, 1, :, :], DT / 6 / WS, rs[1]).then_inc(S["qp_done"], 1)
            dve.wait_ge(S["y14_done"], n + 1)
            dve.wait_ge(S["y23_done"], n + 1)
            stt(sy, y23, 2.0, y14).then_inc(S["sy_done"], 1)
            dve.wait_ge(S["qp_done"], n + 1)
            need(dve, S["ob_done"], n)
            v.tensor_scalar(flat(Qn), flat(qp), CLAMP, -CLAMP, ALU.min, ALU.max).then_inc(S["Q_done"], 1)
            dve.wait_ge(S["sy_done"], n + 1)
            stt(pp, sy, DT * EPSILON / 6, P).then_inc(S["pp_done"], 1)
            dve.wait_ge(S["pp_done"], n + 1)
            need(dve, S["G_done"], n)
            need(dve, S["Z_done"], n)
            v.tensor_scalar(flat(Pn), flat(pp), CLAMP, -CLAMP, ALU.min, ALU.max).then_inc(S["P_done"], 1)
            if isinstance(n, int) and n == T - 1:
                turn_out(n, t.u, t.half)

        run(dve, first, step)

    @block.gpsimd
    def _(pool):
        def settled():
            pool.sem_inc(S["passed"], 1)
            return nc.gpsimd

        def tt(out, in0, in1, op=ALU.add):
            return settled().tensor_tensor(flat(out), flat(in0), flat(in1), op)

        def low_xs(n):
            pool.wait_ge(S["xs_hi"], n + 1)
            settled().tensor_tensor(xs[:, 1, :, :].rearrange("p c b -> p (c b)"), xr(n), xs[:, 0, :, :].rearrange("p c b -> p (c b)"),
                            ALU.subtract).then_inc(S["xs_ready"], 1)

        def low_h(n, src):
            pool.wait_ge(S["hs_hi"], n + 1)
            tt(hs[:, 1, :, :], src, hs[:, 0, :, :], ALU.subtract).then_inc(S["hs_ready"], 1)

        def drive(n, u):
            pool.wait_ge(S["h_done"], n + 1)
            pool.wait_ge(S["xbias_done"], n + 1)
            tt(Dr[u], xbias[u], Hf[u]).then_inc(S["Dr_done"], 1)

        def stream(n, u):
            settled().tensor_tensor(flat(X3[u]), xr(n), flat(Hf[u]), ALU.add).then_inc(S["X3_done"], 1)

        def less_p(n, u):
            pool.wait_ge(S["P_done"], n + 1)
            pool.wait_ge(S["Dr_done"], n + 1)
            need(pool, S["gs_done"], n)
            need(pool, S["Gs_done"], n)
            tt(Gd, Dr[u], Ps[u], ALU.subtract).then_inc(S["G_done"], 1)
            pool.wait_ge(S["Z_done"], n + 1)
            tt(ys[0], Qs[u], Zp).then_inc(S["y1_done"], 1)

        def add_q(n, u):
            pool.wait_ge(S["Q_done"], n + 2)
            need(pool, S["ot_done"], n - 1)
            tt(ob[u], X3[u], Qs[1 - u]).then_inc(S["ob_done"], 1)

        def keep_zh(n, u, old):
            pool.wait_ge(S["rz_sig"], n * 2 + 2)
            need(pool, S["h_done"], n)
            settled().tensor_tensor(flat(en), rz[:, 1, :, :].rearrange("p c b -> p (c b)"), flat(old), ALU.mult)\
                .then_inc(S["zh_done"], 1)

        def q_plus_z(n, s):
            pool.wait_ge(S["q_done"], n * 3 + s + 1)
            tt(yz[s % 2], qs[s], Zp).then_inc(S["yz_done"], 1)

        def first():
            settled().tensor_copy(flat(Ps[0]), flat(condT)).then_inc(S["P_done"], 1)
            low_xs(0)
            low_h(0, condT)
            low_xs(1)
            keep_zh(0, 0, condT)
            drive(0, 0)
            low_h(1, Hf[0])

        def step(t):
            n, u = t.n, t.u
            less_p(n, u)
            if not (isinstance(n, int) and n == 0):
                add_q(n - 1, 1 - u)
            q_plus_z(n, 0)
            stream(n, u)
            if has(t, 2):
                low_xs(n + 2)
            q_plus_z(n, 1)
            pool.wait_ge(S["aq_done"], n + 1)
            need(pool, S["hq_done"], n * 2 - 1)
            tt(cq, aq, Qs[u], ALU.subtract).then_inc(S["cq_done"], 1)
            if has(t, 1):
                keep_zh(n + 1, 1 - u, Hf[u])
            pool.wait_ge(S["y_done"], n * 3 + 2)
            tt(y23, ys[1], ys[2]).then_inc(S["y23_done"], 1)
            q_plus_z(n, 2)
            if has(t, 1):
                drive(n + 1, 1 - u)
            pool.wait_ge(S["y_done"], n * 3 + 3)
            tt(y14, ys[0], ys[3]).then_inc(S["y14_done"], 1)
            if has(t, 1):
                low_h(n + 2, Hf[1 - u])
            if isinstance(n, int) and n == T - 1:
                add_q(n, u)

        run(pool, first, step)

    @block.sync
    def _(sp):
        def step(t):
            sp.wait_ge(S["ot_done"], t.n + 1)
            for q in range(4):
                for h in range(2):
                    dst = out[h * 32:(h + 1) * 32, bass.ds(t.n, 1), :].rearrange("b a (c q f) -> b (a c) q f", q=4, f=32)[:, :, q, :]
                    src = ot[t.u][q * 32:(q + 1) * 32, :, :].rearrange("p c (h f) -> p c h f", h=2)[:, :, h, :]
                    sp.dma_start(dst, src).then_inc(out_sent[t.u], 16)

        run(sp, lambda: None, step)
        for s in out_sent:
            sp.wait_ge(s, (T // 2) * 8 * 16)


_INS = ["x", "cond_2048", "L0_cond_W_emb", "L0_cond_b_emb", "L0_cond_g_norm", "L0_cond_W_qkv", "L0_cond_g_q", "L0_cond_g_k",
        "L0_cond_W_out", "L2_cond_W_ih", "L2_cond_W_hh", "L2_cond_b_ih", "L2_cond_b_hh", "L3_cond_coupling", "L3_cond_bias"]


def kernel(**inputs):
    import numpy as np
    import concourse.bacc as bacc
    from concourse.bass_utils import run_bass_kernel_spmd

    nc = bacc.Bacc("TRN2", target_bir_lowering=False, num_devices=1)
    arrays, args = {}, []
    for name in _INS:
        a = np.ascontiguousarray(inputs[name])
        arrays[f"in_{name}"] = a
        args.append(nc.dram_tensor(f"in_{name}", a.shape, mybir.dt.from_np(a.dtype), kind="ExternalInput").ap())
    shape = inputs["x"].shape
    out = nc.dram_tensor("out", shape, F32, kind="ExternalOutput").ap()
    rows = nc.dram_tensor("rows_dram", (shape[0], shape[2]), F16, kind="Internal").ap()
    program(nc, *args, out, rows)
    r = run_bass_kernel_spmd(nc, [arrays], core_ids=[0])
    return r.results[0]["out"]
```
